# Optimizing a Trainium2 kernel written in Bass

```python
import numpy as np
import jax
import jax.numpy as jnp

def _softmax(x, axis=-1):
    return jax.nn.softmax(x, axis=axis)

def _gelu(x):
    return jax.nn.gelu(x, approximate=True)

def _silu(x):
    return jax.nn.silu(x)

def _sigmoid(x):
    return jax.nn.sigmoid(x)

def _layernorm(x, axis=-1, eps=1e-05):
    m = jnp.mean(x, axis=axis, keepdims=True)
    v = jnp.var(x, axis=axis, keepdims=True)
    return (x - m) / jnp.sqrt(v + eps)

def _scatter_add(tgt, idx, src, axis=0):
    return tgt.at[idx].add(src)

def _segment_sum(src, seg, n):
    return jax.ops.segment_sum(src, seg, n)
kernel_name = 'mk_decoder_postln_d2_seqx_r4_c1fa28'

def setup_inputs(seed: int=0):
    np.random.seed(seed)
    _w = jnp.asarray

    def _rec_inputs():
        import jax
        import jax.numpy as jnp
        _rk = jax.random.key(seed)
        x = 7.22e-05 + 1 * jax.random.normal(jax.random.fold_in(_rk, 1), (8, 256, 256), jnp.float32)
        _lenS = 256 - jax.random.randint(jax.random.fold_in(_rk, 7), (8,), 0, max(1, 256 // 4) + 1, jnp.int32)
        _lenS2 = 256 - jax.random.randint(jax.random.fold_in(_rk, 8), (8,), 0, max(1, 256 // 4) + 1, jnp.int32)
        _ctx_1024P = jax.random.normal(jax.random.fold_in(_rk, 11), (8, 16, 256), jnp.float32)
        _ctx_1024c = jax.random.dirichlet(jax.random.fold_in(_rk, 511), 0.3 * jnp.ones((16,), jnp.float32), (8, 256))
        _ctx_1024t = jnp.einsum('bsk,bkd->bsd', _ctx_1024c, _ctx_1024P)
        _ctx_1024t = _ctx_1024t * jax.lax.rsqrt(jnp.mean(jnp.square(_ctx_1024t)) + 1e-12) * 0.953939
        ctx_1024 = 4.13588e-05 + 0.999923 * (_ctx_1024t + 0.3 * jax.random.normal(jax.random.fold_in(_rk, 611), (8, 256, 256), jnp.float32))
        _validS = jnp.arange(256)[None, :] < _lenS[:, None]
        _validS2 = jnp.arange(256)[None, :] < _lenS2[:, None]
        _causal = jnp.tril(jnp.ones((256, 256), dtype=bool))
        mask_Bx1x1xS2_ik0 = jnp.where(jnp.broadcast_to(_validS2[:, None, None, :], (8, 1, 1, 256)), 0, 1).astype(jnp.int32)
        mask_1x1xSxS2_ik0 = jnp.where(jnp.broadcast_to(_validS2[0:1, None, None, :], (1, 1, 256, 256)), 0, 1).astype(jnp.int32)
        return (x, ctx_1024, mask_Bx1x1xS2_ik0, mask_1x1xSxS2_ik0)
    x, ctx_1024, mask_Bx1x1xS2_ik0, mask_1x1xSxS2_ik0 = _rec_inputs()

    def _L0_attn_setup():
        import jax, jax.numpy as jnp
        import numpy as np
        HEADS = 16
        DIM_HEAD = 64
        WINDOW = 128
        LOOK_BACKWARD = 1
        LOOK_FORWARD = 0
        THETA = 10000.0
        PAD_VALUE = -1

        def look_around(x, backward, forward, pad_value, axis):
            w = x.shape[axis]
            size = backward + forward + 1
            pads = [(0, 0)] * x.ndim
            pads[axis] = (backward, forward)
            p = jnp.pad(x, pads, constant_values=pad_value)
            segs = [jax.lax.slice_in_dim(p, s, s + w, axis=axis) for s in range(size)]
            return jnp.concatenate(segs, axis=axis + 1)

        def rotate_half(t):
            t1, t2 = jnp.split(t, 2, axis=-1)
            return jnp.concatenate([-t2, t1], axis=-1)
        key = jax.random.key(seed)
        k1, k2, k3 = jax.random.split(key, 3)
        dim = 256
        x = jax.random.normal(k1, (4, 1024, dim), dtype=jnp.float32)
        W_qkv = jax.random.normal(k2, (dim, 3 * HEADS * DIM_HEAD), dtype=jnp.float32) * dim ** (-0.5)
        W_out = jax.random.normal(k3, (HEADS * DIM_HEAD, dim), dtype=jnp.float32) * (HEADS * DIM_HEAD) ** (-0.5)
        return {'x': x, 'W_qkv': W_qkv, 'W_out': W_out}
    _L0_attn_all = _L0_attn_setup()
    _L0_attn_in = {k: v for k, v in _L0_attn_all.items() if k in ('W_qkv', 'W_out')}
    del _L0_attn_all

    def _L0_xattn_setup():
        import jax, jax.numpy as jnp
        import numpy as np
        B, S, D = (4, 512, 256)
        H, HD = (16, 64)
        key = jax.random.key(seed)
        ks = jax.random.split(key, 11)
        s = 0.02
        return {'inputs_q': jax.random.normal(ks[0], (B, S, D), jnp.float32), 'inputs_k': jax.random.normal(ks[1], (B, S, D), jnp.float32), 'inputs_v': jax.random.normal(ks[2], (B, S, D), jnp.float32), 'Wq': jax.random.normal(ks[3], (D, H, HD), jnp.float32) * s, 'bq': jnp.zeros((H, HD), jnp.float32), 'Wk': jax.random.normal(ks[4], (D, H, HD), jnp.float32) * s, 'bk': jnp.zeros((H, HD), jnp.float32), 'Wv': jax.random.normal(ks[5], (D, H, HD), jnp.float32) * s, 'bv': jnp.zeros((H, HD), jnp.float32), 'Wo': jax.random.normal(ks[6], (H, HD, D), jnp.float32) * s, 'bo': jnp.zeros((D,), jnp.float32)}
    _L0_xattn_all = _L0_xattn_setup()
    _L0_xattn_in = {k: v for k, v in _L0_xattn_all.items() if k in ('Wq', 'bq', 'Wk', 'bk', 'Wv', 'bv', 'Wo', 'bo')}
    del _L0_xattn_all

    def _L0_ffn_setup():
        import jax, jax.numpy as jnp
        import numpy as np
        IN_FEATURES = 256
        ACT_BITS = 4

        def _hadamard(size: int) -> np.ndarray:
            h = np.array([[1.0]], dtype=np.float64)
            while h.shape[0] < size:
                h = np.block([[h, h], [h, -h]])
            return (h / np.sqrt(size)).astype(np.float32)

        def _quantize_activations(x, bits=ACT_BITS):
            pos = 2 ** (bits - 1) - 1
            neg = 2 ** (bits - 1)
            scale = jnp.clip(jnp.max(jnp.abs(jax.lax.stop_gradient(x)), axis=-1, keepdims=True), 1e-05) / pos
            q = jnp.clip(jnp.round(x / scale), -neg, pos) * scale
            return x + jax.lax.stop_gradient(q - x)

        def _ternary_quantize_ste(w):
            scale = jnp.clip(jnp.mean(jnp.abs(jax.lax.stop_gradient(w)), axis=1, keepdims=True), 1e-05)
            n = w / scale
            tern = jnp.where(n > 0.5, 1.0, jnp.where(n < -0.5, -1.0, 0.0))
            q = tern * scale
            return w + jax.lax.stop_gradient(q - w)
        key = jax.random.key(seed)
        k1, k2 = jax.random.split(key)
        x = jax.random.normal(k1, (8, 2048, IN_FEATURES), dtype=jnp.float32)
        bound = 1.0 / np.sqrt(IN_FEATURES)
        weight = jax.random.uniform(k2, (256, IN_FEATURES), dtype=jnp.float32, minval=-bound, maxval=bound)
        return {'x': x, 'weight': weight}
    _L0_ffn_all = _L0_ffn_setup()
    _L0_ffn_in = {k: v for k, v in _L0_ffn_all.items() if k in ('weight',)}
    del _L0_ffn_all

    def _L1_attn_setup():
        import jax, jax.numpy as jnp
        import numpy as np
        DIM = 256
        HEADS = 16
        HEAD_DIM = DIM // HEADS
        SCALE = float(HEAD_DIM ** (-0.25))
        ROPE_BASE = 10000.0

        def apply_rope(x):
            B, N, H, D = x.shape
            half = D // 2
            inv_freq = 1.0 / ROPE_BASE ** (jnp.arange(half, dtype=jnp.float32) / half)
            freqs = jnp.arange(N, dtype=jnp.float32)[:, None] * inv_freq[None, :]
            cos = jnp.cos(freqs)[None, :, None, :].astype(x.dtype)
            sin = jnp.sin(freqs)[None, :, None, :].astype(x.dtype)
            x1, x2 = (x[..., :half], x[..., half:])
            return jnp.concatenate([x1 * cos - x2 * sin, x1 * sin + x2 * cos], axis=-1)
        key = jax.random.key(seed)
        k1, k2, k3 = jax.random.split(key, 3)
        x = jax.random.normal(k1, (4, 1024, DIM), dtype=jnp.float32)
        w_qkv = jax.random.normal(k2, (DIM, 3 * DIM), dtype=jnp.float32) * 0.02
        w_out = jax.random.normal(k3, (DIM, DIM), dtype=jnp.float32) * 0.02
        return {'x': x, 'w_qkv': w_qkv, 'w_out': w_out}
    _L1_attn_all = _L1_attn_setup()
    _L1_attn_in = {k: v for k, v in _L1_attn_all.items() if k in ('w_qkv', 'w_out')}
    del _L1_attn_all

    def _L1_xattn_setup():
        import jax, jax.numpy as jnp
        import numpy as np
        E, H = (256, 16)
        N, S, T = (2, 512, 512)
        key = jax.random.key(seed)
        ks = jax.random.split(key, 8)
        scale = 1.0 / np.sqrt(E)
        q = jax.random.normal(ks[0], (N, S, E), dtype=jnp.float32)
        k = jax.random.normal(ks[1], (N, T, E), dtype=jnp.float32)
        v = jax.random.normal(ks[2], (N, T, E), dtype=jnp.float32)
        pad_mask = jax.random.randint(ks[3], (N, 1, 1, T), 0, 2, dtype=jnp.int32)
        subsq_mask = jnp.tril(jnp.ones((S, T), dtype=jnp.int32))[None, None]
        Wq = jax.random.normal(ks[4], (E, E), dtype=jnp.float32) * scale
        Wk = jax.random.normal(ks[5], (E, E), dtype=jnp.float32) * scale
        Wv = jax.random.normal(ks[6], (E, E), dtype=jnp.float32) * scale
        bq = jnp.zeros((E,), dtype=jnp.float32)
        bk = jnp.zeros((E,), dtype=jnp.float32)
        bv = jnp.zeros((E,), dtype=jnp.float32)
        return {'query': q, 'key': k, 'value': v, 'pad_mask': pad_mask, 'subsq_mask': subsq_mask, 'Wq': Wq, 'bq': bq, 'Wk': Wk, 'bk': bk, 'Wv': Wv, 'bv': bv}
    _L1_xattn_all = _L1_xattn_setup()
    _L1_xattn_in = {k: v for k, v in _L1_xattn_all.items() if k in ('Wq', 'bq', 'Wk', 'bk', 'Wv', 'bv')}
    del _L1_xattn_all

    def _L1_ffn_setup():
        import jax, jax.numpy as jnp
        import numpy as np
        D_MODEL = 256
        D_FF = 704
        N_EXPERTS = 8
        key = jax.random.key(seed)
        k_in, k1, k2, k3 = jax.random.split(key, 4)
        scale = 0.02
        inputs = jax.random.normal(k_in, (4, N_EXPERTS * 512, D_MODEL), dtype=jnp.float32)
        w1 = jax.random.normal(k1, (N_EXPERTS, D_MODEL, D_FF), dtype=jnp.float32) * scale
        w3 = jax.random.normal(k3, (N_EXPERTS, D_MODEL, D_FF), dtype=jnp.float32) * scale
        w2 = jax.random.normal(k2, (N_EXPERTS, D_FF, D_MODEL), dtype=jnp.float32) * scale
        return {'inputs': inputs, 'w1': w1, 'w3': w3, 'w2': w2}
    _L1_ffn_all = _L1_ffn_setup()
    _L1_ffn_in = {k: v for k, v in _L1_ffn_all.items() if k in ('w1', 'w3', 'w2')}
    del _L1_ffn_all
    return {'x': x, 'ctx_1024': ctx_1024, 'mask_Bx1x1xS2_ik0': mask_Bx1x1xS2_ik0, 'mask_1x1xSxS2_ik0': mask_1x1xSxS2_ik0, 'L0_attn_W_qkv': _L0_attn_in['W_qkv'], 'L0_attn_W_out': _L0_attn_in['W_out'], 'L0_xattn_Wq': _L0_xattn_in['Wq'], 'L0_xattn_bq': _L0_xattn_in['bq'], 'L0_xattn_Wk': _L0_xattn_in['Wk'], 'L0_xattn_bk': _L0_xattn_in['bk'], 'L0_xattn_Wv': _L0_xattn_in['Wv'], 'L0_xattn_bv': _L0_xattn_in['bv'], 'L0_xattn_Wo': _L0_xattn_in['Wo'], 'L0_xattn_bo': _L0_xattn_in['bo'], 'L0_ffn_weight': _L0_ffn_in['weight'], 'L1_attn_w_qkv': _L1_attn_in['w_qkv'], 'L1_attn_w_out': _L1_attn_in['w_out'], 'L1_xattn_Wq': _L1_xattn_in['Wq'], 'L1_xattn_bq': _L1_xattn_in['bq'], 'L1_xattn_Wk': _L1_xattn_in['Wk'], 'L1_xattn_bk': _L1_xattn_in['bk'], 'L1_xattn_Wv': _L1_xattn_in['Wv'], 'L1_xattn_bv': _L1_xattn_in['bv'], 'L1_ffn_w1': _L1_ffn_in['w1'], 'L1_ffn_w3': _L1_ffn_in['w3'], 'L1_ffn_w2': _L1_ffn_in['w2']}

def reference(x, ctx_1024, mask_Bx1x1xS2_ik0, mask_1x1xSxS2_ik0, L0_attn_W_qkv, L0_attn_W_out, L0_xattn_Wq, L0_xattn_bq, L0_xattn_Wk, L0_xattn_bk, L0_xattn_Wv, L0_xattn_bv, L0_xattn_Wo, L0_xattn_bo, L0_ffn_weight, L1_attn_w_qkv, L1_attn_w_out, L1_xattn_Wq, L1_xattn_bq, L1_xattn_Wk, L1_xattn_bk, L1_xattn_Wv, L1_xattn_bv, L1_ffn_w1, L1_ffn_w3, L1_ffn_w2):
    import jax
    import jax.numpy as jnp

    def _L0_attn_ref(x, W_qkv, W_out):
        import jax, jax.numpy as jnp
        import numpy as np
        HEADS = 16
        DIM_HEAD = 64
        WINDOW = 128
        LOOK_BACKWARD = 1
        LOOK_FORWARD = 0
        THETA = 10000.0
        PAD_VALUE = -1

        def look_around(x, backward, forward, pad_value, axis):
            w = x.shape[axis]
            size = backward + forward + 1
            pads = [(0, 0)] * x.ndim
            pads[axis] = (backward, forward)
            p = jnp.pad(x, pads, constant_values=pad_value)
            segs = [jax.lax.slice_in_dim(p, s, s + w, axis=axis) for s in range(size)]
            return jnp.concatenate(segs, axis=axis + 1)

        def rotate_half(t):
            t1, t2 = jnp.split(t, 2, axis=-1)
            return jnp.concatenate([-t2, t1], axis=-1)
        b, n, dim = x.shape
        h, dh, ws = (HEADS, DIM_HEAD, WINDOW)
        w = n // ws
        j = ws * (LOOK_BACKWARD + LOOK_FORWARD + 1)
        qkv = x @ W_qkv
        q, k, v = jnp.split(qkv, 3, axis=-1)

        def to_bhwnd(t):
            return t.reshape(b, n, h, dh).transpose(0, 2, 1, 3).reshape(b, h, w, ws, dh)
        bq = to_bhwnd(q) * dh ** (-0.5)
        bk = look_around(to_bhwnd(k), LOOK_BACKWARD, LOOK_FORWARD, float(PAD_VALUE), axis=2)
        bv = look_around(to_bhwnd(v), LOOK_BACKWARD, LOOK_FORWARD, float(PAD_VALUE), axis=2)
        inv_freq = 1.0 / THETA ** (jnp.arange(0, dh, 2, dtype=jnp.float32) / dh)
        t_pos = jnp.arange(j, dtype=jnp.float32)
        freqs = t_pos[:, None] * inv_freq[None, :]
        freqs = jnp.concatenate([freqs, freqs], axis=-1)
        q_freqs = freqs[-ws:]
        bq = bq * jnp.cos(q_freqs) + rotate_half(bq) * jnp.sin(q_freqs)
        bk = bk * jnp.cos(freqs) + rotate_half(bk) * jnp.sin(freqs)
        sim = jnp.einsum('bhwid,bhwjd->bhwij', bq, bk)
        seq = jnp.arange(n).reshape(w, ws)
        bq_t = seq[:, :, None]
        bq_k = look_around(seq[None], LOOK_BACKWARD, LOOK_FORWARD, PAD_VALUE, axis=1)[0]
        bq_k = bq_k[:, None, :]
        pad_mask = bq_k == PAD_VALUE
        causal_mask = (bq_t < bq_k) | (bq_t > bq_k + ws * LOOK_BACKWARD)
        mask = causal_mask | pad_mask
        mask_value = -jnp.finfo(sim.dtype).max
        sim = jnp.where(mask, mask_value, sim)
        attn = jax.nn.softmax(sim, axis=-1)
        out = jnp.einsum('bhwij,bhwjd->bhwid', attn, bv)
        out = out.reshape(b, h, n, dh).transpose(0, 2, 1, 3).reshape(b, n, h * dh)
        return out @ W_out

    def _L0_xattn_ref(inputs_q, inputs_k, inputs_v, Wq, bq, Wk, bk, Wv, bv, Wo, bo):
        import jax, jax.numpy as jnp
        import numpy as np
        B, S, D = (4, 512, 256)
        H, HD = (16, 64)
        q = jnp.einsum('bsf,fhd->bshd', inputs_q, Wq) + bq
        k = jnp.einsum('bsf,fhd->bshd', inputs_k, Wk) + bk
        v = jnp.einsum('bsf,fhd->bshd', inputs_v, Wv) + bv
        depth = q.shape[-1]
        q = q / jnp.sqrt(jnp.asarray(depth, q.dtype))
        attn = jnp.einsum('bqhd,bkhd->bhqk', q, k)
        attn = jax.nn.softmax(attn, axis=-1)
        x = jnp.einsum('bhqk,bkhd->bqhd', attn, v)
        out = jnp.einsum('bqhd,hdo->bqo', x, Wo) + bo
        return out

    def _L0_ffn_ref(x, weight):
        import jax, jax.numpy as jnp
        import numpy as np
        IN_FEATURES = 256
        ACT_BITS = 4

        def _hadamard(size: int) -> np.ndarray:
            h = np.array([[1.0]], dtype=np.float64)
            while h.shape[0] < size:
                h = np.block([[h, h], [h, -h]])
            return (h / np.sqrt(size)).astype(np.float32)

        def _quantize_activations(x, bits=ACT_BITS):
            pos = 2 ** (bits - 1) - 1
            neg = 2 ** (bits - 1)
            scale = jnp.clip(jnp.max(jnp.abs(jax.lax.stop_gradient(x)), axis=-1, keepdims=True), 1e-05) / pos
            q = jnp.clip(jnp.round(x / scale), -neg, pos) * scale
            return x + jax.lax.stop_gradient(q - x)

        def _ternary_quantize_ste(w):
            scale = jnp.clip(jnp.mean(jnp.abs(jax.lax.stop_gradient(w)), axis=1, keepdims=True), 1e-05)
            n = w / scale
            tern = jnp.where(n > 0.5, 1.0, jnp.where(n < -0.5, -1.0, 0.0))
            q = tern * scale
            return w + jax.lax.stop_gradient(q - w)
        H = jnp.asarray(_hadamard(IN_FEATURES))
        xh = x @ H
        xq = _quantize_activations(xh)
        wq = _ternary_quantize_ste(weight)
        return jnp.einsum('bsi,oi->bso', xq, wq)

    def _L1_attn_ref(x, w_qkv, w_out):
        import jax, jax.numpy as jnp
        import numpy as np
        DIM = 256
        HEADS = 16
        HEAD_DIM = DIM // HEADS
        SCALE = float(HEAD_DIM ** (-0.25))
        ROPE_BASE = 10000.0

        def apply_rope(x):
            B, N, H, D = x.shape
            half = D // 2
            inv_freq = 1.0 / ROPE_BASE ** (jnp.arange(half, dtype=jnp.float32) / half)
            freqs = jnp.arange(N, dtype=jnp.float32)[:, None] * inv_freq[None, :]
            cos = jnp.cos(freqs)[None, :, None, :].astype(x.dtype)
            sin = jnp.sin(freqs)[None, :, None, :].astype(x.dtype)
            x1, x2 = (x[..., :half], x[..., half:])
            return jnp.concatenate([x1 * cos - x2 * sin, x1 * sin + x2 * cos], axis=-1)
        B, N, D = x.shape
        qkv = x @ w_qkv
        q, k, v = jnp.split(qkv, 3, axis=-1)
        q = q.reshape(B, N, HEADS, HEAD_DIM)
        k = k.reshape(B, N, HEADS, HEAD_DIM)
        v = v.reshape(B, N, HEADS, HEAD_DIM)
        q = apply_rope(q)
        k = apply_rope(k)
        q = jax.nn.elu(q * SCALE) + 1.0
        k = jax.nn.elu(k * SCALE) + 1.0
        qT = jnp.moveaxis(q, 1, 0)
        kT = jnp.moveaxis(k, 1, 0)
        vT = jnp.moveaxis(v, 1, 0)
        kv0 = jnp.zeros((B, HEADS, HEAD_DIM, HEAD_DIM), dtype=q.dtype)
        ks0 = jnp.zeros((B, HEADS, HEAD_DIM), dtype=q.dtype)

        def step(carry, qkv_t):
            kv, ks = carry
            qt, kt, vt = qkv_t
            kv = kv + jnp.einsum('bhd,bhm->bhdm', kt, vt)
            ks = ks + kt
            denom = jnp.maximum(jnp.einsum('bhd,bhd->bh', qt, ks), 1e-06)
            out_t = jnp.einsum('bhd,bhdm->bhm', qt, kv) / denom[..., None]
            return ((kv, ks), out_t)
        _, outT = jax.lax.scan(step, (kv0, ks0), (qT, kT, vT))
        out = jnp.moveaxis(outT, 0, 1).reshape(B, N, D)
        return out @ w_out

    def _L1_xattn_ref(query, key, value, pad_mask, subsq_mask, Wq, bq, Wk, bk, Wv, bv):
        import jax, jax.numpy as jnp
        import numpy as np
        E, H = (256, 16)
        N, S, T = (2, 512, 512)
        n, s, e = query.shape
        t = value.shape[1]
        d = e // H
        q = (query @ Wq.T + bq).reshape(n, s, H, d).transpose(0, 2, 1, 3)
        k = (key @ Wk.T + bk).reshape(n, t, H, d).transpose(0, 2, 1, 3)
        v = (value @ Wv.T + bv).reshape(n, t, H, d).transpose(0, 2, 1, 3)
        att = jnp.einsum('bhsd,bhtd->bhst', q, k) / jnp.sqrt(jnp.float32(d))
        att = jnp.where(pad_mask == 0, jnp.float32(-1000000000.0), att)
        att = jnp.where(subsq_mask == 0, jnp.float32(-1000000000.0), att)
        prob = jax.nn.softmax(att, axis=-1)
        out = jnp.einsum('bhst,bhtd->bhsd', prob, v)
        return out.transpose(0, 2, 1, 3).reshape(n, s, e)

    def _L1_ffn_ref(inputs, w1, w3, w2):
        import jax, jax.numpy as jnp
        import numpy as np
        D_MODEL = 256
        D_FF = 704
        N_EXPERTS = 8
        B, T, D = inputs.shape
        E = w1.shape[0]
        C = T // E
        x = inputs.reshape(B, E, C, D)
        gate = jnp.einsum('becd,edf->becf', x, w1)
        up = jnp.einsum('becd,edf->becf', x, w3)
        h = jax.nn.silu(gate) * up
        out = jnp.einsum('becf,efd->becd', h, w2)
        return out.reshape(B, T, D)
    x = _layernorm(x + _L0_attn_ref(x, L0_attn_W_qkv, L0_attn_W_out), axis=-1)
    x = _layernorm(x + _L0_xattn_ref(x, ctx_1024, ctx_1024, L0_xattn_Wq, L0_xattn_bq, L0_xattn_Wk, L0_xattn_bk, L0_xattn_Wv, L0_xattn_bv, L0_xattn_Wo, L0_xattn_bo), axis=-1)
    x = _layernorm(x + _L0_ffn_ref(x, L0_ffn_weight), axis=-1)
    x = _layernorm(x + _L1_attn_ref(x, L1_attn_w_qkv, L1_attn_w_out), axis=-1)
    x = _layernorm(x + _L1_xattn_ref(x, ctx_1024, ctx_1024, mask_Bx1x1xS2_ik0, mask_1x1xSxS2_ik0, L1_xattn_Wq, L1_xattn_bq, L1_xattn_Wk, L1_xattn_bk, L1_xattn_Wv, L1_xattn_bv), axis=-1)
    x = _layernorm(x + _L1_ffn_ref(x, L1_ffn_w1, L1_ffn_w3, L1_ffn_w2), axis=-1)
    return x

_drawn_inputs = setup_inputs


def setup_inputs(seed=0):
    import zlib

    import numpy as np

    out = dict(_drawn_inputs(seed))
    spreads = {'L0_xattn_bq': (0.0, 0.8),
     'L0_xattn_bk': (0.0, 0.8),
     'L0_xattn_bv': (0.0, 0.1),
     'L0_xattn_bo': (0.0, 0.1),
     'L1_xattn_bq': (0.0, 0.318),
     'L1_xattn_bk': (0.0, 0.8),
     'L1_xattn_bv': (0.0, 0.1)}
    factors = {'L0_xattn_Wq': 5.015, 'L0_xattn_Wk': 4.927}
    for name, (base, spread) in spreads.items():
        noise = np.random.default_rng([zlib.crc32(name.encode()), seed]).standard_normal(out[name].shape)
        drawn = base * np.exp(spread * noise) if base else spread * noise
        out[name] = jnp.asarray(drawn.astype(out[name].dtype))
    for name, factor in factors.items():
        out[name] = (out[name] * factor).astype(out[name].dtype)
    return out
```

```python
from contextlib import ExitStack

import numpy as np
import concourse.bass as bass
from concourse import mybir

F32 = mybir.dt.float32
BF16 = mybir.dt.bfloat16
I32 = mybir.dt.int32
ALU = mybir.AluOpType
ACT = mybir.ActivationFunctionType
AX = mybir.AxisListType

P = 128
B = 8
N = 256
D = 256
TT = N // P
KT = D // P
H = 16
DH = 64
HP = H // 2
IN0 = H * DH
D1 = D // H
VW = 32
E = 8
F = 704
FT = -(-F // P)
FR = F - (FT - 1) * P
TE = N // E
BIG = 3.0e38
MASKED = -1.0e9
MAGIC = 12582912.0
EPS = 1e-5
ITERS = B // 2
HALVES = (0, 1)

RINGS = {"S": (0, 1, 2), "T": (3, 4), "O": (5,), "G": (6, 7)}
MOE_RINGS = {"G": (0,), "U": (1, 2, 3, 4), "Y0": (5,), "Y1": (6,)}

UNITS = 2 * HP
LAG = 3
O_LAG = LAG + 2
ATT_STEPS = range(2 * UNITS + O_LAG)
ATT_END = 2 * UNITS
N_ROPE = TT * 4


def stage_groups():
    def attention(heads_per_o):
        fills = []
        for step in ATT_STEPS:
            if step < 2 * UNITS:
                h, u = divmod(step, UNITS)
                fills.append((("S", u), "S", h))
            if LAG <= step < 2 * UNITS + LAG:
                h, u = divmod(step - LAG, UNITS)
                fills.append((("PT", u), "T", h))
            if step >= O_LAG and (step - O_LAG) % 2 == 0:
                h, hp = divmod((step - O_LAG) // 2, HP)
                if hp % heads_per_o == 0:
                    fills.append((("O", hp), "O", h))
        return fills

    return {
        "load": [("xT", "G"), ("cT", "G")],
        "qkv0": [(("qk", k), "G") for k in range(N_ROPE)] + [(("v", k), "G") for k in range(4)]
        + [(("qkT", hp), "T") for hp in range(HP)],
        "att0": attention(1),
        "out0": [("out", "G")],
        "qkvx": [("xT", "G")] + [(("qk", hp), "G") for hp in range(HP)] + [(("v", k), "G") for k in range(4)],
        "attx": attention(1),
        "outx": [("out", "G")],
        "quant": [("xT", "G"), ("xh", "G")],
        "ffn": [("qT", "T"), ("out", "G")],
        "qkv1": [("xT", "G"), (("qk", 0), "G"), (("qk", 1), "G"), ("v", "G")],
        "lin": [("qT", "T"), ("kT", "T"), ("KV", "G")] + [(("A", c, r), "S") for c in range(TT) for r in range(4)],
        "lout": [(("oT", i), "G") for i in range(2)] + [(("o", tt), "T") for tt in range(TT)],
        "out1": [("oTT", "T"), ("out", "G")],
        "qkvy": [("xT", "G"), ("q", "G"), ("k", "G"), ("v", "G")],
        "atty": attention(2),
        "outy": [(("o", tt), "T") for tt in range(TT)],
    }


def plan(order, groups, rings):
    turn = {ring: 0 for ring in rings}
    fills = [0] * 8
    place = {}
    for half, stage in order:
        for name, ring, *own in groups[stage]:
            half = own[0] if own else half
            ring = f"{ring}{half}" if ring == "Y" else ring
            b = rings[ring][turn[ring] % len(rings[ring])]
            turn[ring] += 1
            place[(half, stage, name)] = (b, fills[b])
            fills[b] += 1
    return place, fills


STAGES = ("load", "qkv0", "att0", "out0", "qkvx", "attx", "outx", "quant", "ffn",
          "qkv1", "lin", "lout", "out1", "qkvy", "atty", "outy")
ATT = ("att0", "attx", "atty")
ORDER = [(h, s) for s in STAGES for h in HALVES if s not in ATT or h == 0]
PE_ORDER = []
for h, s in ORDER:
    PE_ORDER += [(h, s), (h, s + "_end")] if s in ATT else [(h, s)]
    if s in ("out0", "outx") and h == 0:
        PE_ORDER[-2:] = [PE_ORDER[-1], PE_ORDER[-2]]
LN = {"out0": 0, "outx": 1, "ffn": 2, "out1": 3, "outy": 4}
N_LN = len(LN)
PLACE, FILLS = plan(ORDER, stage_groups(), RINGS)
MOE_PLACE, MOE_FILLS = plan([(h, "moe") for h in HALVES],
                            {"moe": [("xT", "G")] + [(("gu", j), "U") for j in range(FT)] + [("out", "Y")]}, MOE_RINGS)
N_CONST = 26
N_SETUP_DVE = 16
DVE_LINKS = 102
POOL_LINKS = 22


def decoder_kernel(nc, x_d, ctx_d, padm_d, subm_d, wqkv0_d, wout0_d, wq_d, bq_d, wk_d, bk_d, wv_d, bv_d,
                   wo_d, bo_d, ffn_d, wqkv1_d, wout1_d, wqy_d, bqy_d, wky_d, bky_d, wvy_d, bvy_d,
                   w1_d, w3_d, w2_d, ident_d, rope0_d, rope1_d, mask0_d, tri_d, par_d, bdm_d, had_d, out_d):
    ctx = ExitStack()
    with ctx:
        def sb(name, shape, dt=F32):
            return ctx.enter_context(nc.sbuf_tensor(name, shape, dt))

        def sem(name):
            return ctx.enter_context(nc.semaphore(name))

        w_area = sb("w_area", [P, 16384])
        wqkv0 = w_area[:, 0:6144].rearrange("p (k n) -> p k n", k=KT)
        wout0 = w_area[:, 6144:8192].rearrange("p (k n) -> p k n", k=HP)
        wq = w_area[:, 8192:10240].rearrange("p (k n) -> p k n", k=KT)
        wk = w_area[:, 10240:12288].rearrange("p (k n) -> p k n", k=KT)
        wv = w_area[:, 12288:14336].rearrange("p (k n) -> p k n", k=KT)
        wo = w_area[:, 14336:16384].rearrange("p (k n) -> p k n", k=HP)
        EW = 2 * KT * F + FT * D
        w1 = [w_area[:, i * EW:i * EW + KT * F].rearrange("p (k n) -> p k n", k=KT) for i in range(2)]
        w3 = [w_area[:, i * EW + KT * F:i * EW + 2 * KT * F].rearrange("p (k n) -> p k n", k=KT) for i in range(2)]
        w2 = [w_area[:, i * EW + 2 * KT * F:(i + 1) * EW].rearrange("p (k n) -> p k n", k=FT) for i in range(2)]
        wqkv1 = sb("wqkv1", [P, KT, 3 * D])
        wout1 = sb("wout1", [P, KT, D])
        wqy = sb("wqy", [P, KT, D])
        wky = sb("wky", [P, KT, D])
        wvy = sb("wvy", [P, KT, D])
        had = sb("had", [P, KT, D])
        ternT = sb("ternT", [P, KT, D], BF16)
        ident = sb("ident_s", [P, P])
        identb = sb("identb", [P, P], BF16)
        rope0 = sb("rope0", [P, TT, 2, 2, DH])
        rope1 = sb("rope1", [P, TT, 2, D1])
        mask0 = sb("mask0", [P, 3, P])
        tri = sb("tri", [P, P])
        par = sb("par", [P, 2])
        bdm = sb("bdm", [P, 8, VW])
        bq = sb("bq", [P, HP])
        bk = sb("bk", [P, HP])
        bv = sb("bv", [P, HP])
        bqy = sb("bqy", [P, KT])
        bky = sb("bky", [P, KT])
        bo_row = sb("bo_row", [P, D])
        bvy_row = sb("bvy_row", [P, D])
        bq_s = sb("bq_s", [P, HP])
        bqy_s = sb("bqy_s", [P, KT])
        wscale_row = sb("wscale_row", [P, D])
        sub_kept = sb("sub_kept", [P, TT, N])
        half_neg = sb("half_neg", [P, TT])
        x = [sb(f"x{h}", [P, TT, D]) for h in HALVES]
        xb = [sb(f"xb{h}", [P, TT, D]) for h in HALVES]
        r = [sb(f"r{h}", [P, TT, D]) for h in HALVES]
        cx = [sb(f"cx{h}", [P, TT, D]) for h in HALVES]
        xT = [sb(f"xT{h}", [P, KT, N]) for h in HALVES]
        cT = [sb(f"cT{h}", [P, KT, N]) for h in HALVES]
        qk_area = [sb(f"qk_area{h}", [P, HP * 2 * N]) for h in HALVES]
        v_area = [sb(f"v_area{h}", [P, TT * IN0]) for h in HALVES]
        o_area = sb("o_area", [P, 2 * HP * N])
        Vy = [sb(f"Vy{h}", [P, TT, H, VW]) for h in HALVES]
        p_ring = sb("p_ring", [P, 4, 2, N])
        pt_area = sb("pt_area", [P, 2 * 4 * N])
        qkT = [a[:, :].rearrange("p (m s n) -> p m s n", m=HP, s=2) for a in qk_area]
        V = [a[:, :].rearrange("p (t n) -> p t n", t=TT) for a in v_area]
        OT = [o_area[:, h * HP * N:(h + 1) * HP * N].rearrange("p (m n) -> p m n", m=HP) for h in HALVES]
        roped = o_area[:, :].rearrange("p (t n) -> p t n", t=TT)
        PT = pt_area[:, :].rearrange("p (i a n) -> p i a n", i=2, a=4)
        pt_cols = pt_area[:, :].rearrange("p (i s n) -> p i s n", i=2, s=2)
        rope_t = pt_area[:, :].rearrange("p (i a n) -> p i a n", i=2, a=2)
        qm = [a[:, 0:1024].rearrange("p (k s n) -> p k s n", k=KT, s=2) for a in qk_area]
        kT = [a[:, 1024:1536].rearrange("p (k n) -> p k n", k=KT) for a in qk_area]
        KVm = [a[:, 1536:2048].rearrange("p (k n) -> p k n", k=KT) for a in qk_area]
        AT = [[OT_area[:, :].rearrange("p (r a n) -> p r a n", r=4, a=4) for OT_area in
               (o_area[:, h * HP * N:(h + 1) * HP * N], qk_area[h][:, 2048:4096])] for h in HALVES]
        qkf = [a[:, 0:1024].rearrange("p (t n) -> p t n", t=TT) for a in v_area]
        elu_m = [a[:, 1024:2048].rearrange("p (t n) -> p t n", t=TT) for a in v_area]
        oTr = [a[:, 1024:2048].rearrange("p (m n) -> p m n", m=4) for a in v_area]
        oTT = [a[:, 512:1024].rearrange("p (k n) -> p k n", k=KT) for a in v_area]
        o_tok = [a[:, 0:512].rearrange("p (t n) -> p t n", t=TT) for a in v_area]
        cap = [a[:, 2048:2560].rearrange("p (t n) -> p t n", t=TT) for a in qk_area]
        pad_i = [sb(f"pad_i{h}", [P, N], I32) for h in HALVES]
        qn = [a[:, 0:256].bitcast(BF16).rearrange("p (t n) -> p t n", t=TT) for a in v_area]
        qnT = [a[:, 256:512].bitcast(BF16).rearrange("p (k n) -> p k n", k=KT) for a in v_area]
        negmax = sb("negmax", [P, 4, 2])
        rowsum = sb("rowsum", [P, 4, 2])
        rowinv = sb("rowinv", [P, 4, 2])
        stats = sb("stats", [P, TT, 6])
        mv = sb("mv", [P, 2, TT, 2])
        var_e = sb("var_e", [P, TT])
        rstd = sb("rstd", [P, 2, TT])
        amax = sb("amax", [P, TT])
        aq = sb("aq", [P, 2, TT])
        rden = sb("rden", [P, 2, H])
        wst = sb("wst", [P, KT, 4])
        ones = v_area[0][:, 0:P]
        diag = v_area[0][:, P:P + D].rearrange("p (k n) -> p k n", k=KT)

        bank = [ctx.enter_context(nc.psum_tensor(f"bank{i}", [P, 512], F32)) for i in range(8)]
        scratch = nc.dram_tensor("x_by_expert", (E, B, TE, D), F32, kind="Internal").ap()

        xq = kT

        full = [sem(f"full{b}") for b in range(8)]
        drained = [sem(f"drained{b}") for b in range(8)]
        consts_in = sem("consts_in")
        setup_in = sem("setup_in")
        x_in = [sem(f"x_in{h}") for h in HALVES]
        pad_in = [sem(f"pad_in{h}") for h in HALVES]
        stored = [sem(f"stored{h}") for h in HALVES]     
        setup_pool = sem("setup_pool")
        setup_dve = sem("setup_dve")
        setup_pe = sem("setup_pe")
        rope_done = sem("rope_done")
        s_max = sem("s_max")
        p_exp = sem("p_exp")
        p_norm = sem("p_norm")
        ln_stats = sem("ln_stats")
        ln_rstd = sem("ln_rstd")
        x_ready = sem("x_ready")
        xb_ready = sem("xb_ready")
        lin_min = sem("lin_min")
        lin_exp = sem("lin_exp")
        lin_feat = sem("lin_feat")
        qn_ready = sem("qn_ready")
        o_ready = sem("o_ready")
        cap_ready = sem("cap_ready")
        waits_passed = sem("waits_passed")
        dve_seq = sem("dve_seq")
        pool_seq = sem("pool_seq")
        w_in = [sem(f"w_in{i}") for i in HALVES]
        silu_done = sem("silu_done")
        moe_stats = sem("moe_stats")
        moe_rstd = sem("moe_rstd")
        y_ready = sem("y_ready")
        y_stored = [sem(f"y_stored{i}") for i in HALVES]
        y_free = [sem(f"y_free{i}") for i in HALVES]

        def nth(it, n, h, k, stage=0, stages=1):
            return it * (2 * n * stages) + ((2 * stage + h) * n + k)

        def filled(eng, it, h, stage, name):
            b, k = PLACE[(h, stage, name)]
            eng.wait_ge(full[b], it * FILLS[b] + (k + 1))
            return bank[b], drained[b]

        def emptied(eng, it, h, stage, name):
            b, k = PLACE[(h, stage, name)]
            eng.wait_ge(drained[b], it * FILLS[b] + (k + 2))

        def emptied_all(eng, it, h, stage, names):
            last = {PLACE[(h, stage, name)][0]: name for name in names}
            for name in last.values():
                emptied(eng, it, h, stage, name)

        def claim(eng, it, h, stage, name):
            b, k = PLACE[(h, stage, name)]
            eng.wait_ge(drained[b], it * FILLS[b] + (k + 1))
            return bank[b], full[b]

        def moe_at(it, i, name):
            b, k = MOE_PLACE[(i, "moe", name)]
            return b, it * MOE_FILLS[b] + (ITERS * FILLS[b] + k)

        def rows(dram):
            return dram.rearrange("(k p) n -> p k n", p=P)

        layers = ExitStack()
        block = layers.enter_context(nc.Block())

        def passed(eng):
            eng.sem_inc(waits_passed, 1)

        @block.sync
        def _(sp):
            sp.dma_start(xb[0][:, :, :], rows(ffn_d)).then_inc(setup_in, 16)
            sp.dma_start(r[0][:, :, :].bitcast(I32), rows(subm_d)).then_inc(setup_in, 16)
            loads = [
                (ident[:, :], ident_d), (rope0[:, :, :, :, :].rearrange("p t a c d -> p t (a c d)"), rope0_d.rearrange("(t p) n -> p t n", p=P)),
                (wqkv0, rows(wqkv0_d)),
                (rope1[:, :, :, :].rearrange("p t c d -> p t (c d)"), rope1_d.rearrange("(t p) n -> p t n", p=P)),
                (mask0[:, :, :], mask0_d), (tri[:, :], tri_d), (par[:, :], par_d), (bdm[:, :, :], bdm_d),
                (had[:, :, :], rows(had_d)), (wout0, rows(wout0_d)),
                (wq, rows(wq_d)), (wk, rows(wk_d)), (wv, rows(wv_d)), (wo, rows(wo_d)),
                (wqkv1[:, :, :], rows(wqkv1_d)), (wout1[:, :, :], rows(wout1_d)),
                (wqy[:, :, :], rows(wqy_d)), (wky[:, :, :], rows(wky_d)), (wvy[:, :, :], rows(wvy_d)),
                (bq[:, :], bq_d), (bk[:, :], bk_d), (bv[:, :], bv_d), (bqy[:, :], bqy_d), (bky[:, :], bky_d),
                (bo_row[:, :], bo_d.partition_broadcast(P)), (bvy_row[:, :], bvy_d.partition_broadcast(P)),
            ]
            assert len(loads) == N_CONST
            for dst, src in loads:
                sp.dma_start(dst, src).then_inc(consts_in, 16)
            with sp.Fori(0, ITERS) as it:
                for h in HALVES:
                    sp.wait_ge(xb_ready, nth(it, 1, h, 1, 1, 2))
                    g = it * 2 + h
                    sp.dma_start(x[h][:, :, :], x_d[bass.ds(g, 1)].rearrange("o (t p) n -> p (o t) n", p=P)).then_inc(x_in[h], 16)
                    sp.dma_start(cx[h][:, :, :], ctx_d[bass.ds(g, 1)].rearrange("o (t p) n -> p (o t) n", p=P)).then_inc(x_in[h], 16)
                    sp.dma_start(pad_i[h][:, :], padm_d[bass.ds(g, 1)].rearrange("o n -> (o n)").partition_broadcast(P)).then_inc(pad_in[h], 16)

        @block.gpsimd
        def _(pool):
            for b in range(8):
                pool.sem_inc(drained[b], 1)
            pool.sem_inc(rope_done, 2)
            pool.sem_inc(lin_min, 2)
            pool.sem_inc(xb_ready, 4)
            for h in HALVES:
                pool.sem_inc(y_free[h], 1)
            nc.gpsimd.memset(half_neg[:, :], -0.5).then_inc(setup_pool, 1)
            nc.gpsimd.memset(ones[:, :], 1.0).then_inc(setup_pool, 1)
            for h in HALVES:
                nc.gpsimd.memset(Vy[h][:, :, :, :], 0.0).then_inc(setup_pool, 1)
            pool.wait_ge(setup_pool, 4)
            for h in HALVES:
                nc.gpsimd.memset(Vy[h][:, :, :, D1:D1 + 1], 1.0).then_inc(setup_pool, 1)
            pool.wait_ge(setup_in, 32)
            nc.gpsimd.tensor_scalar(sub_kept[:, :, :], r[0][:, :, :].bitcast(I32), 0.0, None, ALU.is_equal).then_inc(setup_pool, 1)
            pool.wait_ge(setup_pool, 7)
            nc.gpsimd.tensor_scalar(sub_kept[:, :, :], sub_kept[:, :, :], -1.0, 1.0, ALU.mult, ALU.add).then_inc(setup_pool, 1)
            pool.wait_ge(setup_pool, 8)
            pool.wait_ge(consts_in, 16 * N_CONST)
            with pool.Fori(0, ITERS) as it:
                steps = 0

                def link(ins):
                    nonlocal steps
                    steps += 1
                    ins.then_inc(pool_seq, 1)
                    pool.wait_ge(pool_seq, it * POOL_LINKS + steps)
                    passed(pool)

                for h, stage in ORDER:
                    if stage == "qkv0":
                        for k in range(N_ROPE):
                            tt, n = divmod(k, 4)
                            emptied(pool, it, h, "qkv0", ("qk", k))
                            nc.gpsimd.tensor_tensor(roped[:, tt, n * 512:(n + 1) * 512], rope_t[:, k % 2, 0, :],
                                                    rope_t[:, k % 2, 1, :], ALU.add).then_inc(rope_done, 1)
                    if stage == "qkvx":
                        pool.wait_ge(x_ready, nth(it, 1, h, 1, 0, N_LN))
                        nc.gpsimd.tensor_tensor(xb[h][:, :, :], x[h][:, :, :], bo_row[:, None, :].broadcast_to([P, TT, D]),
                                                ALU.add).then_inc(xb_ready, 1)
                    if stage == "qkv1":
                        for tt in range(TT):
                            emptied(pool, it, h, "qkv1", ("qk", tt))
                            link(nc.gpsimd.tensor_tensor(qkf[h][:, tt, :], rope_t[:, tt, 0, :], rope_t[:, tt, 1, :], ALU.add))
                            nc.gpsimd.tensor_scalar(elu_m[h][:, tt, :], qkf[h][:, tt, :], 0.0, None, ALU.min).then_inc(lin_min, 1)
                    if stage == "qkvy":
                        pool.wait_ge(x_ready, nth(it, 1, h, 1, 3, N_LN))
                        pool.wait_ge(pad_in[h], it * 16 + 16)
                        passed(pool)
                        pad_k = cap[h][:, 0, :]
                        link(nc.gpsimd.tensor_scalar(pad_k, pad_i[h][:, :], 0.0, None, ALU.is_equal))
                        link(nc.gpsimd.tensor_scalar(pad_k, pad_k, -1.0, 1.0, ALU.mult, ALU.add))
                        link(nc.gpsimd.tensor_tensor(cap[h][:, 1, :], pad_k, sub_kept[:, 1, :], ALU.mult))
                        link(nc.gpsimd.tensor_tensor(cap[h][:, 0, :], pad_k, sub_kept[:, 0, :], ALU.mult))
                        nc.gpsimd.tensor_scalar(cap[h][:, :, :], cap[h][:, :, :], BIG, MASKED, ALU.mult, ALU.add).then_inc(cap_ready, 1)
                        emptied(pool, it, h, "qkvy", "xT")
                        nc.gpsimd.tensor_tensor(xb[h][:, :, :], x[h][:, :, :], bvy_row[:, None, :].broadcast_to([P, TT, D]),
                                                ALU.add).then_inc(xb_ready, 1)
                    if stage in LN:
                        i = LN[stage]
                        pool.wait_ge(ln_stats, nth(it, 1, h, 1, i, N_LN))
                        passed(pool)
                        link(nc.gpsimd.tensor_scalar(var_e[:, :], mv[:, h, :, 1], EPS, None, ALU.add))
                        nc.gpsimd.tensor_tensor(rstd[:, h, :], var_e[:, :], half_neg[:, :], ALU.pow).then_inc(ln_rstd, 1)
                    if stage == "outy":
                        pool.wait_ge(x_ready, nth(it, 1, h, 1, N_LN - 1, N_LN))
                        for e in range(E):
                            tt, q = divmod(e, 4)
                            pool.dma_start(scratch[e, bass.ds(it * 2 + h, 1)].rearrange("o t n -> (o t) n"),
                                           xb[h][TE * q:TE * q + TE, tt, :]).then_inc(stored[h], 16)
                for h in HALVES:
                    pool.wait_ge(stored[h], it * (16 * E) + 16 * E)
                assert steps == POOL_LINKS, f"POOL_LINKS {steps}"

        @block.scalar
        def _(act):
            act.wait_ge(setup_dve, N_SETUP_DVE)
            with act.Fori(0, ITERS) as it:

                def copy_out(h, stage, name, dst, shape=None, cols=512, **view):
                    b, done = filled(act, it, h, stage, name)
                    src = b[:, 0:cols]
                    if shape:
                        src = src.rearrange(shape, **view)
                    nc.scalar.activation(dst, src, ACT.Copy).then_inc(done, 1)

                for h, stage in ORDER:
                    if stage in ("load", "qkvx", "quant", "qkv1", "qkvy"):
                        copy_out(h, stage, "xT", xT[h][:, :, :], "p (k n) -> p k n", k=KT)
                    if stage == "qkv0":
                        for k in range(4):
                            tt, n = divmod(k, 2)
                            copy_out(h, stage, ("v", k), V[h][:, tt, n * 512:(n + 1) * 512])
                        for hp in range(HP):
                            copy_out(h, stage, ("qkT", hp), qkT[h][:, hp, :, :], "p (s n) -> p s n", s=2)
                    if stage == "qkvx":
                        for hp in range(0, HP, 2):
                            b, done = filled(act, it, h, stage, ("qk", hp))
                            nc.scalar.activation(qkT[h][:, hp, 0, :], b[:, 0:N], ACT.Identity, bias=bq_s[:, hp:hp + 1], scale=DH ** -0.5)
                            nc.scalar.activation(qkT[h][:, hp, 1, :], b[:, N:2 * N], ACT.Identity, bias=bk[:, hp:hp + 1]).then_inc(done, 1)
                        for k in range(0, 4, 2):
                            tt, n = divmod(k, 2)
                            copy_out(h, stage, ("v", k), V[h][:, tt, n * 512:(n + 1) * 512])
                    if stage in ATT:
                        for step in ATT_STEPS:
                            if LAG <= step < 2 * UNITS + LAG:
                                h, u = divmod(step - LAG, UNITS)
                                hp, qb = divmod(u, 2)
                                b, done = filled(act, it, h, stage, ("PT", u))
                                if stage == "atty":
                                    dst = PT[:, hp % 2, :, qb * P:(qb + 1) * P]
                                    src = b[:, :].rearrange("p (a n) -> p a n", a=4)
                                else:
                                    cols = 3 * P if stage == "att0" else 4 * P
                                    dst, src = pt_cols[:, hp % 2, qb, 0:cols], b[:, 0:cols]
                                nc.scalar.activation(dst, src, ACT.Copy).then_inc(done, 1)
                            if step < 2 * UNITS:
                                h, u = divmod(step, UNITS)
                                if stage == "att0":
                                    emptied(act, it, h, stage, ("S", u))
                                else:
                                    act.wait_ge(s_max, nth(it, UNITS, h, u + 1, stage == "atty", 2))
                                for s in range(2):
                                    bias = negmax[:, u % 4, s:s + 1]
                                    total = rowsum[:, u % 4, s:s + 1]
                                    if stage == "att0":
                                        keys = P * (s + 1)
                                        e = nc.scalar.activation(p_ring[:, u % 4, s, 0:keys], p_ring[:, u % 4, s, 0:keys],
                                                                 ACT.Exp, bias=bias, scale=-1.0, accum_out=total)
                                    elif stage == "attx":
                                        b = bank[PLACE[(h, stage, ("S", u))][0]]
                                        e = nc.scalar.activation(p_ring[:, u % 4, s, :], b[:, s * N:(s + 1) * N],
                                                                 ACT.Exp, bias=bias, accum_out=total)
                                    else:
                                        e = nc.scalar.activation(p_ring[:, u % 4, s, :], p_ring[:, u % 4, s, :], ACT.Exp, bias=bias)
                                if stage == "attx":
                                    e.then_inc(drained[PLACE[(h, stage, ("S", u))][0]], 1)
                                else:
                                    e.then_inc(p_exp, 1)
                    if stage == "ffn":
                        b, done = filled(act, it, h, stage, "qT")
                        nc.scalar.activation(qnT[h][:, :, :], b[:, 0:256].bitcast(BF16).rearrange("p (k n) -> p k n", k=KT), ACT.Copy).then_inc(done, 1)
                    if stage == "qkv1":
                        for tt in range(TT):
                            act.wait_ge(lin_min, nth(it, TT, h, tt + 1) + 2)
                            nc.scalar.activation(elu_m[h][:, tt, :], elu_m[h][:, tt, :], ACT.Exp).then_inc(lin_exp, 1)
                    if stage in ("qkv1", "qkvy"):
                        if stage == "qkvy":
                            b, done = filled(act, it, h, stage, "q")
                            for kt in range(KT):
                                q = nc.scalar.activation(xq[h][:, kt, :], b[:, kt * N:(kt + 1) * N], ACT.Identity,
                                                         bias=bqy_s[:, kt:kt + 1], scale=D1 ** -0.5)
                            q.then_inc(done, 1)
                        copy_out(h, stage, "v", Vy[h][:, :, :, 0:D1], "p (t a d) -> p t a d", t=TT, a=H)
                    if stage == "lin":
                        copy_out(h, stage, "kT", kT[h], "p (k n) -> p k n", k=KT)
                    if stage == "lout":
                        for i in range(2):
                            copy_out(h, stage, ("oT", i), oTr[h][:, 2 * i:2 * i + 2, :], "p (m n) -> p m n", m=2)
                    if stage == "out1":
                        copy_out(h, stage, "oTT", oTT[h][:, :, :], "p (k n) -> p k n", k=KT)

        @block.vector
        def _(dve):
            s = 0

            def setup(ins):
                nonlocal s
                s += 1
                ins.then_inc(setup_dve, 1)
                dve.wait_ge(setup_dve, s)

            dve.wait_ge(setup_in, 32)
            dve.wait_ge(consts_in, 16 * N_CONST)
            dve.wait_ge(setup_pool, 8)
            w = xb[0]
            gt, lt = xb[1], r[1]
            setup(nc.vector.tensor_reduce(wst[:, :, 0], w[:, :, :], AX.X, ALU.add, apply_absolute_value=True))
            setup(nc.vector.tensor_scalar(wst[:, :, 1], wst[:, :, 0], 1.0 / D, 1e-5, ALU.mult, ALU.max))
            setup(nc.vector.tensor_scalar(wst[:, :, 2], wst[:, :, 1], 0.5, None, ALU.mult))
            setup(nc.vector.tensor_scalar(wst[:, :, 3], wst[:, :, 1], -0.5, None, ALU.mult))
            for kt in range(KT):
                setup(nc.vector.tensor_scalar(gt[:, kt, :], w[:, kt, :], wst[:, kt, 2:3], None, ALU.is_gt))
                setup(nc.vector.tensor_scalar(lt[:, kt, :], w[:, kt, :], wst[:, kt, 3:4], None, ALU.is_lt))
                setup(nc.vector.tensor_scalar(diag[:, kt, :], ident[:, :], wst[:, kt, 1:2], None, ALU.mult))
            setup(nc.vector.tensor_tensor(gt[:, :, :], gt[:, :, :], lt[:, :, :], ALU.subtract))
            setup(nc.vector.tensor_scalar(bq_s[:, :], bq[:, :], DH ** -0.5, None, ALU.mult))
            setup(nc.vector.tensor_scalar(bqy_s[:, :], bqy[:, :], D1 ** -0.5, None, ALU.mult))
            setup(nc.vector.tensor_copy(identb[:, :], ident[:, :]))
            assert s == N_SETUP_DVE - 2
            dve.wait_ge(setup_pe, 1)
            setup(nc.vector.tensor_copy(ternT[:, :, :], bank[0][:, :].rearrange("p (k n) -> p k n", k=KT)))
            setup(nc.vector.tensor_copy(wscale_row[:, :], bank[1][:, 0:D]))
            with dve.Fori(0, ITERS) as it:
                steps = 0

                def link(ins, alone=False):
                    nonlocal steps
                    steps += 1
                    ins.then_inc(dve_seq, 1)
                    dve.wait_ge(dve_seq, it * DVE_LINKS + steps)
                    if alone:
                        passed(dve)

                def layer_norm(h, stage, dst):
                    i = LN[stage]
                    for tt in range(TT):
                        last = nc.vector.bn_stats(stats[:, tt, :], r[h][:, tt, :])
                    link(last, alone=True)
                    for tt in range(TT):
                        last = nc.vector.bn_aggr(mv[:, h, tt, :], stats[:, tt, :])
                    last.then_inc(ln_stats, 1)
                    dve.wait_ge(ln_rstd, nth(it, 1, h, 1, i, N_LN))
                    for tt in range(TT):
                        last = nc.vector.tensor_scalar(dst[:, tt, :], r[h][:, tt, :], mv[:, h, tt, 0:1], rstd[:, h, tt:tt + 1],
                                                       ALU.subtract, ALU.mult)
                    last.then_inc(x_ready, 1)

                def two(b):
                    return b[:, :].rearrange("p (t n) -> p t n", t=2)

                def residual(h, stage, res):
                    b, done = filled(dve, it, h, stage, "out")
                    nc.vector.tensor_tensor(r[h][:, :, :], two(b), res[:, :, :], ALU.add).then_inc(done, 1)
                    emptied(dve, it, h, stage, "out")

                def rotary(h, stage, k, slot, width, cos, sin):
                    b, done = filled(dve, it, h, stage, ("qk", k))
                    heads = 512 // width
                    nc.vector.tensor_tensor(rope_t[:, slot, 0, :].rearrange("p (h d) -> p h d", d=width),
                                            b[:, :].rearrange("p (h d) -> p h d", d=width),
                                            cos[:, None, :].broadcast_to([P, heads, width]), ALU.mult)
                    half = width // 2
                    for s in range(2):
                        last = nc.vector.tensor_tensor(
                            rope_t[:, slot, 1, :].rearrange("p (h s d) -> p h s d", s=2, d=half)[:, :, s, :],
                            b[:, :].rearrange("p (h s d) -> p h s d", s=2, d=half)[:, :, 1 - s, :],
                            sin[:, None, s * half:(s + 1) * half].broadcast_to([P, heads, half]), ALU.mult)
                    last.then_inc(done, 1)

                def normalised(h, stage, tt, guard):
                    b, done = filled(dve, it, h, stage, ("o", tt))
                    o = b[:, :].rearrange("p (h d) -> p h d", h=H)
                    link(nc.vector.tensor_scalar(rden[:, 0, :], o[:, :, D1], guard, None, ALU.max))
                    link(nc.vector.reciprocal(rden[:, 1, :], rden[:, 0, :]))
                    nc.vector.tensor_tensor(o_tok[h][:, tt, :].rearrange("p (h d) -> p h d", h=H), o[:, :, 0:D1],
                                            rden[:, 1, :, None].broadcast_to([P, H, D1]), ALU.mult).then_inc(done, 1)

                for h, stage in ORDER:
                    if stage == "load":
                        b, done = filled(dve, it, h, stage, "cT")
                        nc.vector.tensor_copy(cT[h][:, :, :], two(b)).then_inc(done, 1)
                    if stage == "qkv0":
                        for k in range(N_ROPE):
                            tt, n = divmod(k, 4)
                            dve.wait_ge(rope_done, nth(it, N_ROPE, h, k + 1))
                            rotary(h, stage, k, k % 2, DH, rope0[:, tt, n // 2, 0, :], rope0[:, tt, n // 2, 1, :])
                    if stage == "qkvx":
                        for hp in range(1, HP, 2):
                            b, done = filled(dve, it, h, stage, ("qk", hp))
                            nc.vector.tensor_scalar(qkT[h][:, hp, 0, :], b[:, 0:N], bq[:, hp:hp + 1], DH ** -0.5, ALU.add, ALU.mult)
                            nc.vector.tensor_scalar(qkT[h][:, hp, 1, :], b[:, N:2 * N], bk[:, hp:hp + 1], None, ALU.add).then_inc(done, 1)
                        for k in range(1, 4, 2):
                            tt, n = divmod(k, 2)
                            b, done = filled(dve, it, h, stage, ("v", k))
                            nc.vector.tensor_copy(V[h][:, tt, n * 512:(n + 1) * 512], b[:, :]).then_inc(done, 1)
                    if stage in ATT:
                        for step in ATT_STEPS:
                            if step < 2 * UNITS:
                                h, u = divmod(step, UNITS)
                                b, done = filled(dve, it, h, stage, ("S", u))
                                if stage == "att0":
                                    passed(dve)
                                if stage == "att0":
                                    for s in range(2):
                                        keys = P * (s + 1)
                                        mask = mask0[:, s:2 * s + 1, :].rearrange("p a n -> p (a n)")
                                        last = nc.vector.tensor_tensor_reduce(p_ring[:, u % 4, s, 0:keys], b[:, s * N:s * N + keys], mask,
                                                                              1.0, BIG, ALU.add, ALU.min, negmax[:, u % 4, s:s + 1])
                                    last.then_inc(done, 1)
                                elif stage == "attx":
                                    nc.vector.tensor_reduce(negmax[:, u % 4, :], two(b), AX.X, ALU.max, negate=True).then_inc(s_max, 1)
                                else:
                                    nc.vector.tensor_tensor(p_ring[:, u % 4, :, :], two(b),
                                                            cap[h][:, u % 2, None, :].broadcast_to([P, 2, N]), ALU.min).then_inc(done, 1)
                                    emptied(dve, it, h, stage, ("S", u))
                                    nc.vector.tensor_reduce(negmax[:, u % 4, :], p_ring[:, u % 4, :, :], AX.X, ALU.max, negate=True).then_inc(s_max, 1)
                            if 1 <= step < 2 * UNITS + 1 and stage != "atty":
                                h, u = divmod(step - 1, UNITS)
                                if stage == "attx":
                                    emptied(dve, it, h, stage, ("S", u))
                                else:
                                    dve.wait_ge(p_exp, nth(it, UNITS, h, u + 1, 0, 2))
                                link(nc.vector.reciprocal(rowinv[:, u % 4, :], rowsum[:, u % 4, :]))
                                for s in range(2):
                                    keys = N if stage == "attx" else P * (s + 1)
                                    last = nc.vector.tensor_scalar(p_ring[:, u % 4, s, 0:keys], p_ring[:, u % 4, s, 0:keys],
                                                                   rowinv[:, u % 4, s:s + 1], None, ALU.mult)
                                last.then_inc(p_norm, 1)
                            if step > O_LAG and (step - O_LAG) % 2:
                                h, hp = divmod((step - O_LAG) // 2, HP)
                                if stage == "atty":
                                    if hp % 2:
                                        b, done = filled(dve, it, h, stage, ("O", hp - 1))
                                        nc.vector.tensor_copy(oTr[h][:, hp // 2, :], b[:, 0:N]).then_inc(done, 1)
                                else:
                                    b, done = filled(dve, it, h, stage, ("O", hp))
                                    if stage == "att0":
                                        nc.vector.tensor_copy(OT[h][:, hp, :], b[:, 0:N]).then_inc(done, 1)
                                    else:
                                        nc.vector.tensor_scalar(OT[h][:, hp, :], b[:, 0:N], bv[:, hp:hp + 1], None, ALU.add).then_inc(done, 1)
                    if stage in ("out0", "outx", "out1"):
                        if stage == "out0":
                            dve.wait_ge(x_in[h], it * 32 + 32)
                        if stage == "outx":
                            dve.wait_ge(xb_ready, nth(it, 1, h, 1, 0, 2) + 4)
                        residual(h, stage, xb[h] if stage == "outx" else x[h])
                        layer_norm(h, stage, x[h])
                    if stage == "quant":
                        b, done = filled(dve, it, h, stage, "xh")
                        link(nc.vector.tensor_reduce(amax[:, :], two(b), AX.X, ALU.max, apply_absolute_value=True))
                        link(nc.vector.tensor_scalar(aq[:, h, :], amax[:, :], 1e-5, 1.0 / 7.0, ALU.max, ALU.mult))
                        link(nc.vector.reciprocal(amax[:, :], aq[:, h, :]))
                        for tt in range(TT):
                            last = nc.vector.tensor_scalar(r[h][:, tt, :], b[:, tt * D:(tt + 1) * D], amax[:, tt:tt + 1], MAGIC, ALU.mult, ALU.add)
                        last.then_inc(done, 1)
                        emptied(dve, it, h, stage, "xh")
                        link(nc.vector.tensor_scalar(r[h][:, :, :], r[h][:, :, :], MAGIC, -8.0, ALU.subtract, ALU.max))
                        nc.vector.tensor_scalar(qn[h][:, :, :], r[h][:, :, :], 7.0, None, ALU.min).then_inc(qn_ready, 1)
                    if stage == "ffn":
                        b, done = filled(dve, it, h, stage, "out")
                        for tt in range(TT):
                            last = nc.vector.scalar_tensor_tensor(out=r[h][:, tt, :], in0=b[:, tt * D:(tt + 1) * D], scalar=aq[:, h, tt:tt + 1],
                                                                  in1=wscale_row[:, :], op0=ALU.mult, op1=ALU.mult)
                        last.then_inc(done, 1)
                        emptied(dve, it, h, stage, "out")
                        link(nc.vector.tensor_tensor(r[h][:, :, :], r[h][:, :, :], x[h][:, :, :], ALU.add))
                        layer_norm(h, stage, x[h])
                    if stage == "qkv1":
                        for tt in range(TT):
                            dve.wait_ge(lin_min, nth(it, TT, h, tt + 1))
                            rotary(h, stage, tt, tt, D1, rope1[:, tt, 0, :], rope1[:, tt, 1, :])
                        for tt in range(TT):
                            dve.wait_ge(lin_exp, nth(it, TT, h, tt + 1))
                            nc.vector.scalar_tensor_tensor(out=qkf[h][:, tt, :], in0=qkf[h][:, tt, :], scalar=0.0, in1=elu_m[h][:, tt, :],
                                                           op0=ALU.max, op1=ALU.add).then_inc(lin_feat, 1)
                    if stage == "lin":
                        b, done = filled(dve, it, h, stage, "qT")
                        for s in range(2):
                            last = nc.vector.tensor_scalar(qm[h][:, :, s, :], two(b), par[:, s:s + 1], None, ALU.mult)
                        last.then_inc(done, 1)
                        b, done = filled(dve, it, h, stage, "KV")
                        nc.vector.tensor_tensor(KVm[h][:, :, :], two(b),
                                                bdm[:, :, :].rearrange("p h v -> p (h v)")[:, None, :].broadcast_to([P, KT, 8 * VW]),
                                                ALU.mult).then_inc(done, 1)
                        for c in range(TT):
                            for q in range(4):
                                b, done = filled(dve, it, h, stage, ("A", c, q))
                                nc.vector.tensor_tensor(AT[h][c][:, q, :, :], b[:, :].rearrange("p (a n) -> p a n", a=4),
                                                        tri[:, None, :].broadcast_to([P, 4, P]), ALU.mult).then_inc(done, 1)
                    if stage == "lout":
                        for tt in range(TT):
                            normalised(h, stage, tt, 1e-6)
                        emptied(dve, it, h, stage, ("o", TT - 1))
                    if stage == "qkvy":
                        b, done = filled(dve, it, h, stage, "k")
                        for kt in range(KT):
                            for s in range(2):
                                last = nc.vector.tensor_scalar(qm[h][:, kt, s, :], b[:, kt * N:(kt + 1) * N], bky[:, kt:kt + 1],
                                                               par[:, s:s + 1], ALU.add, ALU.mult)
                        last.then_inc(done, 1)
                        dve.wait_ge(cap_ready, nth(it, 1, h, 1))
                    if stage == "outy":
                        for tt in range(TT):
                            normalised(h, stage, tt, 0.0)
                        emptied(dve, it, h, stage, ("o", TT - 1))
                        dve.wait_ge(xb_ready, nth(it, 1, h, 1, 1, 2) + 4)
                        link(nc.vector.tensor_tensor(r[h][:, :, :], o_tok[h][:, :, :], xb[h][:, :, :], ALU.add))
                        layer_norm(h, stage, xb[h])
                assert steps == DVE_LINKS, f"DVE_LINKS {steps}"

        @block.tensor
        def _(pe):
            mm, tr = nc.tensor.matmul, nc.tensor.transpose
            pe.wait_ge(setup_dve, N_SETUP_DVE - 2)
            for kt in range(KT):
                for ot in range(KT):
                    tr(bank[0][:, kt * D + ot * P:kt * D + (ot + 1) * P], xb[1][:, ot, kt * P:(kt + 1) * P], ident[:, :])
            for kt in range(KT):
                last = mm(bank[1][:, kt * P:(kt + 1) * P], ones[:, :], diag[:, kt, :], start=True, stop=True)
            last.then_inc(setup_pe, 1)
            pe.wait_ge(setup_dve, N_SETUP_DVE)
            with pe.Fori(0, ITERS) as it:

                def turn(h, stage, name, src):
                    b, done = claim(pe, it, h, stage, name)
                    for kt in range(KT):
                        for tt in range(TT):
                            last = tr(b[:, kt * N + tt * P:kt * N + (tt + 1) * P], src[:, tt, kt * P:(kt + 1) * P], ident[:, :])
                    last.then_inc(done, 1)

                def product(out, pairs):
                    for i, (lhsT, rhs) in enumerate(pairs):
                        last = mm(out, lhsT, rhs, start=(i == 0), stop=(i == len(pairs) - 1))
                    return last

                def token_tiles(h, stage, name, lhs, rhs, n):
                    b, done = claim(pe, it, h, stage, name)
                    for tt in range(TT):
                        last = product(b[:, tt * D:(tt + 1) * D], [(lhs(k, tt), rhs(k)) for k in range(n)])
                    last.then_inc(done, 1)

                def tok(t, tt):
                    return slice(tt * t, (tt + 1) * t)

                for h, stage in PE_ORDER:
                    if stage == "load":
                        pe.wait_ge(x_in[h], it * 32 + 32)
                        turn(h, stage, "xT", x[h])
                        turn(h, stage, "cT", cx[h])
                    if stage in ("qkvx", "quant", "qkv1", "qkvy"):
                        before = {"qkvx": 1, "quant": 2, "qkv1": 3, "qkvy": 4}[stage]
                        pe.wait_ge(x_ready, nth(it, 1, h, 1, before - 1, N_LN))
                        turn(h, stage, "xT", x[h])
                    if stage == "qkv0":
                        emptied(pe, it, h, "load", "xT")
                        for kind, count in (("qk", N_ROPE), ("v", 4)):
                            for k in range(count):
                                tt, n = divmod(k, count // TT)
                                col = n * 512 + (2 * IN0 if kind == "v" else 0)
                                b, done = claim(pe, it, h, stage, (kind, k))
                                product(b[:, :], [(xT[h][:, kt, tok(P, tt)], wqkv0[:, kt, col:col + 512]) for kt in range(KT)]).then_inc(done, 1)
                        pe.wait_ge(rope_done, nth(it, N_ROPE, h, N_ROPE) + 2)
                        for hp in range(HP):
                            b, done = claim(pe, it, h, stage, ("qkT", hp))
                            for s in range(2):
                                for tt in range(TT):
                                    last = tr(b[:, s * N + tt * P:s * N + (tt + 1) * P], roped[:, tt, s * IN0 + hp * P:s * IN0 + (hp + 1) * P], ident[:, :])
                            last.then_inc(done, 1)
                    if stage == "qkvx":
                        emptied(pe, it, h, "load", "cT")
                        emptied(pe, it, h, stage, "xT")
                        for hp in range(HP):
                            b, done = claim(pe, it, h, stage, ("qk", hp))
                            product(b[:, 0:N], [(wq[:, kt, tok(P, hp)], xT[h][:, kt, :]) for kt in range(KT)])
                            product(b[:, N:2 * N], [(wk[:, kt, tok(P, hp)], cT[h][:, kt, :]) for kt in range(KT)]).then_inc(done, 1)
                        for k in range(4):
                            tt, n = divmod(k, 2)
                            b, done = claim(pe, it, h, stage, ("v", k))
                            product(b[:, :], [(cT[h][:, kt, tok(P, tt)], wv[:, kt, n * 512:(n + 1) * 512]) for kt in range(KT)]).then_inc(done, 1)
                    if stage.removesuffix("_end") in ATT:
                        steps = ATT_STEPS[ATT_END:] if stage.endswith("_end") else ATT_STEPS[:ATT_END]
                        stage = stage.removesuffix("_end")
                        prev = {"att0": "qkv0", "attx": "qkvx", "atty": "qkvy"}[stage]
                        for step in steps:
                            if step < 2 * UNITS:
                                h, u = divmod(step, UNITS)
                                if u == 0:
                                    emptied_all(pe, it, h, prev, ("q", "k", "v") if stage == "atty" else [("v", k) for k in range(4)])
                                hp, qb = divmod(u, 2)
                                if stage != "atty" and u % 2 == 0:
                                    emptied(pe, it, h, prev, ("qkT" if stage == "att0" else "qk", hp))
                                b, done = claim(pe, it, h, stage, ("S", u))
                                if stage == "atty":
                                    kt, q = divmod(hp, 4)
                                    last = mm(b[:, :], xq[h][32 * q:32 * q + 32, kt, tok(P, qb)],
                                              qm[h][32 * q:32 * q + 32, kt, :, :], start=True, stop=True)
                                else:
                                    head = slice(DH * (u % 2), DH * (u % 2) + DH)
                                    for qb in range(TT):
                                        keys = N if stage == "attx" else P * (qb + 1)
                                        last = mm(b[:, qb * N:qb * N + keys], qkT[h][head, hp, 0, tok(P, qb)],
                                                  qkT[h][head, hp, 1, 0:keys], start=True, stop=True)
                                last.then_inc(done, 1)
                            if LAG <= step < 2 * UNITS + LAG:
                                h, u = divmod(step - LAG, UNITS)
                                if stage == "atty":
                                    pe.wait_ge(p_exp, nth(it, UNITS, h, u + 1, 1, 2))
                                else:
                                    pe.wait_ge(p_norm, nth(it, UNITS, h, u + 1, stage == "attx", 2))
                                b, done = claim(pe, it, h, stage, ("PT", u))
                                for s in range(2):
                                    for kb in range(TT):
                                        if stage == "atty":
                                            col = 2 * s + kb
                                        elif stage == "attx":
                                            col = 2 * kb + s
                                        else:
                                            if kb > s:
                                                continue
                                            col = kb + s
                                        last = tr(b[:, tok(P, col)], p_ring[:, u % 4, s, tok(P, kb)], ident[:, :])
                                last.then_inc(done, 1)
                            if step >= O_LAG and (step - O_LAG) % 2 == 0:
                                h, hp = divmod((step - O_LAG) // 2, HP)
                                emptied_all(pe, it, h, stage, [("PT", 2 * hp), ("PT", 2 * hp + 1)])
                                if stage == "atty":
                                    if hp % 2 == 0:
                                        o_bank, o_done = claim(pe, it, h, stage, ("O", hp))
                                    for kb in range(TT):
                                        for s in range(2):
                                            j = 2 * (hp % 2) + s
                                            last = mm(o_bank[32 * j:32 * j + 32, 0:N], Vy[h][:, kb, 2 * hp + s, :], PT[:, hp % 2, 2 * s + kb, :],
                                                      start=(kb == 0), stop=(kb == 1))
                                    if hp % 2:
                                        last.then_inc(o_done, 1)
                                else:
                                    b, done = claim(pe, it, h, stage, ("O", hp))
                                    for kb in range(TT):
                                        for s in range(2):
                                            q0 = P if stage == "att0" and kb else 0
                                            last = mm(b[64 * s:64 * s + 64, q0:N], V[h][:, kb, (2 * hp + s) * DH:(2 * hp + s + 1) * DH],
                                                      pt_cols[:, hp % 2, s, kb * N:kb * N + N - q0], start=(kb == 0), stop=(kb == 1))
                                    last.then_inc(done, 1)
                    if stage in ("out0", "outx"):
                        att = "att0" if stage == "out0" else "attx"
                        w = wout0 if stage == "out0" else wo
                        emptied(pe, it, h, att, ("O", HP - 1))
                        token_tiles(h, stage, "out", lambda k, tt: OT[h][:, k, tok(P, tt)], lambda k: w[:, k, :], HP)
                    if stage == "quant":
                        emptied(pe, it, h, stage, "xT")
                        token_tiles(h, stage, "xh", lambda k, tt: xT[h][:, k, tok(P, tt)], lambda k: had[:, k, :], KT)
                    if stage == "ffn":
                        pe.wait_ge(qn_ready, nth(it, 1, h, 1))
                        b, done = claim(pe, it, h, stage, "qT")
                        bb = b[:, 0:256].bitcast(BF16)
                        for kt in range(KT):
                            for tt in range(TT):
                                last = tr(bb[:, kt * N + tt * P:kt * N + (tt + 1) * P], qn[h][:, tt, tok(P, kt)], identb[:, :])
                        last.then_inc(done, 1)
                        emptied(pe, it, h, stage, "qT")
                        token_tiles(h, stage, "out", lambda k, tt: qnT[h][:, k, tok(P, tt)], lambda k: ternT[:, k, :], KT)
                    if stage == "qkv1":
                        emptied(pe, it, h, stage, "xT")
                        for tt in range(TT):
                            b, done = claim(pe, it, h, stage, ("qk", tt))
                            product(b[:, :], [(xT[h][:, kt, tok(P, tt)], wqkv1[:, kt, 0:512]) for kt in range(KT)]).then_inc(done, 1)
                        token_tiles(h, stage, "v", lambda k, tt: xT[h][:, k, tok(P, tt)], lambda k: wqkv1[:, k, 512:768], KT)
                    if stage == "lin":
                        pe.wait_ge(lin_feat, nth(it, TT, h, TT))
                        turn(h, stage, "qT", qkf[h][:, :, 0:D])
                        turn(h, stage, "kT", qkf[h][:, :, D:2 * D])
                        emptied(pe, it, h, "qkv1", "v")
                        b, done = claim(pe, it, h, stage, "KV")
                        for kt in range(KT):
                            last = mm(b[:, kt * 256:(kt + 1) * 256], qkf[h][:, 0, D + kt * P:D + (kt + 1) * P],
                                      Vy[h][:, 0, 8 * kt:8 * kt + 8, :], start=True, stop=True)
                        last.then_inc(done, 1)
                        emptied_all(pe, it, h, stage, ("qT", "kT"))
                        for c in range(TT):
                            for q in range(4):
                                b, done = claim(pe, it, h, stage, ("A", c, q))
                                for kt in range(KT):
                                    last = mm(b[:, kt * 256:(kt + 1) * 256], kT[h][32 * q:32 * q + 32, kt, tok(P, c)],
                                              qm[h][32 * q:32 * q + 32, kt, :, tok(P, c)], start=True, stop=True)
                                last.then_inc(done, 1)
                    if stage == "lout":
                        emptied(pe, it, h, "lin", "KV")
                        emptied_all(pe, it, h, "lin", [("A", c, q) for c in range(TT) for q in range(4)])
                        for kt in range(KT):
                            b, done = claim(pe, it, h, stage, ("oT", kt))
                            for mi in range(2):
                                for c in range(TT):
                                    for j in range(4):
                                        lh = 4 * mi + j
                                        q, s = divmod(lh, 2)
                                        out = b[32 * j:32 * j + 32, mi * N + c * P:mi * N + (c + 1) * P]
                                        last = mm(out, Vy[h][:, c, 8 * kt + lh, :], AT[h][c][:, q, 2 * kt + s, :],
                                                  start=True, stop=(c == 0))
                                    if c == 1:
                                        for j in range(4):
                                            lh = 4 * mi + j
                                            out = b[32 * j:32 * j + 32, mi * N + P:mi * N + 2 * P]
                                            last = mm(out, KVm[h][:, kt, lh * VW:(lh + 1) * VW], qm[h][:, kt, lh % 2, P:2 * P],
                                                      start=False, stop=True)
                            last.then_inc(done, 1)
                    if stage in ("lout", "outy"):
                        if stage == "lout":
                            emptied_all(pe, it, h, stage, [("oT", kt) for kt in range(KT)])
                        else:
                            emptied(pe, it, h, "atty", ("O", HP - 2))
                        for tt in range(TT):
                            b, done = claim(pe, it, h, stage, ("o", tt))
                            for m in range(4):
                                last = tr(b[:, tok(P, m)], oTr[h][:, m, tok(P, tt)], ident[:, :])
                            last.then_inc(done, 1)
                    if stage == "out1":
                        emptied_all(pe, it, h, "lout", [("o", tt) for tt in range(TT)])
                        turn(h, stage, "oTT", o_tok[h])
                        emptied(pe, it, h, stage, "oTT")
                        token_tiles(h, stage, "out", lambda k, tt: oTT[h][:, k, tok(P, tt)], lambda k: wout1[:, k, :], KT)
                    if stage == "qkvy":
                        emptied(pe, it, h, stage, "xT")
                        for name, w, src in (("q", wqy, xT[h]), ("k", wky, cT[h])):
                            b, done = claim(pe, it, h, stage, name)
                            for ft in range(KT):
                                last = product(b[:, ft * N:(ft + 1) * N], [(w[:, kt, tok(P, ft)], src[:, kt, :]) for kt in range(KT)])
                            last.then_inc(done, 1)
                        token_tiles(h, stage, "v", lambda k, tt: cT[h][:, k, tok(P, tt)], lambda k: wvy[:, k, :], KT)

        layers.close()

        xe, xeT, re, ye = x, xT, r, xb
        hT = [qk_area[i][:, 0:FT * N].rearrange("p (j n) -> p j n", j=FT) for i in HALVES]
        sg = v_area[0][:, 0:4 * N].rearrange("p (j n) -> p j n", j=4)

        def width(j):
            return P if j < FT - 1 else FR

        experts = ctx.enter_context(nc.Block())

        @experts.sync
        def _(sp):
            with sp.Fori(0, ITERS) as it:
                for i in HALVES:
                    b, k = moe_at(it, i, "out")
                    sp.wait_ge(drained[b], k + 1)
                    e = it * 2 + i
                    sp.dma_start(w1[i], w1_d[bass.ds(e, 1)].rearrange("o (k p) n -> p (o k) n", p=P)).then_inc(w_in[i], 16)
                    sp.dma_start(w3[i], w3_d[bass.ds(e, 1)].rearrange("o (k p) n -> p (o k) n", p=P)).then_inc(w_in[i], 16)
                    main = (FT - 1) * P
                    sp.dma_start(w2[i][:, 0:FT - 1, :], w2_d[bass.ds(e, 1), 0:main].rearrange("o (k p) n -> p (o k) n", p=P)).then_inc(w_in[i], 16)
                    sp.dma_start(w2[i][0:FR, FT - 1, :], w2_d[bass.ds(e, 1), main:F].rearrange("o p n -> p (o n)")).then_inc(w_in[i], 16)
                    sp.dma_start(xe[i][:, :, :], scratch[bass.ds(e, 1)].rearrange("o (t b) s n -> (b s) (o t) n", t=TT)).then_inc(w_in[i], 16)

        @experts.gpsimd
        def _(pool):
            with pool.Fori(0, ITERS) as it:
                for i in HALVES:
                    pool.wait_ge(moe_stats, nth(it, 1, i, 1))
                    passed(pool)
                    nc.gpsimd.tensor_scalar(var_e[:, :], mv[:, i, :, 1], EPS, None, ALU.add).then_inc(pool_seq, 1)
                    pool.wait_ge(pool_seq, nth(it, 1, i, 1) + ITERS * POOL_LINKS)
                    nc.gpsimd.tensor_tensor(rstd[:, i, :], var_e[:, :], half_neg[:, :], ALU.pow).then_inc(moe_rstd, 1)
                    pool.wait_ge(y_ready, nth(it, 1, i, 1))
                    for b in range(B):
                        tt, q = divmod(b, 4)
                        pool.dma_start(out_d[b, bass.ds((it * 2 + i) * TE, TE), :], ye[i][TE * q:TE * q + TE, tt, :]).then_inc(y_stored[i], 16)
                for i in HALVES:
                    pool.wait_ge(y_stored[i], it * (16 * B) + 16 * B)
                    pool.sem_inc(y_free[i], 1)

        @experts.scalar
        def _(act):
            with act.Fori(0, ITERS) as it:
                for i in HALVES:
                    b, k = moe_at(it, i, "xT")
                    act.wait_ge(full[b], k + 1)
                    nc.scalar.activation(xeT[i][:, :, :], bank[b][:, :].rearrange("p (k n) -> p k n", k=KT), ACT.Copy).then_inc(drained[b], 1)
                    for j in range(FT):
                        b, k = moe_at(it, i, ("gu", j))
                        act.wait_ge(full[b], k + 1)
                        w = width(j)
                        nc.scalar.activation(sg[0:w, b - 1, :], bank[b][0:w, 0:N], ACT.Silu).then_inc(silu_done, 1)

        @experts.vector
        def _(dve):
            steps = 0
            with dve.Fori(0, ITERS) as it:
                for i in HALVES:
                    for j in range(FT):
                        b, k = moe_at(it, i, ("gu", j))
                        w = width(j)
                        dve.wait_ge(silu_done, nth(it, FT, i, j + 1))
                        nc.vector.tensor_tensor(hT[i][0:w, j, :], sg[0:w, b - 1, :], bank[b][0:w, N:2 * N], ALU.mult).then_inc(drained[b], 1)
                    b, k = moe_at(it, i, "out")
                    dve.wait_ge(full[b], k + 1)
                    dve.wait_ge(w_in[i], it * 80 + 80)
                    nc.vector.tensor_tensor(re[i][:, :, :], bank[b][:, :].rearrange("p (t n) -> p t n", t=TT), xe[i][:, :, :], ALU.add).then_inc(drained[b], 1)
                    dve.wait_ge(drained[b], k + 2)
                    for tt in range(TT):
                        last = nc.vector.bn_stats(stats[:, tt, :], re[i][:, tt, :])
                    last.then_inc(dve_seq, 1)
                    dve.wait_ge(dve_seq, nth(it, 1, i, 1) + ITERS * DVE_LINKS)
                    passed(dve)
                    for tt in range(TT):
                        last = nc.vector.bn_aggr(mv[:, i, tt, :], stats[:, tt, :])
                    last.then_inc(moe_stats, 1)
                    dve.wait_ge(moe_rstd, nth(it, 1, i, 1))
                    dve.wait_ge(y_free[i], it + 1)
                    for tt in range(TT):
                        last = nc.vector.tensor_scalar(ye[i][:, tt, :], re[i][:, tt, :], mv[:, i, tt, 0:1], rstd[:, i, tt:tt + 1],
                                                       ALU.subtract, ALU.mult)
                    last.then_inc(y_ready, 1)

        @experts.tensor
        def _(pe):
            mm = nc.tensor.matmul
            with pe.Fori(0, ITERS) as it:
                for i in HALVES:
                    pe.wait_ge(w_in[i], it * 80 + 80)
                    b, k = moe_at(it, i, "xT")
                    pe.wait_ge(drained[b], k + 1)
                    for kt in range(KT):
                        for tt in range(TT):
                            last = nc.tensor.transpose(bank[b][:, kt * N + tt * P:kt * N + (tt + 1) * P], xe[i][:, tt, kt * P:(kt + 1) * P], ident[:, :])
                    last.then_inc(full[b], 1)
                    pe.wait_ge(drained[b], k + 2)
                    for j in range(FT):
                        b, k = moe_at(it, i, ("gu", j))
                        pe.wait_ge(drained[b], k + 1)
                        w = width(j)
                        for s, wx in enumerate((w1[i], w3[i])):
                            for kt in range(KT):
                                last = mm(bank[b][0:w, s * N:(s + 1) * N], wx[:, kt, j * P:j * P + w], xeT[i][:, kt, :],
                                          start=(kt == 0), stop=(kt == KT - 1))
                        last.then_inc(full[b], 1)
                    for j in range(FT - 4, FT):
                        gb, gk = moe_at(it, i, ("gu", j))
                        pe.wait_ge(drained[gb], gk + 2)
                    b, k = moe_at(it, i, "out")
                    pe.wait_ge(drained[b], k + 1)
                    for tt in range(TT):
                        for j in range(FT):
                            w = width(j)
                            last = mm(bank[b][:, tt * D:(tt + 1) * D], hT[i][0:w, j, tt * P:(tt + 1) * P], w2[i][0:w, j, :],
                                      start=(j == 0), stop=(j == FT - 1))
                    last.then_inc(full[b], 1)


def shape_constants():
    f32 = np.float32

    def rotary(dh, tokens):
        inv = (1.0 / 10000.0 ** (np.arange(0, dh, 2, dtype=np.float64) / dh)).astype(f32)
        angle = (np.arange(tokens, dtype=f32)[:, None] * inv[None, :]).astype(f32)
        c, s = np.cos(angle.astype(np.float64)), np.sin(angle.astype(np.float64))
        return np.concatenate([c, c], 1), np.concatenate([-s, s], 1)

    c0, s0 = rotary(DH, N)
    rope0 = np.stack([np.stack([-c0, -s0], 1) * DH ** -0.5, np.stack([c0, s0], 1)], 1)
    c1, s1 = rotary(D1, N)
    rope1 = np.stack([c1, s1], 1) * D1 ** -0.25
    q, k = np.arange(P)[:, None], np.arange(P)[None, :]
    causal = np.where(k <= q, 0.0, BIG)
    window = np.where(k >= q, 0.0, BIG)
    mask0 = np.stack([causal, window, causal], 1)
    tri = (q <= k) * 1.0
    parity = np.stack([(np.arange(P) % 32) < 16, (np.arange(P) % 32) >= 16], 1) * 1.0
    bdm = np.repeat((np.arange(P)[:, None] // D1 == np.arange(8)[None, :])[:, :, None], VW, 2) * 1.0
    had = np.ones((1, 1))
    while had.shape[0] < D:
        had = np.block([[had, had], [had, -had]])
    had = had / np.sqrt(D)
    return {"c_ident": np.eye(P), "c_rope0": rope0.reshape(N, -1), "c_rope1": rope1.reshape(N, -1), "c_mask0": mask0,
            "c_tri": tri, "c_par": parity, "c_bdm": bdm, "c_had": had}


def kernel(**inputs):
    import concourse.bacc as bacc
    from concourse.bass_utils import run_bass_kernel_spmd

    def arr(name):
        return np.asarray(inputs[name])

    def columns(a):
        return np.ascontiguousarray(a.reshape(-1, P).T)

    feeds = {
        "x": arr("x"), "ctx": arr("ctx_1024"),
        "padm": arr("mask_Bx1x1xS2_ik0").reshape(B, N), "subm": arr("mask_1x1xSxS2_ik0").reshape(N, N),
        "wqkv0": arr("L0_attn_W_qkv"), "wout0": arr("L0_attn_W_out"),
        "wq": arr("L0_xattn_Wq").reshape(D, IN0), "bq": columns(arr("L0_xattn_bq")),
        "wk": arr("L0_xattn_Wk").reshape(D, IN0), "bk": columns(arr("L0_xattn_bk")),
        "wv": arr("L0_xattn_Wv").reshape(D, IN0), "bv": columns(arr("L0_xattn_bv")),
        "wo": arr("L0_xattn_Wo").reshape(IN0, D), "bo": arr("L0_xattn_bo"),
        "ffn": arr("L0_ffn_weight"), "wqkv1": arr("L1_attn_w_qkv"), "wout1": arr("L1_attn_w_out"),
        "wqy": arr("L1_xattn_Wq").T, "bqy": columns(arr("L1_xattn_bq")),
        "wky": arr("L1_xattn_Wk").T, "bky": columns(arr("L1_xattn_bk")),
        "wvy": arr("L1_xattn_Wv").T, "bvy": arr("L1_xattn_bv"),
        "w1": arr("L1_ffn_w1"), "w3": arr("L1_ffn_w3"), "w2": arr("L1_ffn_w2"),
    }
    for name, a in shape_constants().items():
        feeds[name] = a.astype(np.float32)
    nc = bacc.Bacc("TRN2", target_bir_lowering=False, num_devices=1)
    arrays, args = {}, []
    for name, a in feeds.items():
        arrays[f"in_{name}"] = np.ascontiguousarray(a)
        args.append(nc.dram_tensor(f"in_{name}", a.shape, mybir.dt.from_np(a.dtype), kind="ExternalInput").ap())
    args.append(nc.dram_tensor("out_0", (B, N, D), F32, kind="ExternalOutput").ap())
    decoder_kernel(nc, *args)
    result = run_bass_kernel_spmd(nc, [arrays], core_ids=[0])
    return result.results[0]["out_0"]
```

```python
from contextlib import ExitStack

import numpy as np
import concourse.bass as bass
from concourse import mybir

F32 = mybir.dt.float32
BF16 = mybir.dt.bfloat16
I32 = mybir.dt.int32
ALU = mybir.AluOpType
ACT = mybir.ActivationFunctionType
AX = mybir.AxisListType

P = 128
B = 8
N = 256
D = 256
TT = N // P
KT = D // P
H = 16
DH = 64
HP = H // 2
IN0 = H * DH
D1 = D // H
VW = 32
E = 8
F = 704
FT = -(-F // P)
FR = F - (FT - 1) * P
TE = N // E
BIG = 3.0e38
MASKED = -1.0e9
MAGIC = 12582912.0
EPS = 1e-5
ITERS = B // 2
HALVES = (0, 1)

RINGS = {"S": (0, 1, 2), "T": (3, 4), "O": (5,), "G": (6, 7)}
MOE_RINGS = {"G": (0,), "U": (1, 2, 3, 4), "Y0": (5,), "Y1": (6,)}

UNITS = 2 * HP
LAG = 4
O_LAG = LAG + 2
P_SLOTS = LAG + 1
SLOTS = 8
N_ROPE = TT * 4
GAP = O_LAG

EARLY = 10
WORK = []
for _stage, _h, _first, _last, _gap in (
        ("att0", 0, 0, UNITS, 0), ("att0", 1, 0, EARLY, 0), ("attx", 0, 0, UNITS, 0), ("att0", 1, EARLY, UNITS, GAP),
        ("attx", 1, 0, UNITS, GAP), ("atty", 0, 0, UNITS, GAP), ("atty", 1, 0, UNITS, 0)):
    WORK += [(_stage, _h, _u) for _u in range(_first, _last)] + [None] * _gap
N_STEPS = len(WORK) + O_LAG
QKVX = [("qk", hp) for hp in range(HP)] + [("v", k) for k in range(4)]
QKV0 = ([("v", k) for k in range(4)] + [("qk", k) for k in range(N_ROPE)],
        [("qk", k) for k in range(N_ROPE)] + [("v", k) for k in range(4)])
QKVX_PARTS = 6


def unit_at(step):
    return WORK[step] if 0 <= step < len(WORK) else None


def n_normalised(step):
    return sum(1 for unit in WORK[:step + 1] if unit and unit[0] != "atty")


def pair_at(step):
    unit = unit_at(step - O_LAG)
    return (unit[0], unit[1], unit[2] // 2) if unit and unit[2] % 2 == 0 else None




def stage_groups():
    return {
        "load": [("xT", "G"), ("cT", "G")],
        **{f"qkv0.{h}": [(name, "G") for name in QKV0[h]] + [(("qkT", hp), "T") for hp in range(HP)] for h in HALVES},
        "out0": [("out", "G")],
        "tx": [("xT", "G")],
        **{f"qkvx.{p}": [(name, "G") for name in QKVX[2 * p:2 * p + 2]] for p in range(QKVX_PARTS)},
        "outx": [("out", "G")],
        "tq": [("xT", "G")],
        "quant": [("xh", "G")],
        "tf": [("qT", "T")],
        "ffn": [("out", "G")],
        "t1": [("xT", "G")],
        "qkv1": [(("qk", 0), "G"), (("qk", 1), "G"), ("v", "G")],
        "tl": [("qT", "T"), ("kT", "T")],
        "lin": [("KV", "G")] + [(("A", c, r), "S") for c in range(TT) for r in range(4)],
        "lout": [(("oT", i), "G") for i in range(2)],
        "to": [(("o", tt), "T") for tt in range(TT)],
        "tp": [("oTT", "T")],
        "out1": [("out", "G")],
        "ty": [("xT", "G")],
        "qkvy": [("q", "G"), ("k", "G"), ("v", "G")],
        "outy": [(("o", tt), "T") for tt in range(TT)],
        "ny": [],
    }


def attention_fills(step):
    fills = []
    if unit_at(step):
        stage, h, u = unit_at(step)
        fills.append((h, stage, ("S", u), "S"))
    if unit_at(step - LAG):
        stage, h, u = unit_at(step - LAG)
        fills.append((h, stage, ("PT", u), "T"))
    if pair_at(step):
        stage, h, hp = pair_at(step)
        if stage != "atty" or hp % 2 == 0:
            fills.append((h, stage, ("O", hp), "O"))
    return fills


def plan(order, groups, rings):
    turn = {ring: 0 for ring in rings}
    fills = [0] * 8
    place = {}
    for who, item in order:
        stage = item.split(".")[0]
        made = attention_fills(who) if item == "att" else [(who, stage, name, ring) for name, ring in groups[item]]
        for half, stage, name, ring in made:
            ring = f"{ring}{half}" if ring == "Y" else ring
            b = rings[ring][turn[ring] % len(rings[ring])]
            turn[ring] += 1
            place[(half, stage, name)] = (b, fills[b])
            fills[b] += 1
    return place, fills


def iteration_order():
    a, b = HALVES
    x_a, x_b, y_a, y_b = (WORK.index((stage, h, 0)) for stage, h in (("attx", a), ("attx", b), ("atty", a), ("atty", b)))
    order = []

    def steps(n):
        done = sum(stage == "att" for _, stage in order)
        order.extend((step, "att") for step in range(done, done + n))

    def steps_until(n):
        steps(n - sum(stage == "att" for _, stage in order))

    def do(h, *stages):
        order.extend((h, stage) for stage in stages)

    do(a, "load")
    do(b, "load")
    do(a, "qkv0.0")
    do(b, "qkv0.1")
    steps(UNITS + O_LAG)
    do(a, "out0")
    steps(3)
    do(a, "tx")
    steps_until(x_a)
    do(a, *[f"qkvx.{p}" for p in range(QKVX_PARTS)])
    steps(UNITS + O_LAG)
    do(a, "outx")
    steps(3)
    do(a, "tq")
    steps(1)
    do(a, "quant")
    steps_until(x_b)
    do(b, "out0")
    do(a, "tf", "ffn")
    do(b, "tx", "qkvx.0", "qkvx.1")
    do(a, "t1")
    do(b, "qkvx.2")
    do(a, "qkv1")
    do(b, "qkvx.3", "qkvx.4")
    do(a, "tl")
    do(b, "qkvx.5")
    steps(UNITS)
    do(a, "lin")
    steps(2)
    do(a, "lout")
    steps(2)
    do(a, "to")
    steps(1)
    do(a, "tp")
    steps_until(y_a)
    do(a, "out1")
    do(b, "outx")
    do(a, "ty")
    do(a, "qkvy")
    do(b, "tq", "quant")
    for stage, n in (("tf", 1), ("ffn", 4), ("t1", 1), ("qkv1", 5), ("tl", 1), ("lin", 1), ("lout", 1)):
        if stage == "tf":
            steps(2)
        do(b, stage)
        steps(n)
    do(b, "to")
    steps(2)
    do(b, "tp")
    steps(1)
    do(b, "out1")
    steps_until(y_b)
    do(b, "ty")
    do(a, "outy")
    do(b, "qkvy")
    steps(4)
    do(a, "ny")
    steps_until(N_STEPS + 1)
    do(b, "outy", "ny")
    return order


ORDER = iteration_order()
LN = {"out0": 0, "outx": 1, "ffn": 2, "out1": 3, "outy": 4}
NORM = {"tx": "out0", "tq": "outx", "t1": "ffn", "ty": "out1", "ny": "outy"}
N_LN = len(LN)
STATS_RANK = {item: k for k, item in enumerate([item for item in ORDER if item[1] in LN])}
NORM_RANK = {(h, NORM[stage]): k for k, (h, stage) in enumerate([item for item in ORDER if item[1] in NORM])}
PLACE, FILLS = plan(ORDER, stage_groups(), RINGS)
MOE_PLACE, MOE_FILLS = plan([(h, "moe") for h in HALVES],
                            {"moe": [("xT", "G")] + [(("gu", j), "U") for j in range(FT)] + [("out", "Y")]}, MOE_RINGS)
QTR = P // TE
N_SETUP_DVE = 16
SETUP_IN, OUT0_IN, ATTX_IN, REST_IN = 16 * 5, 16 * 2, 16 * 6, 16 * 14
DVE_LINKS = 38
POOL_LINKS = 18


def decoder_kernel(nc, x_d, ctx_d, padm_d, subm_d, wqkv0_d, wout0_d, wq_d, bq_d, wk_d, bk_d, wv_d, bv_d,
                   wo_d, bo_d, ffn_d, wqkv1_d, wout1_d, wqy_d, bqy_d, wky_d, bky_d, wvy_d, bvy_d,
                   w1_d, w3_d, w2_d, ident_d, rope0_d, rope1_d, mask0_d, tri_d, par_d, rows8_d, bdm_d, had_d, out_d):
    ctx = ExitStack()
    with ctx:
        def sb(name, shape, dt=F32):
            return ctx.enter_context(nc.sbuf_tensor(name, shape, dt))

        def sem(name):
            return ctx.enter_context(nc.semaphore(name))

        w_area = sb("w_area", [P, 16384])
        wqkv0 = w_area[:, 0:6144].rearrange("p (k n) -> p k n", k=KT)
        wout0 = w_area[:, 6144:8192].rearrange("p (k n) -> p k n", k=HP)
        wq = w_area[:, 8192:10240].rearrange("p (k n) -> p k n", k=KT)
        wk = w_area[:, 10240:12288].rearrange("p (k n) -> p k n", k=KT)
        wv = w_area[:, 12288:14336].rearrange("p (k n) -> p k n", k=KT)
        wo = w_area[:, 14336:16384].rearrange("p (k n) -> p k n", k=HP)
        EW = 2 * KT * F + FT * D
        w1 = [w_area[:, i * EW:i * EW + KT * F].rearrange("p (k n) -> p k n", k=KT) for i in range(2)]
        w3 = [w_area[:, i * EW + KT * F:i * EW + 2 * KT * F].rearrange("p (k n) -> p k n", k=KT) for i in range(2)]
        w2 = [w_area[:, i * EW + 2 * KT * F:(i + 1) * EW].rearrange("p (k n) -> p k n", k=FT) for i in range(2)]
        wqkv1 = sb("wqkv1", [P, KT, 3 * D])
        wout1 = sb("wout1", [P, KT, D])
        wqy = sb("wqy", [P, KT, D])
        wky = sb("wky", [P, KT, D])
        wvy = sb("wvy", [P, KT, D])
        had = sb("had", [P, D])
        ternT = sb("ternT", [P, KT, D], BF16)
        ident = sb("ident_s", [P, P])
        identb = sb("identb", [P, P], BF16)
        rope0 = sb("rope0", [P, TT, 2, 2, DH])
        rope1 = sb("rope1", [P, TT, 2, D1])
        mask0 = sb("mask0", [P, 3, P])
        tri = sb("tri", [P, P])
        par = sb("par", [P, 2])
        head_rows = sb("head_rows", [P, 8])
        bdm = sb("bdm", [P, 8, VW])
        bq = sb("bq", [P, HP])
        bk = sb("bk", [P, HP])
        bv = sb("bv", [P, HP])
        bqy = sb("bqy", [P, KT])
        bky = sb("bky", [P, KT])
        bo_row = sb("bo_row", [P, D])
        bvy_row = sb("bvy_row", [P, D])
        bq_s = sb("bq_s", [P, HP])
        bqy_s = sb("bqy_s", [P, KT])
        wscale_row = sb("wscale_row", [P, D])
        sub_kept = sb("sub_kept", [P, TT, N], BF16)
        half_neg = sb("half_neg", [P, TT])
        x = [sb(f"x{h}", [P, TT, D]) for h in HALVES]
        xb = [sb(f"xb{h}", [P, TT, D]) for h in HALVES]
        r = [sb(f"r{h}", [P, TT, D]) for h in HALVES]
        cx = [sb(f"cx{h}", [P, TT, D]) for h in HALVES]
        xT = [sb(f"xT{h}", [P, KT, N]) for h in HALVES]
        cT = [sb(f"cT{h}", [P, KT, N]) for h in HALVES]
        qk_area = [sb(f"qk_area{h}", [P, HP * 2 * N]) for h in HALVES]
        v_area = [sb(f"v_area{h}", [P, TT * IN0]) for h in HALVES]
        o_area = sb("o_area", [P, 2 * HP * N])
        Vy = [sb(f"Vy{h}", [P, TT, H, VW]) for h in HALVES]
        p_ring = sb("p_ring", [P, P_SLOTS, 2, N])
        pt_area = sb("pt_area", [P, 2 * 4 * N])
        qkT = [a[:, :].rearrange("p (m s n) -> p m s n", m=HP, s=2) for a in qk_area]
        V = [a[:, :].rearrange("p (t n) -> p t n", t=TT) for a in v_area]
        OT = [o_area[:, h * HP * N:(h + 1) * HP * N].rearrange("p (m n) -> p m n", m=HP) for h in HALVES]
        roped = o_area[:, :].rearrange("p (t n) -> p t n", t=TT)
        PT = pt_area[:, :].rearrange("p (i a n) -> p i a n", i=2, a=4)
        pt_cols = pt_area[:, :].rearrange("p (i s n) -> p i s n", i=2, s=2)
        rope_t = pt_area[:, :].rearrange("p (i a n) -> p i a n", i=2, a=2)
        rope_t1 = [o_area[:, h * HP * N:(h + 1) * HP * N].rearrange("p (i a n) -> p i a n", i=2, a=2) for h in HALVES]
        qm = [a[:, 0:1024].rearrange("p (k s n) -> p k s n", k=KT, s=2) for a in qk_area]
        kT = [a[:, 1024:1536].rearrange("p (k n) -> p k n", k=KT) for a in qk_area]
        KVm = [a[:, 1536:2048].rearrange("p (k n) -> p k n", k=KT) for a in qk_area]
        AT = [[OT_area[:, :].rearrange("p (r a n) -> p r a n", r=4, a=4) for OT_area in
               (o_area[:, h * HP * N:(h + 1) * HP * N], qk_area[h][:, 2048:4096])] for h in HALVES]
        qkf = [a[:, 0:1024].rearrange("p (t n) -> p t n", t=TT) for a in v_area]
        elu_m = [a[:, 1024:2048].rearrange("p (t n) -> p t n", t=TT) for a in v_area]
        oTr = [a[:, 1024:2048].rearrange("p (m n) -> p m n", m=4) for a in v_area]
        oTT = [a[:, 512:1024].rearrange("p (k n) -> p k n", k=KT) for a in v_area]
        o_tok = [a[:, 0:512].rearrange("p (t n) -> p t n", t=TT) for a in v_area]
        y_tok = [a[:, 1536:2048].rearrange("p (t n) -> p t n", t=TT) for a in qk_area]
        km = [a[:, :].rearrange("p (m n) -> p m n", m=H) for a in qk_area]
        ky = [a[:, 1536:2048].rearrange("p (k n) -> p k n", k=KT) for a in v_area]
        cap = [a[:, 512:1024].rearrange("p (t n) -> p t n", t=TT) for a in v_area]
        pad_i = [sb(f"pad_i{h}", [P, N], I32) for h in HALVES]
        qn = [a[:, 0:256].bitcast(BF16).rearrange("p (t n) -> p t n", t=TT) for a in v_area]
        qnT = [a[:, 256:512].bitcast(BF16).rearrange("p (k n) -> p k n", k=KT) for a in v_area]
        negmax = sb("negmax", [P, SLOTS, 2])
        rowsum = sb("rowsum", [P, SLOTS, 2])
        rowinv = sb("rowinv", [P, SLOTS, 2])
        stats = sb("stats", [P, TT, 6])
        mv = sb("mv", [P, 2, TT, 2])
        var_e = sb("var_e", [P, 2, TT])
        rstd = sb("rstd", [P, 2, TT])
        amax = sb("amax", [P, TT])
        aq = sb("aq", [P, 2, TT])
        rden = sb("rden", [P, 2, H])
        wst = sb("wst", [P, KT, 4])
        ones = v_area[0][:, 0:P]
        diag = v_area[0][:, P:P + D].rearrange("p (k n) -> p k n", k=KT)

        bank = [ctx.enter_context(nc.psum_tensor(f"bank{i}", [P, 512], F32)) for i in range(8)]
        scratch = nc.dram_tensor("x_by_expert", (E, B, TE, D), F32, kind="Internal").ap()

        xq = [a[:, 0:512].rearrange("p (k n) -> p k n", k=KT) for a in v_area]

        full = [sem(f"full{b}") for b in range(8)]
        drained = [sem(f"drained{b}") for b in range(8)]
        setup_in = sem("setup_in")
        w0_in = [sem(f"w0_in{n}") for n in range(6)]
        rope_in = sem("rope_in")
        out0_in = sem("out0_in")
        attx_in = sem("attx_in")
        rest_in = sem("rest_in")
        x_in = [sem(f"x_in{h}") for h in HALVES]
        pad_in = [sem(f"pad_in{h}") for h in HALVES]
        stored = [sem(f"stored{h}") for h in HALVES]     
        setup_pool = sem("setup_pool")
        setup_dve = sem("setup_dve")
        setup_pe = sem("setup_pe")
        rope_done = sem("rope_done")
        s_max = sem("s_max")
        p_exp = sem("p_exp")
        inv_ready = sem("inv_ready")
        p_norm = sem("p_norm")
        p_norm0 = sem("p_norm0")
        ln_stats = sem("ln_stats")
        ln_rstd = sem("ln_rstd")
        x_ready = sem("x_ready")
        xb_ready = sem("xb_ready")
        lin_rot = sem("lin_rot")
        lin_relu = sem("lin_relu")
        lin_exp = sem("lin_exp")
        lin_feat = sem("lin_feat")
        qn_ready = sem("qn_ready")
        o_ready = sem("o_ready")
        km_ready = sem("km_ready")
        cap_ready = sem("cap_ready")
        waits_passed = sem("waits_passed")
        dve_seq = sem("dve_seq")
        pool_seq = sem("pool_seq")
        w_in = [sem(f"w_in{i}") for i in HALVES]
        tok_in = [sem(f"tok_in{i}") for i in HALVES]
        silu_done = sem("silu_done")
        moe_stats = sem("moe_stats")
        moe_rstd = sem("moe_rstd")
        y_ready = sem("y_ready")
        y_stored = [sem(f"y_stored{i}") for i in HALVES]
        y_free = [sem(f"y_free{i}") for i in HALVES]

        def nth(it, n, h, k, stage=0, stages=1):
            return it * (2 * n * stages) + ((2 * stage + h) * n + k)

        def probs(it, w):
            return it * n_normalised(len(WORK)) + n_normalised(w)

        def normed(it, h, stage):
            return it * (2 * N_LN) + (NORM_RANK[(h, stage)] + 1)

        def summed(it, h, stage):
            return it * (2 * N_LN) + (STATS_RANK[(h, stage)] + 1)

        def filled(eng, it, h, stage, name):
            b, k = PLACE[(h, stage, name)]
            eng.wait_ge(full[b], it * FILLS[b] + (k + 1))
            return bank[b], drained[b]

        def emptied(eng, it, h, stage, name):
            b, k = PLACE[(h, stage, name)]
            eng.wait_ge(drained[b], it * FILLS[b] + (k + 2))

        def emptied_all(eng, it, h, stage, names):
            last = {PLACE[(h, stage, name)][0]: name for name in names}
            for name in last.values():
                emptied(eng, it, h, stage, name)

        def claim(eng, it, h, stage, name, operands=()):
            b, k = PLACE[(h, stage, name)]
            count = {b: k + 1}
            for source in operands:
                source_b, source_k = PLACE[(h, *source)]
                count[source_b] = max(count.get(source_b, 0), source_k + 2)
            for waited, c in count.items():
                eng.wait_ge(drained[waited], it * FILLS[waited] + c)
            return bank[b], full[b]

        def moe_at(it, i, name):
            b, k = MOE_PLACE[(i, "moe", name)]
            return b, it * MOE_FILLS[b] + (ITERS * FILLS[b] + k)

        def rows(dram):
            return dram.rearrange("(k p) n -> p k n", p=P)

        layers = ExitStack()
        block = layers.enter_context(nc.Block())

        def expert_weights(sp, i, e):
            main = (FT - 1) * P
            for dst, src in (
                    (w1[i], w1_d[bass.ds(e, 1)].rearrange("o (k p) n -> p (o k) n", p=P)),
                    (w3[i], w3_d[bass.ds(e, 1)].rearrange("o (k p) n -> p (o k) n", p=P)),
                    (w2[i][:, 0:FT - 1, :], w2_d[bass.ds(e, 1), 0:main].rearrange("o (k p) n -> p (o k) n", p=P)),
                    (w2[i][0:FR, FT - 1, :], w2_d[bass.ds(e, 1), main:F].rearrange("o p n -> p (o n)"))):
                sp.dma_start(dst, src).then_inc(w_in[i], 16)

        def passed(eng):
            eng.sem_inc(waits_passed, 1)

        @block.sync
        def _(sp):
            def load(sem_in, *pairs):
                for dst, src in pairs:
                    sp.dma_start(dst, src).then_inc(sem_in, 16)
                return 16 * len(pairs)

            def sequences(it):
                for h in HALVES:
                    g = it * 2 + h
                    load(x_in[h], (x[h][:, :, :], x_d[bass.ds(g, 1)].rearrange("o (t p) n -> p (o t) n", p=P)),
                         (cx[h][:, :, :], ctx_d[bass.ds(g, 1)].rearrange("o (t p) n -> p (o t) n", p=P)))
                    load(pad_in[h], (pad_i[h][:, :], padm_d[bass.ds(g, 1)].rearrange("o n -> (o n)").partition_broadcast(P)))

            def results(it):
                for h in HALVES:
                    sp.wait_ge(x_ready, normed(it, h, "outy"))
                    for q in range(QTR):
                        to = scratch.rearrange("(t q) b s n -> q b s t n", q=QTR)[q, bass.ds(it * 2 + h, 1)]
                        load(stored[h], (to.rearrange("o s t n -> (o s) t n"), xb[h][TE * q:TE * q + TE, :, :]))

            assert SETUP_IN == load(setup_in, (xb[0][:, :, :], rows(ffn_d)), (r[0][:, :, :].bitcast(I32), rows(subm_d)),
                                    (ident[:, :], ident_d), (bq[:, :], bq_d), (bqy[:, :], bqy_d))
            sequences(0)
            w0 = rows(wqkv0_d)
            for n in (4, 5, 0, 1, 2, 3):
                load(w0_in[n], (wqkv0[:, :, n * 512:(n + 1) * 512], w0[:, :, n * 512:(n + 1) * 512]))
                if n == 5:
                    load(rope_in, (rope0[:, :, :, :, :].rearrange("p t a c d -> p t (a c d)"), rope0_d.rearrange("(t p) n -> p t n", p=P)))
            assert OUT0_IN == load(out0_in, (mask0[:, :, :], mask0_d), (wout0, rows(wout0_d)))
            assert ATTX_IN == load(attx_in, (bk[:, :], bk_d), (bv[:, :], bv_d), (bo_row[:, :], bo_d.partition_broadcast(P)),
                                   (wq, rows(wq_d)), (wk, rows(wk_d)), (wv, rows(wv_d)))
            assert REST_IN == load(
                rest_in, (wo, rows(wo_d)), (had[:, :], had_d), (wqkv1[:, :, :], rows(wqkv1_d)),
                (rope1[:, :, :, :].rearrange("p t c d -> p t (c d)"), rope1_d.rearrange("(t p) n -> p t n", p=P)),
                (tri[:, :], tri_d), (par[:, :], par_d), (head_rows[:, :], rows8_d), (bdm[:, :, :], bdm_d),
                (wout1[:, :, :], rows(wout1_d)), (wqy[:, :, :], rows(wqy_d)), (wky[:, :, :], rows(wky_d)),
                (wvy[:, :, :], rows(wvy_d)), (bky[:, :], bky_d), (bvy_row[:, :], bvy_d.partition_broadcast(P)))
            with sp.Fori(0, ITERS - 1) as it:
                sp.wait_ge(xb_ready, nth(it, 1, 1, 1, 1, 2) + 4)
                sequences(it + 1)
                results(it)
            b, k = PLACE[(1, "qkvx", ("v", 3))]
            sp.wait_ge(drained[b], (ITERS - 1) * FILLS[b] + k + 2)
            for i in HALVES:
                expert_weights(sp, i, i)
            results(ITERS - 1)

        @block.gpsimd
        def _(pool):
            for b in range(8):
                pool.sem_inc(drained[b], 1)
            pool.sem_inc(rope_done, 2)
            pool.sem_inc(xb_ready, 4)
            for h in HALVES:
                pool.sem_inc(y_free[h], 1)
            nc.gpsimd.memset(half_neg[:, :], -0.5).then_inc(setup_pool, 1)
            nc.gpsimd.memset(ones[:, :], 1.0).then_inc(setup_pool, 1)
            for h in HALVES:
                nc.gpsimd.memset(Vy[h][:, :, :, :], 0.0).then_inc(setup_pool, 1)
            pool.wait_ge(setup_pool, 4)
            for h in HALVES:
                nc.gpsimd.memset(Vy[h][:, :, :, D1:D1 + 1], 1.0).then_inc(setup_pool, 1)
            pool.wait_ge(setup_in, SETUP_IN)
            nc.gpsimd.tensor_scalar(sub_kept[:, :, :], r[0][:, :, :].bitcast(I32), 0.0, None, ALU.is_equal).then_inc(setup_pool, 1)
            pool.wait_ge(setup_pool, 7)
            nc.gpsimd.tensor_scalar(sub_kept[:, :, :], sub_kept[:, :, :], -1.0, 1.0, ALU.mult, ALU.add).then_inc(setup_pool, 1)
            pool.wait_ge(setup_pool, 8)
            with pool.Fori(0, ITERS) as it:
                steps = 0

                def link(ins):
                    nonlocal steps
                    steps += 1
                    ins.then_inc(pool_seq, 1)
                    pool.wait_ge(pool_seq, it * POOL_LINKS + steps)
                    passed(pool)

                for h, stage in ORDER:
                    if stage == f"qkv0.{h}":
                        for k in range(N_ROPE):
                            tt, n = divmod(k, 4)
                            emptied(pool, it, h, "qkv0", ("qk", k))
                            nc.gpsimd.tensor_tensor(roped[:, tt, n * 512:(n + 1) * 512], rope_t[:, k % 2, 0, :],
                                                    rope_t[:, k % 2, 1, :], ALU.add).then_inc(rope_done, 1)
                    if stage == "ty":
                        pool.wait_ge(rest_in, REST_IN)
                    if stage == "tx":
                        pool.wait_ge(attx_in, ATTX_IN)
                        pool.wait_ge(x_ready, normed(it, h, "out0"))
                        nc.gpsimd.tensor_tensor(xb[h][:, :, :], x[h][:, :, :], bo_row[:, None, :].broadcast_to([P, TT, D]),
                                                ALU.add).then_inc(xb_ready, 1)
                    if stage == "att" and unit_at(h - 1) and unit_at(h - 1)[0] != "atty":
                        w = h - 1
                        att, h, u = WORK[w]
                        keys = P if att == "att0" else N
                        pool.wait_ge(inv_ready, probs(it, w))
                        passed(pool)
                        nc.gpsimd.tensor_scalar(p_ring[:, w % P_SLOTS, 0, 0:keys], p_ring[:, w % P_SLOTS, 0, 0:keys],
                                                rowinv[:, w % SLOTS, 0:1], None, ALU.mult).then_inc(p_norm0, 1)
                    if stage == "ty":
                        pool.wait_ge(x_ready, normed(it, h, "out1"))
                        pool.wait_ge(pad_in[h], it * 16 + 16)
                        passed(pool)
                        pad_k = cap[h][:, 0, :]
                        link(nc.gpsimd.tensor_scalar(pad_k, pad_i[h][:, :], 0.0, None, ALU.is_equal))
                        link(nc.gpsimd.tensor_scalar(pad_k, pad_k, -1.0, 1.0, ALU.mult, ALU.add))
                        link(nc.gpsimd.tensor_tensor(cap[h][:, 1, :], pad_k, sub_kept[:, 1, :], ALU.mult))
                        link(nc.gpsimd.tensor_tensor(cap[h][:, 0, :], pad_k, sub_kept[:, 0, :], ALU.mult))
                        nc.gpsimd.tensor_scalar(cap[h][:, :, :], cap[h][:, :, :], BIG, MASKED, ALU.mult, ALU.add).then_inc(cap_ready, 1)
                        emptied(pool, it, h, "ty", "xT")
                        nc.gpsimd.tensor_tensor(xb[h][:, :, :], x[h][:, :, :], bvy_row[:, None, :].broadcast_to([P, TT, D]),
                                                ALU.add).then_inc(xb_ready, 1)
                    if stage == "qkvy":
                        emptied(pool, it, h, stage, "k")
                        passed(pool)
                        for m in range(H):
                            nc.gpsimd.tensor_scalar(km[h][:, m, :], ky[h][:, m // 8, :], head_rows[:, m % 8:m % 8 + 1], None,
                                                    ALU.mult).then_inc(km_ready, 1)
                    if stage in LN:
                        pool.wait_ge(ln_stats, summed(it, h, stage))
                        passed(pool)
                        link(nc.gpsimd.tensor_scalar(var_e[:, h, :], mv[:, h, :, 1], EPS, None, ALU.add))
                        nc.gpsimd.tensor_tensor(rstd[:, h, :], var_e[:, h, :], half_neg[:, :], ALU.pow).then_inc(ln_rstd, 1)
                for h in HALVES:
                    pool.wait_ge(stored[h], it * (16 * QTR) + 16 * QTR)
                assert steps == POOL_LINKS, f"POOL_LINKS {steps}"

        @block.scalar
        def _(act):
            act.wait_ge(setup_dve, N_SETUP_DVE)
            with act.Fori(0, ITERS) as it:

                def copy_out(h, stage, name, dst, shape=None, cols=512, **view):
                    b, done = filled(act, it, h, stage, name)
                    src = b[:, 0:cols]
                    if shape:
                        src = src.rearrange(shape, **view)
                    nc.scalar.activation(dst, src, ACT.Copy).then_inc(done, 1)

                for h, stage in ORDER:
                    if stage == "tx":
                        act.wait_ge(attx_in, ATTX_IN)
                    if stage in ("load", "tx", "tq", "t1", "ty"):
                        copy_out(h, stage, "xT", xT[h][:, :, :], "p (k n) -> p k n", k=KT)
                    if stage == "load":
                        copy_out(h, stage, "cT", cT[h][:, :, :], "p (k n) -> p k n", k=KT)
                    if stage == f"qkv0.{h}":
                        for k in range(4):
                            tt, n = divmod(k, 2)
                            copy_out(h, "qkv0", ("v", k), V[h][:, tt, n * 512:(n + 1) * 512])
                        for hp in range(HP):
                            copy_out(h, "qkv0", ("qkT", hp), qkT[h][:, hp, :, :], "p (s n) -> p s n", s=2)
                    if stage.startswith("qkvx"):
                        kind, k = QKVX[2 * int(stage[-1])]
                        if kind == "qk":
                            b, done = filled(act, it, h, "qkvx", ("qk", k))
                            nc.scalar.activation(qkT[h][:, k, 0, :], b[:, 0:N], ACT.Identity, bias=bq_s[:, k:k + 1], scale=DH ** -0.5)
                            nc.scalar.activation(qkT[h][:, k, 1, :], b[:, N:2 * N], ACT.Identity, bias=bk[:, k:k + 1]).then_inc(done, 1)
                        else:
                            tt, n = divmod(k, 2)
                            copy_out(h, "qkvx", ("v", k), V[h][:, tt, n * 512:(n + 1) * 512])
                    if stage == "att":
                        step = h
                        if unit_at(step - LAG):
                            att, h, u = unit_at(step - LAG)
                            qb = u % 2
                            b, done = filled(act, it, h, att, ("PT", u))
                            if att == "atty":
                                dst = PT[:, (step - LAG) // 2 % 2, :, qb * P:(qb + 1) * P]
                                src = b[:, :].rearrange("p (a n) -> p a n", a=4)
                            else:
                                cols = 3 * P if att == "att0" else 4 * P
                                dst, src = pt_cols[:, (step - LAG) // 2 % 2, qb, 0:cols], b[:, 0:cols]
                            nc.scalar.activation(dst, src, ACT.Copy).then_inc(done, 1)
                        if unit_at(step):
                            att, h, u = unit_at(step)
                            p = p_ring[:, step % P_SLOTS, :, :]
                            if att == "att0":
                                emptied(act, it, h, att, ("S", u))
                            else:
                                act.wait_ge(s_max, nth(it, UNITS, h, u + 1, att == "atty", 2))
                            for s in range(2):
                                bias = negmax[:, step % SLOTS, s:s + 1]
                                total = rowsum[:, step % SLOTS, s:s + 1]
                                if att == "att0":
                                    keys = P * (s + 1)
                                    e = nc.scalar.activation(p[:, s, 0:keys], p[:, s, 0:keys], ACT.Exp, bias=bias, scale=-1.0, accum_out=total)
                                elif att == "attx":
                                    b = bank[PLACE[(h, att, ("S", u))][0]]
                                    e = nc.scalar.activation(p[:, s, :], b[:, s * N:(s + 1) * N], ACT.Exp, bias=bias, accum_out=total)
                                else:
                                    e = nc.scalar.activation(p[:, s, :], p[:, s, :], ACT.Exp, bias=bias)
                            if att == "attx":
                                e.then_inc(drained[PLACE[(h, att, ("S", u))][0]], 1)
                            else:
                                e.then_inc(p_exp, 1)
                    if stage == "tf":
                        b, done = filled(act, it, h, stage, "qT")
                        nc.scalar.activation(qnT[h][:, :, :], b[:, 0:256].bitcast(BF16).rearrange("p (k n) -> p k n", k=KT), ACT.Copy).then_inc(done, 1)
                    if stage == "qkv1":
                        for tt in range(TT):
                            act.wait_ge(lin_rot, nth(it, TT, h, tt + 1))
                            nc.scalar.activation(elu_m[h][:, tt, :], qkf[h][:, tt, :], ACT.Relu, scale=-1.0).then_inc(lin_relu, 1)
                            act.wait_ge(lin_relu, nth(it, TT, h, tt + 1))
                            nc.scalar.activation(elu_m[h][:, tt, :], elu_m[h][:, tt, :], ACT.Exp, scale=-1.0).then_inc(lin_exp, 1)
                    if stage in ("qkv1", "qkvy"):
                        if stage == "qkvy":
                            b, done = filled(act, it, h, stage, "q")
                            for kt in range(KT):
                                q = nc.scalar.activation(xq[h][:, kt, :], b[:, kt * N:(kt + 1) * N], ACT.Identity,
                                                         bias=bqy_s[:, kt:kt + 1], scale=D1 ** -0.5)
                            q.then_inc(done, 1)
                        copy_out(h, stage, "v", Vy[h][:, :, :, 0:D1], "p (t a d) -> p t a d", t=TT, a=H)
                    if stage == "tl":
                        copy_out(h, stage, "kT", kT[h], "p (k n) -> p k n", k=KT)
                    if stage == "lout":
                        for i in range(2):
                            copy_out(h, stage, ("oT", i), oTr[h][:, 2 * i:2 * i + 2, :], "p (m n) -> p m n", m=2)
                    if stage == "tp":
                        copy_out(h, stage, "oTT", oTT[h][:, :, :], "p (k n) -> p k n", k=KT)

        @block.vector
        def _(dve):
            s = 0

            def setup(ins):
                nonlocal s
                s += 1
                ins.then_inc(setup_dve, 1)
                dve.wait_ge(setup_dve, s)

            dve.wait_ge(setup_in, SETUP_IN)
            dve.wait_ge(setup_pool, 8)
            w = xb[0]
            gt, lt = xb[1], r[1]
            setup(nc.vector.tensor_reduce(wst[:, :, 0], w[:, :, :], AX.X, ALU.add, apply_absolute_value=True))
            setup(nc.vector.tensor_scalar(wst[:, :, 1], wst[:, :, 0], 1.0 / D, 1e-5, ALU.mult, ALU.max))
            setup(nc.vector.tensor_scalar(wst[:, :, 2], wst[:, :, 1], 0.5, None, ALU.mult))
            setup(nc.vector.tensor_scalar(wst[:, :, 3], wst[:, :, 1], -0.5, None, ALU.mult))
            for kt in range(KT):
                setup(nc.vector.tensor_scalar(gt[:, kt, :], w[:, kt, :], wst[:, kt, 2:3], None, ALU.is_gt))
                setup(nc.vector.tensor_scalar(lt[:, kt, :], w[:, kt, :], wst[:, kt, 3:4], None, ALU.is_lt))
                setup(nc.vector.tensor_scalar(diag[:, kt, :], ident[:, :], wst[:, kt, 1:2], None, ALU.mult))
            setup(nc.vector.tensor_tensor(gt[:, :, :], gt[:, :, :], lt[:, :, :], ALU.subtract))
            setup(nc.vector.tensor_scalar(bq_s[:, :], bq[:, :], DH ** -0.5, None, ALU.mult))
            setup(nc.vector.tensor_scalar(bqy_s[:, :], bqy[:, :], D1 ** -0.5, None, ALU.mult))
            setup(nc.vector.tensor_copy(identb[:, :], ident[:, :]))
            assert s == N_SETUP_DVE - 2
            dve.wait_ge(setup_pe, 1)
            setup(nc.vector.tensor_copy(ternT[:, :, :], bank[0][:, :].rearrange("p (k n) -> p k n", k=KT)))
            setup(nc.vector.tensor_copy(wscale_row[:, :], bank[1][:, 0:D]))
            with dve.Fori(0, ITERS) as it:
                steps = 0

                def link(ins, alone=False):
                    nonlocal steps
                    steps += 1
                    ins.then_inc(dve_seq, 1)
                    dve.wait_ge(dve_seq, it * DVE_LINKS + steps)
                    if alone:
                        passed(dve)

                def statistics(h):
                    for tt in range(TT):
                        last = nc.vector.bn_stats(stats[:, tt, :], r[h][:, tt, :])
                    link(last, alone=True)
                    for tt in range(TT):
                        last = nc.vector.bn_aggr(mv[:, h, tt, :], stats[:, tt, :])
                    last.then_inc(ln_stats, 1)

                def normalise(h, stage, dst):
                    dve.wait_ge(ln_rstd, summed(it, h, stage))
                    for tt in range(TT):
                        last = nc.vector.tensor_scalar(dst[:, tt, :], r[h][:, tt, :], mv[:, h, tt, 0:1], rstd[:, h, tt:tt + 1],
                                                       ALU.subtract, ALU.mult)
                    last.then_inc(x_ready, 1)

                def two(b):
                    return b[:, :].rearrange("p (t n) -> p t n", t=2)

                def residual(h, stage, res):
                    b, done = filled(dve, it, h, stage, "out")
                    nc.vector.tensor_tensor(r[h][:, :, :], two(b), res[:, :, :], ALU.add).then_inc(done, 1)
                    emptied(dve, it, h, stage, "out")

                def rotary(h, stage, k, rope_t, width, cos, sin):
                    b, done = filled(dve, it, h, stage, ("qk", k))
                    heads = 512 // width
                    nc.vector.tensor_tensor(rope_t[:, 0, :].rearrange("p (h d) -> p h d", d=width),
                                            b[:, :].rearrange("p (h d) -> p h d", d=width),
                                            cos[:, None, :].broadcast_to([P, heads, width]), ALU.mult)
                    half = width // 2
                    for s in range(2):
                        last = nc.vector.tensor_tensor(
                            rope_t[:, 1, :].rearrange("p (h s d) -> p h s d", s=2, d=half)[:, :, s, :],
                            b[:, :].rearrange("p (h s d) -> p h s d", s=2, d=half)[:, :, 1 - s, :],
                            sin[:, None, s * half:(s + 1) * half].broadcast_to([P, heads, half]), ALU.mult)
                    last.then_inc(done, 1)

                def normalised(h, stage, dst, tt, guard):
                    b, done = filled(dve, it, h, stage, ("o", tt))
                    o = b[:, :].rearrange("p (h d) -> p h d", h=H)
                    link(nc.vector.tensor_scalar(rden[:, 0, :], o[:, :, D1], guard, None, ALU.max))
                    link(nc.vector.reciprocal(rden[:, 1, :], rden[:, 0, :]))
                    nc.vector.tensor_tensor(dst[:, tt, :].rearrange("p (h d) -> p h d", h=H), o[:, :, 0:D1],
                                            rden[:, 1, :, None].broadcast_to([P, H, D1]), ALU.mult).then_inc(done, 1)

                for h, stage in ORDER:
                    if stage in NORM:
                        normalise(h, NORM[stage], xb[h] if stage == "ny" else x[h])
                    if stage == "qkv0.0":
                        dve.wait_ge(rope_in, 16)
                    if stage == "tx":
                        dve.wait_ge(attx_in, ATTX_IN)
                    if stage == "outx":
                        dve.wait_ge(rest_in, REST_IN)
                    if stage == f"qkv0.{h}":
                        for k in range(N_ROPE):
                            tt, n = divmod(k, 4)
                            dve.wait_ge(rope_done, nth(it, N_ROPE, h, k + 1))
                            rotary(h, "qkv0", k, rope_t[:, k % 2, :, :], DH, rope0[:, tt, n // 2, 0, :], rope0[:, tt, n // 2, 1, :])
                    if stage.startswith("qkvx"):
                        kind, k = QKVX[2 * int(stage[-1]) + 1]
                        b, done = filled(dve, it, h, "qkvx", (kind, k))
                        if kind == "qk":
                            nc.vector.tensor_scalar(qkT[h][:, k, 0, :], b[:, 0:N], bq[:, k:k + 1], DH ** -0.5, ALU.add, ALU.mult)
                            nc.vector.tensor_scalar(qkT[h][:, k, 1, :], b[:, N:2 * N], bk[:, k:k + 1], None, ALU.add).then_inc(done, 1)
                        else:
                            tt, n = divmod(k, 2)
                            nc.vector.tensor_copy(V[h][:, tt, n * 512:(n + 1) * 512], b[:, :]).then_inc(done, 1)
                    if stage == "att":
                        step = h
                        if step == 0:
                            dve.wait_ge(out0_in, OUT0_IN)
                        if unit_at(step):
                            att, h, u = unit_at(step)
                            p, least = p_ring[:, step % P_SLOTS, :, :], negmax[:, step % SLOTS, :]
                            b, done = filled(dve, it, h, att, ("S", u))
                            if att == "att0":
                                passed(dve)
                                for s in range(2):
                                    keys = P * (s + 1)
                                    mask = mask0[:, s:2 * s + 1, :].rearrange("p a n -> p (a n)")
                                    last = nc.vector.tensor_tensor_reduce(p[:, s, 0:keys], b[:, s * N:s * N + keys], mask,
                                                                          1.0, BIG, ALU.add, ALU.min, least[:, s:s + 1])
                                last.then_inc(done, 1)
                            elif att == "attx":
                                nc.vector.tensor_reduce(least, two(b), AX.X, ALU.max, negate=True).then_inc(s_max, 1)
                            else:
                                nc.vector.tensor_tensor(p, two(b), cap[h][:, u % 2, None, :].broadcast_to([P, 2, N]), ALU.min).then_inc(done, 1)
                                emptied(dve, it, h, att, ("S", u))
                                nc.vector.tensor_reduce(least, p, AX.X, ALU.max, negate=True).then_inc(s_max, 1)
                        if pair_at(step - 1):
                            att, h, hp = pair_at(step - 1)
                            if att == "atty":
                                if hp % 2:
                                    b, done = filled(dve, it, h, att, ("O", hp - 1))
                                    nc.vector.tensor_copy(oTr[h][:, hp // 2, :], b[:, 0:N]).then_inc(done, 1)
                            else:
                                b, done = filled(dve, it, h, att, ("O", hp))
                                if att == "att0":
                                    nc.vector.tensor_copy(OT[h][:, hp, :], b[:, 0:N]).then_inc(done, 1)
                                else:
                                    nc.vector.tensor_scalar(OT[h][:, hp, :], b[:, 0:N], bv[:, hp:hp + 1], None, ALU.add).then_inc(done, 1)
                        if unit_at(step - 2) and unit_at(step - 2)[0] != "atty":
                            w = step - 2
                            att, h, u = WORK[w]
                            dve.wait_ge(inv_ready, probs(it, w))
                            nc.vector.tensor_scalar(p_ring[:, w % P_SLOTS, 1, :], p_ring[:, w % P_SLOTS, 1, :],
                                                    rowinv[:, w % SLOTS, 1:2], None, ALU.mult).then_inc(p_norm, 1)
                        if unit_at(step - 1) and unit_at(step - 1)[0] != "atty":
                            w = step - 1
                            att, h, u = WORK[w]
                            if att == "attx":
                                emptied(dve, it, h, att, ("S", u))
                            else:
                                dve.wait_ge(p_exp, nth(it, UNITS, h, u + 1, 0, 2))
                            nc.vector.reciprocal(rowinv[:, w % SLOTS, :], rowsum[:, w % SLOTS, :]).then_inc(inv_ready, 1)
                    if stage in ("out0", "outx", "out1"):
                        if stage == "out0":
                            dve.wait_ge(x_in[h], it * 32 + 32)
                        if stage == "outx":
                            dve.wait_ge(xb_ready, nth(it, 1, h, 1, 0, 2) + 4)
                        residual(h, stage, xb[h] if stage == "outx" else x[h])
                        statistics(h)
                    if stage == "quant":
                        b, done = filled(dve, it, h, stage, "xh")
                        link(nc.vector.tensor_reduce(amax[:, :], two(b), AX.X, ALU.max, apply_absolute_value=True))
                        link(nc.vector.tensor_scalar(aq[:, h, :], amax[:, :], 1e-5, 1.0 / 7.0, ALU.max, ALU.mult))
                        link(nc.vector.reciprocal(amax[:, :], aq[:, h, :]))
                        for tt in range(TT):
                            last = nc.vector.tensor_scalar(r[h][:, tt, :], b[:, tt * D:(tt + 1) * D], amax[:, tt:tt + 1], MAGIC, ALU.mult, ALU.add)
                        last.then_inc(done, 1)
                        emptied(dve, it, h, stage, "xh")
                        link(nc.vector.tensor_scalar(r[h][:, :, :], r[h][:, :, :], MAGIC, -8.0, ALU.subtract, ALU.max))
                        nc.vector.tensor_scalar(qn[h][:, :, :], r[h][:, :, :], 7.0, None, ALU.min).then_inc(qn_ready, 1)
                    if stage == "ffn":
                        b, done = filled(dve, it, h, stage, "out")
                        for tt in range(TT):
                            last = nc.vector.scalar_tensor_tensor(out=r[h][:, tt, :], in0=b[:, tt * D:(tt + 1) * D], scalar=aq[:, h, tt:tt + 1],
                                                                  in1=wscale_row[:, :], op0=ALU.mult, op1=ALU.mult)
                        last.then_inc(done, 1)
                        emptied(dve, it, h, stage, "out")
                        link(nc.vector.tensor_tensor(r[h][:, :, :], r[h][:, :, :], x[h][:, :, :], ALU.add))
                        statistics(h)
                    if stage == "qkv1":
                        for tt in range(TT):
                            rotary(h, stage, tt, rope_t1[h][:, tt, :, :], D1, rope1[:, tt, 0, :], rope1[:, tt, 1, :])
                            emptied(dve, it, h, stage, ("qk", tt))
                            nc.vector.tensor_tensor(qkf[h][:, tt, :], rope_t1[h][:, tt, 0, :], rope_t1[h][:, tt, 1, :], ALU.add).then_inc(lin_rot, 1)
                        for tt in range(TT):
                            dve.wait_ge(lin_exp, nth(it, TT, h, tt + 1))
                            nc.vector.scalar_tensor_tensor(out=qkf[h][:, tt, :], in0=qkf[h][:, tt, :], scalar=0.0, in1=elu_m[h][:, tt, :],
                                                           op0=ALU.max, op1=ALU.add).then_inc(lin_feat, 1)
                    if stage == "tl":
                        b, done = filled(dve, it, h, stage, "qT")
                        for s in range(2):
                            last = nc.vector.tensor_scalar(qm[h][:, :, s, :], two(b), par[:, s:s + 1], None, ALU.mult)
                        last.then_inc(done, 1)
                    if stage == "lin":
                        b, done = filled(dve, it, h, stage, "KV")
                        nc.vector.tensor_tensor(KVm[h][:, :, :], two(b),
                                                bdm[:, :, :].rearrange("p h v -> p (h v)")[:, None, :].broadcast_to([P, KT, 8 * VW]),
                                                ALU.mult).then_inc(done, 1)
                        for c in range(TT):
                            for q in range(4):
                                b, done = filled(dve, it, h, stage, ("A", c, q))
                                nc.vector.tensor_tensor(AT[h][c][:, q, :, :], b[:, :].rearrange("p (a n) -> p a n", a=4),
                                                        tri[:, None, :].broadcast_to([P, 4, P]), ALU.mult).then_inc(done, 1)
                    if stage == "to":
                        for tt in range(TT):
                            normalised(h, stage, o_tok[h], tt, 1e-6)
                        emptied(dve, it, h, stage, ("o", TT - 1))
                    if stage == "qkvy":
                        b, done = filled(dve, it, h, stage, "k")
                        for kt in range(KT):
                            last = nc.vector.tensor_scalar(ky[h][:, kt, :], b[:, kt * N:(kt + 1) * N], bky[:, kt:kt + 1], None, ALU.add)
                        last.then_inc(done, 1)
                        dve.wait_ge(cap_ready, nth(it, 1, h, 1))
                    if stage == "outy":
                        for tt in range(TT):
                            normalised(h, stage, y_tok[h], tt, 0.0)
                        emptied(dve, it, h, stage, ("o", TT - 1))
                        dve.wait_ge(xb_ready, nth(it, 1, h, 1, 1, 2) + 4)
                        link(nc.vector.tensor_tensor(r[h][:, :, :], y_tok[h][:, :, :], xb[h][:, :, :], ALU.add))
                        statistics(h)
                assert steps == DVE_LINKS, f"DVE_LINKS {steps}"

        @block.tensor
        def _(pe):
            mm, tr = nc.tensor.matmul, nc.tensor.transpose
            pe.wait_ge(setup_dve, N_SETUP_DVE - 2)
            for kt in range(KT):
                for ot in range(KT):
                    tr(bank[0][:, kt * D + ot * P:kt * D + (ot + 1) * P], xb[1][:, ot, kt * P:(kt + 1) * P], ident[:, :])
            for kt in range(KT):
                last = mm(bank[1][:, kt * P:(kt + 1) * P], ones[:, :], diag[:, kt, :], start=True, stop=True)
            last.then_inc(setup_pe, 1)
            pe.wait_ge(setup_dve, N_SETUP_DVE)
            with pe.Fori(0, ITERS) as it:

                def turn(h, stage, name, src, operands=()):
                    b, done = claim(pe, it, h, stage, name, operands)
                    for kt in range(KT):
                        for tt in range(TT):
                            last = tr(b[:, kt * N + tt * P:kt * N + (tt + 1) * P], src[:, tt, kt * P:(kt + 1) * P], ident[:, :])
                    last.then_inc(done, 1)

                def product(out, pairs):
                    for i, (lhsT, rhs) in enumerate(pairs):
                        last = mm(out, lhsT, rhs, start=(i == 0), stop=(i == len(pairs) - 1))
                    return last

                def token_tiles(h, stage, name, lhs, rhs, n, operands=()):
                    b, done = claim(pe, it, h, stage, name, operands)
                    for tt in range(TT):
                        last = product(b[:, tt * D:(tt + 1) * D], [(lhs(k, tt), rhs(k)) for k in range(n)])
                    last.then_inc(done, 1)

                def tok(t, tt):
                    return slice(tt * t, (tt + 1) * t)

                for h, stage in ORDER:
                    if stage == "out0":
                        pe.wait_ge(out0_in, OUT0_IN)
                    if stage == "tx":
                        pe.wait_ge(attx_in, ATTX_IN)
                    if stage == "outx":
                        pe.wait_ge(rest_in, REST_IN)
                    if stage == "load":
                        pe.wait_ge(x_in[h], it * 32 + 32)
                        turn(h, stage, "xT", x[h])
                        turn(h, stage, "cT", cx[h])
                    if stage in ("tx", "tq", "t1", "ty"):
                        pe.wait_ge(x_ready, normed(it, h, NORM[stage]))
                        turn(h, stage, "xT", x[h])
                    if stage == f"qkv0.{h}":
                        for kind, k in QKV0[h]:
                            tt, n = divmod(k, 2 if kind == "v" else 4)
                            col = n * 512 + (2 * IN0 if kind == "v" else 0)
                            pe.wait_ge(w0_in[col // 512], 16)
                            b, done = claim(pe, it, h, "qkv0", (kind, k), [("load", "xT")])
                            product(b[:, :], [(xT[h][:, kt, tok(P, tt)], wqkv0[:, kt, col:col + 512]) for kt in range(KT)]).then_inc(done, 1)
                        pe.wait_ge(rope_done, nth(it, N_ROPE, h, N_ROPE) + 2)
                        for hp in range(HP):
                            b, done = claim(pe, it, h, "qkv0", ("qkT", hp))
                            for s in range(2):
                                for tt in range(TT):
                                    last = tr(b[:, s * N + tt * P:s * N + (tt + 1) * P], roped[:, tt, s * IN0 + hp * P:s * IN0 + (hp + 1) * P], ident[:, :])
                            last.then_inc(done, 1)
                    if stage.startswith("qkvx"):
                        for kind, k in QKVX[2 * int(stage[-1]):2 * int(stage[-1]) + 2]:
                            b, done = claim(pe, it, h, "qkvx", (kind, k), [("load", "cT"), ("tx", "xT")])
                            if kind == "qk":
                                product(b[:, 0:N], [(wq[:, kt, tok(P, k)], xT[h][:, kt, :]) for kt in range(KT)])
                                product(b[:, N:2 * N], [(wk[:, kt, tok(P, k)], cT[h][:, kt, :]) for kt in range(KT)]).then_inc(done, 1)
                            else:
                                tt, n = divmod(k, 2)
                                product(b[:, :], [(cT[h][:, kt, tok(P, tt)], wv[:, kt, n * 512:(n + 1) * 512]) for kt in range(KT)]).then_inc(done, 1)
                    if stage == "att":
                        step = h
                        if unit_at(step):
                            att, h, u = unit_at(step)
                            hp, qb = divmod(u, 2)
                            prev = {"att0": "qkv0", "attx": "qkvx", "atty": "qkvy"}[att]
                            operands = []
                            if att != "atty":
                                operands.append((prev, ("qkT" if att == "att0" else "qk", hp)))
                            if u == 0:
                                operands += [(prev, name) for name in (("q", "k", "v") if att == "atty" else [("v", k) for k in range(4)])]
                            b, done = claim(pe, it, h, att, ("S", u), operands)
                            if att == "atty":
                                pe.wait_ge(km_ready, nth(it, H, h, 2 * hp + 2))
                                last = mm(b[:, :], xq[h][:, hp // 4, tok(P, qb)], km[h][:, 2 * hp:2 * hp + 2, :], start=True, stop=True)
                            else:
                                head = slice(DH * (u % 2), DH * (u % 2) + DH)
                                for qb in range(TT):
                                    keys = N if att == "attx" else P * (qb + 1)
                                    last = mm(b[:, qb * N:qb * N + keys], qkT[h][head, hp, 0, tok(P, qb)],
                                              qkT[h][head, hp, 1, 0:keys], start=True, stop=True)
                            last.then_inc(done, 1)
                        if unit_at(step - LAG):
                            w = step - LAG
                            att, h, u = WORK[w]
                            if att == "atty":
                                pe.wait_ge(p_exp, nth(it, UNITS, h, u + 1, 1, 2))
                            else:
                                pe.wait_ge(p_norm, probs(it, w))
                                pe.wait_ge(p_norm0, probs(it, w))
                            b, done = claim(pe, it, h, att, ("PT", u))
                            for s in range(2):
                                for kb in range(TT):
                                    if att == "att0" and kb > s:
                                        continue
                                    col = {"att0": kb + s, "attx": 2 * kb + s, "atty": 2 * s + kb}[att]
                                    last = tr(b[:, tok(P, col)], p_ring[:, w % P_SLOTS, s, tok(P, kb)], ident[:, :])
                            last.then_inc(done, 1)
                        if pair_at(step):
                            att, h, hp = pair_at(step)
                            slot = (step - O_LAG) // 2 % 2
                            operands = [(att, ("PT", 2 * hp)), (att, ("PT", 2 * hp + 1))]
                            if att == "atty":
                                if hp % 2 == 0:
                                    o_bank, o_done = claim(pe, it, h, att, ("O", hp), operands)
                                else:
                                    emptied_all(pe, it, h, att, [("PT", 2 * hp), ("PT", 2 * hp + 1)])
                                for kb in range(TT):
                                    for s in range(2):
                                        j = 2 * (hp % 2) + s
                                        last = mm(o_bank[32 * j:32 * j + 32, 0:N], Vy[h][:, kb, 2 * hp + s, :], PT[:, slot, 2 * s + kb, :],
                                                  start=(kb == 0), stop=(kb == 1))
                                if hp % 2:
                                    last.then_inc(o_done, 1)
                            else:
                                b, done = claim(pe, it, h, att, ("O", hp), operands)
                                for kb in range(TT):
                                    for s in range(2):
                                        q0 = P if att == "att0" and kb else 0
                                        last = mm(b[64 * s:64 * s + 64, q0:N], V[h][:, kb, (2 * hp + s) * DH:(2 * hp + s + 1) * DH],
                                                  pt_cols[:, slot, s, kb * N:kb * N + N - q0], start=(kb == 0), stop=(kb == 1))
                                last.then_inc(done, 1)
                    if stage in ("out0", "outx"):
                        att = "att0" if stage == "out0" else "attx"
                        w = wout0 if stage == "out0" else wo
                        token_tiles(h, stage, "out", lambda k, tt: OT[h][:, k, tok(P, tt)], lambda k: w[:, k, :], HP, [(att, ("O", HP - 1))])
                    if stage == "quant":
                        token_tiles(h, stage, "xh", lambda k, tt: xT[h][:, k, tok(P, tt)], lambda k: had[:, :] if k else had[:, None, 0:P].broadcast_to([P, 2, P]), KT,
                                    [("tq", "xT")])
                    if stage == "tf":
                        pe.wait_ge(qn_ready, nth(it, 1, h, 1))
                        b, done = claim(pe, it, h, stage, "qT")
                        bb = b[:, 0:256].bitcast(BF16)
                        for kt in range(KT):
                            for tt in range(TT):
                                last = tr(bb[:, kt * N + tt * P:kt * N + (tt + 1) * P], qn[h][:, tt, tok(P, kt)], identb[:, :])
                        last.then_inc(done, 1)
                    if stage == "ffn":
                        token_tiles(h, stage, "out", lambda k, tt: qnT[h][:, k, tok(P, tt)], lambda k: ternT[:, k, :], KT, [("tf", "qT")])
                    if stage == "qkv1":
                        for tt in range(TT):
                            b, done = claim(pe, it, h, stage, ("qk", tt), [("t1", "xT")])
                            product(b[:, :], [(xT[h][:, kt, tok(P, tt)], wqkv1[:, kt, 0:512]) for kt in range(KT)]).then_inc(done, 1)
                        token_tiles(h, stage, "v", lambda k, tt: xT[h][:, k, tok(P, tt)], lambda k: wqkv1[:, k, 512:768], KT)
                    if stage == "tl":
                        pe.wait_ge(lin_feat, nth(it, TT, h, TT))
                        turn(h, stage, "qT", qkf[h][:, :, 0:D])
                        turn(h, stage, "kT", qkf[h][:, :, D:2 * D])
                    if stage == "lin":
                        b, done = claim(pe, it, h, stage, "KV", [("qkv1", "v")])
                        for kt in range(KT):
                            last = mm(b[:, kt * 256:(kt + 1) * 256], qkf[h][:, 0, D + kt * P:D + (kt + 1) * P],
                                      Vy[h][:, 0, 8 * kt:8 * kt + 8, :], start=True, stop=True)
                        last.then_inc(done, 1)
                        for c in range(TT):
                            for q in range(4):
                                b, done = claim(pe, it, h, stage, ("A", c, q), [("tl", "qT"), ("tl", "kT")])
                                for kt in range(KT):
                                    last = mm(b[:, kt * 256:(kt + 1) * 256], kT[h][32 * q:32 * q + 32, kt, tok(P, c)],
                                              qm[h][32 * q:32 * q + 32, kt, :, tok(P, c)], start=True, stop=True)
                                last.then_inc(done, 1)
                    if stage == "lout":
                        operands = [("lin", "KV")] + [("lin", ("A", c, q)) for c in range(TT) for q in range(4)]
                        for kt in range(KT):
                            b, done = claim(pe, it, h, stage, ("oT", kt), operands)
                            for mi in range(2):
                                for c in range(TT):
                                    for j in range(4):
                                        lh = 4 * mi + j
                                        q, s = divmod(lh, 2)
                                        out = b[32 * j:32 * j + 32, mi * N + c * P:mi * N + (c + 1) * P]
                                        last = mm(out, Vy[h][:, c, 8 * kt + lh, :], AT[h][c][:, q, 2 * kt + s, :],
                                                  start=True, stop=(c == 0))
                                    if c == 1:
                                        for j in range(4):
                                            lh = 4 * mi + j
                                            out = b[32 * j:32 * j + 32, mi * N + P:mi * N + 2 * P]
                                            last = mm(out, KVm[h][:, kt, lh * VW:(lh + 1) * VW], qm[h][:, kt, lh % 2, P:2 * P],
                                                      start=False, stop=True)
                            last.then_inc(done, 1)
                    if stage in ("to", "outy"):
                        operands = [("lout", ("oT", kt)) for kt in range(KT)] if stage == "to" else [("atty", ("O", HP - 2))]
                        for tt in range(TT):
                            b, done = claim(pe, it, h, stage, ("o", tt), operands)
                            for m in range(4):
                                last = tr(b[:, tok(P, m)], oTr[h][:, m, tok(P, tt)], ident[:, :])
                            last.then_inc(done, 1)
                    if stage == "tp":
                        turn(h, stage, "oTT", o_tok[h], [("to", ("o", tt)) for tt in range(TT)])
                    if stage == "out1":
                        token_tiles(h, stage, "out", lambda k, tt: oTT[h][:, k, tok(P, tt)], lambda k: wout1[:, k, :], KT, [("tp", "oTT")])
                    if stage == "qkvy":
                        for name, w, src in (("q", wqy, xT[h]), ("k", wky, cT[h])):
                            b, done = claim(pe, it, h, stage, name, [("ty", "xT")])
                            for ft in range(KT):
                                last = product(b[:, ft * N:(ft + 1) * N], [(w[:, kt, tok(P, ft)], src[:, kt, :]) for kt in range(KT)])
                            last.then_inc(done, 1)
                        token_tiles(h, stage, "v", lambda k, tt: cT[h][:, k, tok(P, tt)], lambda k: wvy[:, k, :], KT)

        layers.close()

        xe, xeT, re, ye = x, xT, r, xb
        hT = [qk_area[i][:, 0:FT * N].rearrange("p (j n) -> p j n", j=FT) for i in HALVES]
        sg = v_area[0][:, 0:4 * N].rearrange("p (j n) -> p j n", j=4)

        def width(j):
            return P if j < FT - 1 else FR

        experts = ctx.enter_context(nc.Block())

        @experts.sync
        def _(sp):
            def tokens(i, e):
                sp.dma_start(xe[i][:, :, :], scratch[bass.ds(e, 1)].rearrange("o (t b) s n -> (b s) (o t) n", t=TT)).then_inc(tok_in[i], 16)

            def outputs(it, i):
                sp.wait_ge(y_ready, nth(it, 1, i, 1))
                for q in range(QTR):
                    to = out_d.rearrange("(t q) s n -> q s t n", q=QTR)[q, bass.ds((it * 2 + i) * TE, TE)]
                    sp.dma_start(to, ye[i][TE * q:TE * q + TE, :, :]).then_inc(y_stored[i], 16)

            for i in HALVES:
                tokens(i, i)
            with sp.Fori(0, ITERS - 1) as it:
                for i in HALVES:
                    b, k = moe_at(it, i, "out")
                    sp.wait_ge(drained[b], k + 2)
                    expert_weights(sp, i, it * 2 + i + 2)
                    tokens(i, it * 2 + i + 2)
                    outputs(it, i)
            for i in HALVES:
                outputs(ITERS - 1, i)

        @experts.gpsimd
        def _(pool):
            with pool.Fori(0, ITERS) as it:
                for i in HALVES:
                    pool.wait_ge(moe_stats, nth(it, 1, i, 1))
                    passed(pool)
                    nc.gpsimd.tensor_scalar(var_e[:, i, :], mv[:, i, :, 1], EPS, None, ALU.add).then_inc(pool_seq, 1)
                    pool.wait_ge(pool_seq, nth(it, 1, i, 1) + ITERS * POOL_LINKS)
                    nc.gpsimd.tensor_tensor(rstd[:, i, :], var_e[:, i, :], half_neg[:, :], ALU.pow).then_inc(moe_rstd, 1)
                for i in HALVES:
                    pool.wait_ge(y_stored[i], it * (16 * QTR) + 16 * QTR)
                    pool.sem_inc(y_free[i], 1)

        @experts.scalar
        def _(act):
            with act.Fori(0, ITERS) as it:
                for i in HALVES:
                    b, k = moe_at(it, i, "xT")
                    act.wait_ge(full[b], k + 1)
                    nc.scalar.activation(xeT[i][:, :, :], bank[b][:, :].rearrange("p (k n) -> p k n", k=KT), ACT.Copy).then_inc(drained[b], 1)
                    for j in range(FT):
                        b, k = moe_at(it, i, ("gu", j))
                        act.wait_ge(full[b], k + 1)
                        w = width(j)
                        nc.scalar.activation(sg[0:w, b - 1, :], bank[b][0:w, 0:N], ACT.Silu).then_inc(silu_done, 1)

        @experts.vector
        def _(dve):
            steps = 0
            with dve.Fori(0, ITERS) as it:
                for i in HALVES:
                    for j in range(FT):
                        b, k = moe_at(it, i, ("gu", j))
                        w = width(j)
                        dve.wait_ge(silu_done, nth(it, FT, i, j + 1))
                        nc.vector.tensor_tensor(hT[i][0:w, j, :], sg[0:w, b - 1, :], bank[b][0:w, N:2 * N], ALU.mult).then_inc(drained[b], 1)
                    b, k = moe_at(it, i, "out")
                    dve.wait_ge(full[b], k + 1)
                    dve.wait_ge(tok_in[i], it * 16 + 16)
                    nc.vector.tensor_tensor(re[i][:, :, :], bank[b][:, :].rearrange("p (t n) -> p t n", t=TT), xe[i][:, :, :], ALU.add).then_inc(drained[b], 1)
                    dve.wait_ge(drained[b], k + 2)
                    for tt in range(TT):
                        last = nc.vector.bn_stats(stats[:, tt, :], re[i][:, tt, :])
                    last.then_inc(dve_seq, 1)
                    dve.wait_ge(dve_seq, nth(it, 1, i, 1) + ITERS * DVE_LINKS)
                    passed(dve)
                    for tt in range(TT):
                        last = nc.vector.bn_aggr(mv[:, i, tt, :], stats[:, tt, :])
                    last.then_inc(moe_stats, 1)
                    dve.wait_ge(moe_rstd, nth(it, 1, i, 1))
                    dve.wait_ge(y_free[i], it + 1)
                    for tt in range(TT):
                        last = nc.vector.tensor_scalar(ye[i][:, tt, :], re[i][:, tt, :], mv[:, i, tt, 0:1], rstd[:, i, tt:tt + 1],
                                                       ALU.subtract, ALU.mult)
                    last.then_inc(y_ready, 1)

        @experts.tensor
        def _(pe):
            mm = nc.tensor.matmul
            with pe.Fori(0, ITERS) as it:
                for i in HALVES:
                    pe.wait_ge(tok_in[i], it * 16 + 16)
                    b, k = moe_at(it, i, "xT")
                    pe.wait_ge(drained[b], k + 1)
                    for kt in range(KT):
                        for tt in range(TT):
                            last = nc.tensor.transpose(bank[b][:, kt * N + tt * P:kt * N + (tt + 1) * P], xe[i][:, tt, kt * P:(kt + 1) * P], ident[:, :])
                    last.then_inc(full[b], 1)
                    pe.wait_ge(drained[b], k + 2)
                    pe.wait_ge(w_in[i], it * 64 + 64)
                    for j in range(FT):
                        b, k = moe_at(it, i, ("gu", j))
                        pe.wait_ge(drained[b], k + 1)
                        w = width(j)
                        for s, wx in enumerate((w1[i], w3[i])):
                            for kt in range(KT):
                                last = mm(bank[b][0:w, s * N:(s + 1) * N], wx[:, kt, j * P:j * P + w], xeT[i][:, kt, :],
                                          start=(kt == 0), stop=(kt == KT - 1))
                        last.then_inc(full[b], 1)
                    for j in range(FT - 4, FT):
                        gb, gk = moe_at(it, i, ("gu", j))
                        pe.wait_ge(drained[gb], gk + 2)
                    b, k = moe_at(it, i, "out")
                    pe.wait_ge(drained[b], k + 1)
                    for tt in range(TT):
                        for j in range(FT):
                            w = width(j)
                            last = mm(bank[b][:, tt * D:(tt + 1) * D], hT[i][0:w, j, tt * P:(tt + 1) * P], w2[i][0:w, j, :],
                                      start=(j == 0), stop=(j == FT - 1))
                    last.then_inc(full[b], 1)


def shape_constants():
    f32 = np.float32

    def rotary(dh, tokens):
        inv = (1.0 / 10000.0 ** (np.arange(0, dh, 2, dtype=np.float64) / dh)).astype(f32)
        angle = (np.arange(tokens, dtype=f32)[:, None] * inv[None, :]).astype(f32)
        c, s = np.cos(angle.astype(np.float64)), np.sin(angle.astype(np.float64))
        return np.concatenate([c, c], 1), np.concatenate([-s, s], 1)

    c0, s0 = rotary(DH, N)
    rope0 = np.stack([np.stack([-c0, -s0], 1) * DH ** -0.5, np.stack([c0, s0], 1)], 1)
    c1, s1 = rotary(D1, N)
    rope1 = np.stack([c1, s1], 1) * D1 ** -0.25
    q, k = np.arange(P)[:, None], np.arange(P)[None, :]
    causal = np.where(k <= q, 0.0, BIG)
    window = np.where(k >= q, 0.0, BIG)
    mask0 = np.stack([causal, window, causal], 1)
    tri = (q <= k) * 1.0
    parity = np.stack([(np.arange(P) % 32) < 16, (np.arange(P) % 32) >= 16], 1) * 1.0
    heads8 = (np.arange(P)[:, None] // D1 == np.arange(8)[None, :]) * 1.0
    bdm = np.repeat((np.arange(P)[:, None] // D1 == np.arange(8)[None, :])[:, :, None], VW, 2) * 1.0
    had = np.ones((1, 1))
    while had.shape[0] < D:
        had = np.block([[had, had], [had, -had]])
    had = had / np.sqrt(D)
    return {"c_ident": np.eye(P), "c_rope0": rope0.reshape(N, -1), "c_rope1": rope1.reshape(N, -1), "c_mask0": mask0,
            "c_tri": tri, "c_par": parity, "c_rows8": heads8, "c_bdm": bdm, "c_had": had[P:, :]}


def kernel(**inputs):
    import concourse.bacc as bacc
    from concourse.bass_utils import run_bass_kernel_spmd

    def arr(name):
        return np.asarray(inputs[name])

    def columns(a):
        return np.ascontiguousarray(a.reshape(-1, P).T)

    feeds = {
        "x": arr("x"), "ctx": arr("ctx_1024"),
        "padm": arr("mask_Bx1x1xS2_ik0").reshape(B, N), "subm": arr("mask_1x1xSxS2_ik0").reshape(N, N),
        "wqkv0": arr("L0_attn_W_qkv"), "wout0": arr("L0_attn_W_out"),
        "wq": arr("L0_xattn_Wq").reshape(D, IN0), "bq": columns(arr("L0_xattn_bq")),
        "wk": arr("L0_xattn_Wk").reshape(D, IN0), "bk": columns(arr("L0_xattn_bk")),
        "wv": arr("L0_xattn_Wv").reshape(D, IN0), "bv": columns(arr("L0_xattn_bv")),
        "wo": arr("L0_xattn_Wo").reshape(IN0, D), "bo": arr("L0_xattn_bo"),
        "ffn": arr("L0_ffn_weight"), "wqkv1": arr("L1_attn_w_qkv"), "wout1": arr("L1_attn_w_out"),
        "wqy": arr("L1_xattn_Wq").T, "bqy": columns(arr("L1_xattn_bq")),
        "wky": arr("L1_xattn_Wk").T, "bky": columns(arr("L1_xattn_bk")),
        "wvy": arr("L1_xattn_Wv").T, "bvy": arr("L1_xattn_bv"),
        "w1": arr("L1_ffn_w1"), "w3": arr("L1_ffn_w3"), "w2": arr("L1_ffn_w2"),
    }
    for name, a in shape_constants().items():
        feeds[name] = a.astype(np.float32)
    nc = bacc.Bacc("TRN2", target_bir_lowering=False, num_devices=1)
    arrays, args = {}, []
    for name, a in feeds.items():
        arrays[f"in_{name}"] = np.ascontiguousarray(a)
        args.append(nc.dram_tensor(f"in_{name}", a.shape, mybir.dt.from_np(a.dtype), kind="ExternalInput").ap())
    args.append(nc.dram_tensor("out_0", (B, N, D), F32, kind="ExternalOutput").ap())
    decoder_kernel(nc, *args)
    result = run_bass_kernel_spmd(nc, [arrays], core_ids=[0])
    return result.results[0]["out_0"]
```

```python
from contextlib import ExitStack

import numpy as np
import concourse.bass as bass
from concourse import mybir

F32 = mybir.dt.float32
BF16 = mybir.dt.bfloat16
I32 = mybir.dt.int32
ALU = mybir.AluOpType
ACT = mybir.ActivationFunctionType
AX = mybir.AxisListType

P = 128
B = 8
N = 256
D = 256
TT = N // P
KT = D // P
H = 16
DH = 64
HP = H // 2
IN0 = H * DH
D1 = D // H
VW = 32
E = 8
F = 704
FT = -(-F // P)
FR = F - (FT - 1) * P
TE = N // E
BIG = 3.0e38
MAGIC = 12582912.0
EPS = 1e-5
ITERS = B // 2
HALVES = (0, 1)

RINGS = {"S": (0, 1, 2), "T": (3, 4), "O": (5,), "G": (6, 7)}
MOE_RINGS = {"G": (0,), "U": (1, 2, 3, 4), "Y0": (5,), "Y1": (6,)}

UNITS = 2 * HP
LAG = 4
O_LAG = LAG + 2
P_SLOTS = LAG + 1
SLOTS = 8
N_ROPE = TT * 4
GAP = O_LAG

WORK = []
for _stage, _h, _gap in (("att0", 0, 0), ("att0", 1, 0), ("attx", 0, GAP), ("attx", 1, GAP), ("atty", 0, GAP), ("atty", 1, 0)):
    WORK += [(_stage, _h, _u) for _u in range(UNITS)] + [None] * _gap
N_STEPS = len(WORK) + O_LAG
QKVX = [("qk", hp) for hp in range(HP)] + [("v", k) for k in range(4)]
QKV0 = {"qkv0.v0": [("v", 0), ("v", 1)], "qkv0.v1": [("v", 2), ("v", 3)], "qkv0.qk": [("qk", k) for k in range(N_ROPE)]}
QKVX_PARTS = 6


def unit_at(step):
    return WORK[step] if 0 <= step < len(WORK) else None


def n_normalised(step):
    return sum(1 for unit in WORK[:step + 1] if unit and unit[0] != "atty")


def pair_at(step):
    unit = unit_at(step - O_LAG)
    return (unit[0], unit[1], unit[2] // 2) if unit and unit[2] % 2 == 0 else None


def stage_groups():
    return {
        "load": [("xT", "G"), ("cT", "G")],
        **{stage: [(name, "G") for name in names] for stage, names in QKV0.items()},
        "qkv0.t": [(("qkT", hp), "T") for hp in range(HP)],
        "out0": [("out", "G")],
        "tx": [("xT", "G")],
        **{f"qkvx.{p}": [(name, "G") for name in QKVX[2 * p:2 * p + 2]] for p in range(QKVX_PARTS)},
        "outx": [("out", "G")],
        "tq": [("xT", "G")],
        "quant": [("xh", "G")],
        "tf": [("qT", "T")],
        "ffn": [("out", "G")],
        "t1": [("xT", "G")],
        "qkv1": [(("qk", 0), "G"), (("qk", 1), "G"), ("v", "G")],
        "tl": [("qT", "T"), ("kT", "T")],
        "lin": [("KV", "G")] + [(("A", c, r), "S") for c in range(TT) for r in range(4)],
        "lout": [(("oT", i), "G") for i in range(2)],
        "to": [(("o", tt), "T") for tt in range(TT)],
        "tp": [("oTT", "T")],
        "out1": [("out", "G")],
        "ty": [("xT", "G")],
        "qkvy": [("q", "G"), ("k", "G"), ("v", "G")],
        "outy": [(("o", tt), "T") for tt in range(TT)],
        **{stage: [] for stage in ("nx", "nq", "n1", "f1", "ny", "nz")},
    }


def attention_fills(step):
    fills = []
    if unit_at(step):
        stage, h, u = unit_at(step)
        fills.append((h, stage, ("S", u), "S"))
    if unit_at(step - LAG):
        stage, h, u = unit_at(step - LAG)
        fills.append((h, stage, ("PT", u), "T"))
    if pair_at(step):
        stage, h, hp = pair_at(step)
        if stage != "atty" or hp % 2 == 0:
            fills.append((h, stage, ("O", hp), "O"))
    return fills


def plan(order, groups, rings):
    turn = {ring: 0 for ring in rings}
    fills = [0] * 8
    place = {}
    for who, item in order:
        stage = item.split(".")[0]
        made = attention_fills(who) if item == "att" else [(who, stage, name, ring) for name, ring in groups[item]]
        for half, stage, name, ring in made:
            ring = f"{ring}{half}" if ring == "Y" else ring
            b = rings[ring][turn[ring] % len(rings[ring])]
            turn[ring] += 1
            place[(half, stage, name)] = (b, fills[b])
            fills[b] += 1
    return place, fills


SCHEDULE = [
    "a load", "b load", "a qkv0.v0", "a qkv0.v1", "b qkv0.v0", "a qkv0.qk", "b qkv0.v1", "a qkv0.t", "b qkv0.qk", 3,
    "b qkv0.t", 20, "a out0", 1, "a nx", 1, "a tx", 1, "a qkvx.0", "a qkvx.1", "a qkvx.3", "a qkvx.4", 2, "a qkvx.2",
    2, "a qkvx.5", 8, "b out0", 3, "b nx", 3, "b tx", 4, "b qkvx.0", 2, "b qkvx.1", 4, "a outx", "a nq", "b qkvx.2",
    "a tq", "b qkvx.3", "a quant", "b qkvx.4", "a tf", "b qkvx.5", "a ffn", 2, "a n1", 2, "a t1", 1, "a qkv1", "a f1",
    5, "a tl", 5, "a lin", 3, "a lout", 1, "a to", 2, "a tp", 1, "a out1", "a ny", "b outx", "a ty", "b nq", "a qkvy",
    "b tq", "b quant", 2, "b tf", 2, "b ffn", 3, "b n1", "b t1", 1, "b qkv1", "b f1", 2, "b tl", 4, "b lin", 1,
    "b lout", 1, "b to", 1, "b tp", 1, "b out1", "b ny", 4, "b ty", "b qkvy", 4, "a outy", 1, "a nz", 18, "b outy",
    "b nz",
]


def iteration_order():
    order, step = [], 0
    for turn in SCHEDULE:
        if isinstance(turn, int):
            order += [(step + n, "att") for n in range(turn)]
            step += turn
        else:
            half, stage = turn.split()
            order.append(("ab".index(half), stage))
    assert step == N_STEPS + 1
    return order


ORDER = iteration_order()
LN = {"out0": 0, "outx": 1, "ffn": 2, "out1": 3, "outy": 4}
NORM = {"nx": "out0", "nq": "outx", "n1": "ffn", "ny": "out1", "nz": "outy"}
N_LN = len(LN)
STATS_RANK = {item: k for k, item in enumerate([item for item in ORDER if item[1] in LN])}
NORM_RANK = {(h, NORM[stage]): k for k, (h, stage) in enumerate([item for item in ORDER if item[1] in NORM])}
PLACE, FILLS = plan(ORDER, stage_groups(), RINGS)
MOE_PLACE, MOE_FILLS = plan([(h, stage) for stage in ("gates", "down") for h in HALVES],
                            {"gates": [("xT", "G")] + [(("gu", j), "U") for j in range(FT)], "down": [("out", "Y")]}, MOE_RINGS)
QTR = P // TE
N_SETUP_DVE = 14
SETUP_IN, OUT0_IN, ATTX_IN, REST_IN = 16 * 5, 16 * 2, 16 * 6, 16 * 14
DVE_LINKS = 38
POOL_LINKS = 12


def decoder_kernel(nc, x_d, ctx_d, padm_d, subm_d, wqkv0_d, wout0_d, wq_d, bq_d, wk_d, bk_d, wv_d, bv_d,
                   wo_d, bo_d, ffn_d, wqkv1_d, wout1_d, wqy_d, bqy_d, wky_d, bky_d, wvy_d, bvy_d,
                   w1_d, w3_d, w2_d, ident_d, rope0_d, rope1_d, mask0_d, tri_d, par_d, rows8_d, bdm_d, had_d, out_d):
    ctx = ExitStack()
    with ctx:
        def sb(name, shape, dt=F32):
            return ctx.enter_context(nc.sbuf_tensor(name, shape, dt))

        def sem(name):
            return ctx.enter_context(nc.semaphore(name))

        w_area = sb("w_area", [P, 16384])
        wqkv0 = w_area[:, 0:6144].rearrange("p (k n) -> p k n", k=KT)
        wout0 = w_area[:, 6144:8192].rearrange("p (k n) -> p k n", k=HP)
        wq = w_area[:, 8192:10240].rearrange("p (k n) -> p k n", k=KT)
        wk = w_area[:, 10240:12288].rearrange("p (k n) -> p k n", k=KT)
        wv = w_area[:, 12288:14336].rearrange("p (k n) -> p k n", k=KT)
        wo = w_area[:, 14336:16384].rearrange("p (k n) -> p k n", k=HP)
        EW = 2 * KT * F + FT * D
        w1 = [w_area[:, i * EW:i * EW + KT * F].rearrange("p (k n) -> p k n", k=KT) for i in range(2)]
        w3 = [w_area[:, i * EW + KT * F:i * EW + 2 * KT * F].rearrange("p (k n) -> p k n", k=KT) for i in range(2)]
        w2 = [w_area[:, i * EW + 2 * KT * F:(i + 1) * EW].rearrange("p (k n) -> p k n", k=FT) for i in range(2)]
        wqkv1 = sb("wqkv1", [P, KT, 3 * D])
        wout1 = sb("wout1", [P, KT, D])
        wqy = sb("wqy", [P, KT, D])
        wky = sb("wky", [P, KT, D])
        wvy = sb("wvy", [P, KT, D])
        had = sb("had", [P, D])
        ternT = sb("ternT", [P, KT, D], BF16)
        ident = sb("ident_s", [P, P])
        identb = sb("identb", [P, P], BF16)
        rope0 = sb("rope0", [P, TT, 2, 2, DH])
        rope1 = sb("rope1", [P, TT, 2, D1])
        mask0 = sb("mask0", [P, 3, P])
        tri = sb("tri", [P, P])
        par = sb("par", [P, 2])
        head_rows = sb("head_rows", [P, 8])
        bdm = sb("bdm", [P, 8, VW])
        bq = sb("bq", [P, HP])
        bk = sb("bk", [P, HP])
        bv = sb("bv", [P, HP])
        bqy = sb("bqy", [P, KT])
        bky = sb("bky", [P, KT])
        bo_row = sb("bo_row", [P, D])
        bvy_row = sb("bvy_row", [P, D])
        bq_s = sb("bq_s", [P, HP])
        bqy_s = sb("bqy_s", [P, KT])
        wscale_row = sb("wscale_row", [P, D])
        sub_kept = sb("sub_kept", [P, TT, N], BF16)
        half_neg = sb("half_neg", [P, TT])
        x = [sb(f"x{h}", [P, TT, D]) for h in HALVES]
        xb = [sb(f"xb{h}", [P, TT, D]) for h in HALVES]
        r = [sb(f"r{h}", [P, TT, D]) for h in HALVES]
        cx = [sb(f"cx{h}", [P, TT, D]) for h in HALVES]
        xT = [sb(f"xT{h}", [P, KT, N]) for h in HALVES]
        cT = [sb(f"cT{h}", [P, KT, N]) for h in HALVES]
        qk_area = [sb(f"qk_area{h}", [P, HP * 2 * N]) for h in HALVES]
        v_area = [sb(f"v_area{h}", [P, TT * IN0]) for h in HALVES]
        o_area = sb("o_area", [P, 2 * HP * N])
        Vy = [sb(f"Vy{h}", [P, TT, H, VW]) for h in HALVES]
        p_ring = sb("p_ring", [P, P_SLOTS, 2, N])
        pt_area = sb("pt_area", [P, 2 * 4 * N])
        qkT = [a[:, :].rearrange("p (m s n) -> p m s n", m=HP, s=2) for a in qk_area]
        V = [a[:, :].rearrange("p (t n) -> p t n", t=TT) for a in v_area]
        OT = [o_area[:, h * HP * N:(h + 1) * HP * N].rearrange("p (m n) -> p m n", m=HP) for h in HALVES]
        roped = o_area[:, :].rearrange("p (t n) -> p t n", t=TT)
        PT = pt_area[:, :].rearrange("p (i a n) -> p i a n", i=2, a=4)
        pt_cols = pt_area[:, :].rearrange("p (i s n) -> p i s n", i=2, s=2)
        rope_t = pt_area[:, :].rearrange("p (i a n) -> p i a n", i=2, a=2)
        rope_t1 = [o_area[:, h * HP * N:(h + 1) * HP * N].rearrange("p (i a n) -> p i a n", i=2, a=2) for h in HALVES]
        qm = [a[:, 0:1024].rearrange("p (k s n) -> p k s n", k=KT, s=2) for a in qk_area]
        kT = [a[:, 1024:1536].rearrange("p (k n) -> p k n", k=KT) for a in qk_area]
        KVm = [a[:, 1536:2048].rearrange("p (k n) -> p k n", k=KT) for a in qk_area]
        AT = [[OT_area[:, :].rearrange("p (r a n) -> p r a n", r=4, a=4) for OT_area in
               (o_area[:, h * HP * N:(h + 1) * HP * N], qk_area[h][:, 2048:4096])] for h in HALVES]
        qkf = [a[:, 0:1024].rearrange("p (t n) -> p t n", t=TT) for a in v_area]
        elu_m = [a[:, 1024:2048].rearrange("p (t n) -> p t n", t=TT) for a in v_area]
        oTr = [a[:, 1024:2048].rearrange("p (m n) -> p m n", m=4) for a in v_area]
        oTT = [a[:, 512:1024].rearrange("p (k n) -> p k n", k=KT) for a in v_area]
        o_tok = [a[:, 0:512].rearrange("p (t n) -> p t n", t=TT) for a in v_area]
        y_tok = [a[:, 1536:2048].rearrange("p (t n) -> p t n", t=TT) for a in qk_area]
        km = [a[:, :].rearrange("p (m n) -> p m n", m=H) for a in qk_area]
        ky = [a[:, 1536:2048].rearrange("p (k n) -> p k n", k=KT) for a in v_area]
        mask1 = [a[:, 512:1024].rearrange("p (t n) -> p t n", t=TT) for a in v_area]
        pad_i = [sb(f"pad_i{h}", [P, N], I32) for h in HALVES]
        pad_kept = [a[:, :].bitcast(F32) for a in pad_i]
        qn = [a[:, 0:256].bitcast(BF16).rearrange("p (t n) -> p t n", t=TT) for a in v_area]
        qnT = [a[:, 256:512].bitcast(BF16).rearrange("p (k n) -> p k n", k=KT) for a in v_area]
        negmax = sb("negmax", [P, SLOTS, 2])
        rowsum = sb("rowsum", [P, SLOTS, 2])
        rowinv = sb("rowinv", [P, SLOTS, 2])
        stats = sb("stats", [P, TT, 6])
        mv = sb("mv", [P, 2, TT, 2])
        var_e = sb("var_e", [P, 2, TT])
        rstd = sb("rstd", [P, 2, TT])
        amax = sb("amax", [P, TT])
        aq = sb("aq", [P, 2, TT])
        rden = sb("rden", [P, 2, H])
        wst = sb("wst", [P, KT, 4])
        ones = v_area[0][:, 0:P]
        diag = v_area[0][:, P:P + D].rearrange("p (k n) -> p k n", k=KT)

        bank = [ctx.enter_context(nc.psum_tensor(f"bank{i}", [P, 512], F32)) for i in range(8)]
        scratch = nc.dram_tensor("x_by_expert", (E, B, TE, D), F32, kind="Internal").ap()

        xq = [a[:, 0:512].rearrange("p (k n) -> p k n", k=KT) for a in v_area]

        full = [sem(f"full{b}") for b in range(8)]
        drained = [sem(f"drained{b}") for b in range(8)]
        setup_in = sem("setup_in")
        w0_in = [sem(f"w0_in{n}") for n in range(6)]
        rope_in = sem("rope_in")
        out0_in = sem("out0_in")
        attx_in = sem("attx_in")
        rest_in = sem("rest_in")
        x_in = [sem(f"x_in{h}") for h in HALVES]
        pad_in = [sem(f"pad_in{h}") for h in HALVES]
        stored = [sem(f"stored{h}") for h in HALVES]     
        setup_pool = sem("setup_pool")
        setup_dve = sem("setup_dve")
        setup_pe = sem("setup_pe")
        setup_act = sem("setup_act")
        rope_done = sem("rope_done")
        s_max = sem("s_max")
        p_exp = sem("p_exp")
        inv_ready = sem("inv_ready")
        p_norm = sem("p_norm")
        p_norm0 = sem("p_norm0")
        ln_stats = sem("ln_stats")
        ln_rstd = sem("ln_rstd")
        x_ready = sem("x_ready")
        xb_ready = sem("xb_ready")
        lin_rot = sem("lin_rot")
        lin_relu = sem("lin_relu")
        lin_exp = sem("lin_exp")
        lin_feat = sem("lin_feat")
        qn_ready = sem("qn_ready")
        km_ready = sem("km_ready")
        mask1_ready = sem("mask1_ready")
        waits_passed = sem("waits_passed")
        dve_seq = sem("dve_seq")
        pool_kept = sem("pool_kept")
        pool_seq = sem("pool_seq")
        w13_in = [sem(f"w13_in{i}") for i in HALVES]
        w2_in = [sem(f"w2_in{i}") for i in HALVES]
        tok_in = [sem(f"tok_in{i}") for i in HALVES]
        silu_done = sem("silu_done")
        moe_stats = sem("moe_stats")
        moe_rstd = sem("moe_rstd")
        y_ready = sem("y_ready")
        y_stored = [sem(f"y_stored{i}") for i in HALVES]
        y_free = [sem(f"y_free{i}") for i in HALVES]

        def nth(it, n, h, k, stage=0, stages=1):
            return it * (2 * n * stages) + ((2 * stage + h) * n + k)

        def probs(it, w):
            return it * n_normalised(len(WORK)) + n_normalised(w)

        def normed(it, h, stage):
            return it * (2 * N_LN) + (NORM_RANK[(h, stage)] + 1)

        def summed(it, h, stage):
            return it * (2 * N_LN) + (STATS_RANK[(h, stage)] + 1)

        def filled(eng, it, h, stage, name):
            b, k = PLACE[(h, stage, name)]
            eng.wait_ge(full[b], it * FILLS[b] + (k + 1))
            return bank[b], drained[b]

        def emptied(eng, it, h, stage, name):
            b, k = PLACE[(h, stage, name)]
            eng.wait_ge(drained[b], it * FILLS[b] + (k + 2))

        def emptied_all(eng, it, h, stage, names):
            last = {PLACE[(h, stage, name)][0]: name for name in names}
            for name in last.values():
                emptied(eng, it, h, stage, name)

        def claim(eng, it, h, stage, name, operands=()):
            b, k = PLACE[(h, stage, name)]
            count = {b: k + 1}
            for source in operands:
                source_b, source_k = PLACE[(h, *source)]
                count[source_b] = max(count.get(source_b, 0), source_k + 2)
            for waited, c in count.items():
                eng.wait_ge(drained[waited], it * FILLS[waited] + c)
            return bank[b], full[b]

        def moe_at(it, i, name):
            b, k = MOE_PLACE[(i, "down" if name == "out" else "gates", name)]
            return b, it * MOE_FILLS[b] + (ITERS * FILLS[b] + k)

        def rows(dram):
            return dram.rearrange("(k p) n -> p k n", p=P)

        layers = ExitStack()
        block = layers.enter_context(nc.Block())

        def gate_weights(sp, i, e):
            for dst, src in ((w1[i], w1_d), (w3[i], w3_d)):
                sp.dma_start(dst, src[bass.ds(e, 1)].rearrange("o (k p) n -> p (o k) n", p=P)).then_inc(w13_in[i], 16)

        def down_weight(sp, i, e):
            main = (FT - 1) * P
            sp.dma_start(w2[i][:, 0:FT - 1, :], w2_d[bass.ds(e, 1), 0:main].rearrange("o (k p) n -> p (o k) n", p=P)).then_inc(w2_in[i], 16)
            sp.dma_start(w2[i][0:FR, FT - 1, :], w2_d[bass.ds(e, 1), main:F].rearrange("o p n -> p (o n)")).then_inc(w2_in[i], 16)

        def passed(eng):
            eng.sem_inc(waits_passed, 1)

        @block.sync
        def _(sp):
            def load(sem_in, *pairs, count=None):
                for dst, src in pairs:
                    sp.dma_start(dst, src).then_inc(sem_in, 16)
                assert count in (None, 16 * len(pairs))

            def sequences(it):
                for h in HALVES:
                    g = it * 2 + h
                    load(x_in[h], (x[h][:, :, :], x_d[bass.ds(g, 1)].rearrange("o (t p) n -> p (o t) n", p=P)),
                         (cx[h][:, :, :], ctx_d[bass.ds(g, 1)].rearrange("o (t p) n -> p (o t) n", p=P)))
                    load(pad_in[h], (pad_i[h][:, :], padm_d[bass.ds(g, 1)].rearrange("o n -> (o n)").partition_broadcast(P)))

            def results(it):
                for h in HALVES:
                    sp.wait_ge(x_ready, normed(it, h, "outy"))
                    for q in range(QTR):
                        to = scratch.rearrange("(t q) b s n -> q b s t n", q=QTR)[q, bass.ds(it * 2 + h, 1)]
                        load(stored[h], (to.rearrange("o s t n -> (o s) t n"), xb[h][TE * q:TE * q + TE, :, :]))

            load(setup_in, (xb[0][:, :, :], rows(ffn_d)), (r[0][:, :, :].bitcast(I32), rows(subm_d)),
                                    (ident[:, :], ident_d), (bq[:, :], bq_d), (bqy[:, :], bqy_d), count=SETUP_IN)
            sequences(0)
            w0 = rows(wqkv0_d)
            for n in (4, 5, 0, 1, 2, 3):
                load(w0_in[n], (wqkv0[:, :, n * 512:(n + 1) * 512], w0[:, :, n * 512:(n + 1) * 512]))
                if n == 5:
                    load(rope_in, (rope0[:, :, :, :, :].rearrange("p t a c d -> p t (a c d)"), rope0_d.rearrange("(t p) n -> p t n", p=P)))
            load(out0_in, (mask0[:, :, :], mask0_d), (wout0, rows(wout0_d)), count=OUT0_IN)
            load(attx_in, (bk[:, :], bk_d), (bv[:, :], bv_d), (bo_row[:, :], bo_d.partition_broadcast(P)),
                                   (wq, rows(wq_d)), (wk, rows(wk_d)), (wv, rows(wv_d)), count=ATTX_IN)
            load(
                rest_in, (wo, rows(wo_d)), (had[:, :], had_d), (wqkv1[:, :, :], rows(wqkv1_d)),
                (rope1[:, :, :, :].rearrange("p t c d -> p t (c d)"), rope1_d.rearrange("(t p) n -> p t n", p=P)),
                (tri[:, :], tri_d), (par[:, :], par_d), (head_rows[:, :], rows8_d), (bdm[:, :, :], bdm_d),
                (wout1[:, :, :], rows(wout1_d)), (wqy[:, :, :], rows(wqy_d)), (wky[:, :, :], rows(wky_d)),
                (wvy[:, :, :], rows(wvy_d)), (bky[:, :], bky_d), (bvy_row[:, :], bvy_d.partition_broadcast(P)), count=REST_IN)
            with sp.Fori(0, ITERS - 1) as it:
                sp.wait_ge(xb_ready, nth(it, 1, 1, 1, 1, 2) + 4)
                sequences(it + 1)
                results(it)
            b, k = PLACE[(1, "qkvx", ("v", 3))]
            sp.wait_ge(drained[b], (ITERS - 1) * FILLS[b] + k + 2)
            for i in HALVES:
                gate_weights(sp, i, i)
                down_weight(sp, i, i)
            results(ITERS - 1)

        @block.gpsimd
        def _(pool):
            for b in range(8):
                pool.sem_inc(drained[b], 1)
            pool.sem_inc(rope_done, 2)
            pool.sem_inc(xb_ready, 4)
            for h in HALVES:
                pool.sem_inc(y_free[h], 1)
            nc.gpsimd.memset(half_neg[:, :], -0.5).then_inc(setup_pool, 1)
            nc.gpsimd.memset(ones[:, :], 1.0).then_inc(setup_pool, 1)
            for h in HALVES:
                nc.gpsimd.memset(Vy[h][:, :, :, :], 0.0).then_inc(setup_pool, 1)
            pool.wait_ge(setup_pool, 4)
            for h in HALVES:
                nc.gpsimd.memset(Vy[h][:, :, :, D1:D1 + 1], 1.0).then_inc(setup_pool, 1)
            pool.wait_ge(setup_in, SETUP_IN)
            nc.gpsimd.tensor_scalar(sub_kept[:, :, :], r[0][:, :, :].bitcast(I32), 0.0, None, ALU.is_equal).then_inc(setup_pool, 1)
            pool.wait_ge(setup_pool, 7)
            nc.gpsimd.tensor_scalar(sub_kept[:, :, :], sub_kept[:, :, :], -1.0, 1.0, ALU.mult, ALU.add).then_inc(setup_pool, 1)
            pool.wait_ge(setup_pool, 8)
            with pool.Fori(0, ITERS) as it:
                steps = 0

                def link(ins):
                    nonlocal steps
                    steps += 1
                    ins.then_inc(pool_seq, 1)
                    pool.wait_ge(pool_seq, it * POOL_LINKS + steps)
                    passed(pool)

                def head_keys(h, hp):
                    for m in (2 * hp, 2 * hp + 1):
                        nc.gpsimd.tensor_scalar(km[h][:, m, :], ky[h][:, m // 8, :], head_rows[:, m % 8:m % 8 + 1], None,
                                                ALU.mult).then_inc(km_ready, 1)

                for h, stage in ORDER:
                    step = h if stage == "att" else None
                    if stage == "qkv0.qk":
                        for k in range(N_ROPE):
                            tt, n = divmod(k, 4)
                            emptied(pool, it, h, "qkv0", ("qk", k))
                            nc.gpsimd.tensor_tensor(roped[:, tt, n * 512:(n + 1) * 512], rope_t[:, k % 2, 0, :],
                                                    rope_t[:, k % 2, 1, :], ALU.add).then_inc(rope_done, 1)
                    if stage == "ty":
                        pool.wait_ge(rest_in, REST_IN)
                    if stage == "tx":
                        pool.wait_ge(pad_in[h], it * 16 + 16)
                        passed(pool)
                        nc.gpsimd.tensor_scalar(pad_kept[h], pad_i[h][:, :], 0.0, 0.0, ALU.is_equal, ALU.is_equal).then_inc(pool_kept, 1)
                        pool.wait_ge(attx_in, ATTX_IN)
                        pool.wait_ge(x_ready, normed(it, h, "out0"))
                        nc.gpsimd.tensor_tensor(xb[h][:, :, :], x[h][:, :, :], bo_row[:, None, :].broadcast_to([P, TT, D]),
                                                ALU.add).then_inc(xb_ready, 1)
                    if stage == "att" and unit_at(step - 1) and unit_at(step - 1)[0] != "atty":
                        w = step - 1
                        att, h, u = WORK[w]
                        keys = P if att == "att0" else N
                        pool.wait_ge(inv_ready, probs(it, w))
                        passed(pool)
                        nc.gpsimd.tensor_scalar(p_ring[:, w % P_SLOTS, 0, 0:keys], p_ring[:, w % P_SLOTS, 0, 0:keys],
                                                rowinv[:, w % SLOTS, 0:1], None, ALU.mult).then_inc(p_norm0, 1)
                    if stage == "ty":
                        pool.wait_ge(x_ready, normed(it, h, "out1"))
                        pool.wait_ge(pool_kept, nth(it, 1, h, 1))
                        link(nc.gpsimd.tensor_tensor(mask1[h][:, :, :], sub_kept[:, :, :], pad_kept[h][:, None, :].broadcast_to([P, TT, N]), ALU.mult))
                        nc.gpsimd.tensor_scalar(mask1[h][:, :, :], mask1[h][:, :, :], -BIG, BIG, ALU.mult, ALU.add).then_inc(mask1_ready, 1)
                    if stage == "qkvy":
                        emptied(pool, it, h, stage, "k")
                        passed(pool)
                        head_keys(h, 0)
                        head_keys(h, 1)
                        emptied(pool, it, h, "ty", "xT")
                        nc.gpsimd.tensor_tensor(xb[h][:, :, :], x[h][:, :, :], bvy_row[:, None, :].broadcast_to([P, TT, D]),
                                                ALU.add).then_inc(xb_ready, 1)
                    if stage == "att" and unit_at(step) and unit_at(step)[0] == "atty" and unit_at(step)[2] % 2 == 0:
                        att, h, u = unit_at(step)
                        if u // 2 + 2 < HP:
                            head_keys(h, u // 2 + 2)
                    if stage in LN:
                        pool.wait_ge(ln_stats, summed(it, h, stage))
                        passed(pool)
                        link(nc.gpsimd.tensor_scalar(var_e[:, h, :], mv[:, h, :, 1], EPS, None, ALU.add))
                        nc.gpsimd.tensor_tensor(rstd[:, h, :], var_e[:, h, :], half_neg[:, :], ALU.pow).then_inc(ln_rstd, 1)
                for h in HALVES:
                    pool.wait_ge(stored[h], it * (16 * QTR) + 16 * QTR)
                assert steps == POOL_LINKS, f"POOL_LINKS {steps}"

        @block.scalar
        def _(act):
            act.wait_ge(setup_in, SETUP_IN)
            nc.scalar.activation(bq_s[:, :], bq[:, :], ACT.Copy, scale=DH ** -0.5).then_inc(setup_act, 1)
            nc.scalar.activation(bqy_s[:, :], bqy[:, :], ACT.Copy, scale=-D1 ** -0.5).then_inc(setup_act, 1)
            act.wait_ge(setup_act, 2)
            act.wait_ge(setup_dve, N_SETUP_DVE)
            with act.Fori(0, ITERS) as it:

                def copy_out(h, stage, name, dst, shape=None, cols=512, **view):
                    b, done = filled(act, it, h, stage, name)
                    src = b[:, 0:cols]
                    if shape:
                        src = src.rearrange(shape, **view)
                    nc.scalar.activation(dst, src, ACT.Copy).then_inc(done, 1)

                for h, stage in ORDER:
                    if stage == "tx":
                        act.wait_ge(attx_in, ATTX_IN)
                    if stage in ("load", "tx", "tq", "t1", "ty"):
                        copy_out(h, stage, "xT", xT[h][:, :, :], "p (k n) -> p k n", k=KT)
                    if stage == "load":
                        copy_out(h, stage, "cT", cT[h][:, :, :], "p (k n) -> p k n", k=KT)
                    if stage in ("qkv0.v0", "qkv0.v1"):
                        for kind, k in QKV0[stage]:
                            tt, n = divmod(k, 2)
                            copy_out(h, "qkv0", (kind, k), V[h][:, tt, n * 512:(n + 1) * 512])
                    if stage == "qkv0.t":
                        for hp in range(HP):
                            copy_out(h, "qkv0", ("qkT", hp), qkT[h][:, hp, :, :], "p (s n) -> p s n", s=2)
                    if stage.startswith("qkvx"):
                        kind, k = QKVX[2 * int(stage[-1])]
                        if kind == "qk":
                            b, done = filled(act, it, h, "qkvx", ("qk", k))
                            nc.scalar.activation(qkT[h][:, k, 0, :], b[:, 0:N], ACT.Identity, bias=bq_s[:, k:k + 1], scale=DH ** -0.5)
                            nc.scalar.activation(qkT[h][:, k, 1, :], b[:, N:2 * N], ACT.Identity, bias=bk[:, k:k + 1]).then_inc(done, 1)
                        else:
                            tt, n = divmod(k, 2)
                            copy_out(h, "qkvx", ("v", k), V[h][:, tt, n * 512:(n + 1) * 512])
                    if stage == "att":
                        step = h
                        if unit_at(step - LAG):
                            att, h, u = unit_at(step - LAG)
                            qb = u % 2
                            b, done = filled(act, it, h, att, ("PT", u))
                            if att == "atty":
                                dst = PT[:, (step - LAG) // 2 % 2, :, qb * P:(qb + 1) * P]
                                src = b[:, :].rearrange("p (a n) -> p a n", a=4)
                            else:
                                cols = 3 * P if att == "att0" else 4 * P
                                dst, src = pt_cols[:, (step - LAG) // 2 % 2, qb, 0:cols], b[:, 0:cols]
                            nc.scalar.activation(dst, src, ACT.Copy).then_inc(done, 1)
                        if unit_at(step):
                            att, h, u = unit_at(step)
                            p = p_ring[:, step % P_SLOTS, :, :]
                            if att == "attx":
                                act.wait_ge(s_max, nth(it, UNITS, h, u + 1))
                            else:
                                emptied(act, it, h, att, ("S", u))
                            for s in range(2):
                                bias = negmax[:, step % SLOTS, s:s + 1]
                                total = rowsum[:, step % SLOTS, s:s + 1]
                                if att == "att0":
                                    keys = P * (s + 1)
                                    e = nc.scalar.activation(p[:, s, 0:keys], p[:, s, 0:keys], ACT.Exp, bias=bias, scale=-1.0, accum_out=total)
                                elif att == "attx":
                                    b = bank[PLACE[(h, att, ("S", u))][0]]
                                    e = nc.scalar.activation(p[:, s, :], b[:, s * N:(s + 1) * N], ACT.Exp, bias=bias, accum_out=total)
                                else:
                                    e = nc.scalar.activation(p[:, s, :], p[:, s, :], ACT.Exp, bias=bias, scale=-1.0)
                            if att == "attx":
                                e.then_inc(drained[PLACE[(h, att, ("S", u))][0]], 1)
                            else:
                                e.then_inc(p_exp, 1)
                    if stage == "tf":
                        b, done = filled(act, it, h, stage, "qT")
                        nc.scalar.activation(qnT[h][:, :, :], b[:, 0:256].bitcast(BF16).rearrange("p (k n) -> p k n", k=KT), ACT.Copy).then_inc(done, 1)
                    if stage == "qkv1":
                        for tt in range(TT):
                            act.wait_ge(lin_rot, nth(it, TT, h, tt + 1))
                            nc.scalar.activation(elu_m[h][:, tt, :], qkf[h][:, tt, :], ACT.Relu, scale=-1.0).then_inc(lin_relu, 1)
                            act.wait_ge(lin_relu, nth(it, TT, h, tt + 1))
                            nc.scalar.activation(elu_m[h][:, tt, :], elu_m[h][:, tt, :], ACT.Exp, scale=-1.0).then_inc(lin_exp, 1)
                    if stage in ("qkv1", "qkvy"):
                        if stage == "qkvy":
                            b, done = filled(act, it, h, stage, "q")
                            for kt in range(KT):
                                q = nc.scalar.activation(xq[h][:, kt, :], b[:, kt * N:(kt + 1) * N], ACT.Identity,
                                                         bias=bqy_s[:, kt:kt + 1], scale=-D1 ** -0.5)
                            q.then_inc(done, 1)
                        copy_out(h, stage, "v", Vy[h][:, :, :, 0:D1], "p (t a d) -> p t a d", t=TT, a=H)
                    if stage == "tl":
                        copy_out(h, stage, "kT", kT[h], "p (k n) -> p k n", k=KT)
                    if stage == "lout":
                        for i in range(2):
                            copy_out(h, stage, ("oT", i), oTr[h][:, 2 * i:2 * i + 2, :], "p (m n) -> p m n", m=2)
                    if stage == "tp":
                        copy_out(h, stage, "oTT", oTT[h][:, :, :], "p (k n) -> p k n", k=KT)

        @block.vector
        def _(dve):
            s = 0

            def setup(ins, last=False):
                nonlocal s
                s += 1
                ins.then_inc(setup_dve, 1)
                if last:
                    dve.wait_ge(setup_dve, s)

            dve.wait_ge(setup_in, SETUP_IN)
            w = xb[0]
            gt, lt = xb[1], r[1]
            setup(nc.vector.tensor_reduce(wst[:, :, 0], w[:, :, :], AX.X, ALU.add, apply_absolute_value=True), last=True)
            setup(nc.vector.tensor_scalar(wst[:, :, 1], wst[:, :, 0], 1.0 / D, 1e-5, ALU.mult, ALU.max), last=True)
            setup(nc.vector.tensor_scalar(wst[:, :, 2], wst[:, :, 1], 0.5, None, ALU.mult))
            setup(nc.vector.tensor_scalar(wst[:, :, 3], wst[:, :, 1], -0.5, None, ALU.mult), last=True)
            for kt in range(KT):
                setup(nc.vector.tensor_scalar(gt[:, kt, :], w[:, kt, :], wst[:, kt, 2:3], None, ALU.is_gt))
                setup(nc.vector.tensor_scalar(lt[:, kt, :], w[:, kt, :], wst[:, kt, 3:4], None, ALU.is_lt), last=(kt == 1))
            setup(nc.vector.tensor_tensor(gt[:, :, :], gt[:, :, :], lt[:, :, :], ALU.subtract))
            for kt in range(KT):
                setup(nc.vector.tensor_scalar(diag[:, kt, :], ident[:, :], wst[:, kt, 1:2], None, ALU.mult))
            setup(nc.vector.tensor_copy(identb[:, :], ident[:, :]))
            assert s == N_SETUP_DVE - 2
            dve.wait_ge(setup_pe, 1)
            setup(nc.vector.tensor_copy(ternT[:, :, :], bank[0][:, :].rearrange("p (k n) -> p k n", k=KT)))
            setup(nc.vector.tensor_copy(wscale_row[:, :], bank[1][:, 0:D]), last=True)
            dve.wait_ge(setup_pool, 8)
            with dve.Fori(0, ITERS) as it:
                steps = 0

                def link(ins, alone=False):
                    nonlocal steps
                    steps += 1
                    ins.then_inc(dve_seq, 1)
                    dve.wait_ge(dve_seq, it * DVE_LINKS + steps)
                    if alone:
                        passed(dve)

                def statistics(h):
                    for tt in range(TT):
                        last = nc.vector.bn_stats(stats[:, tt, :], r[h][:, tt, :])
                    link(last, alone=True)
                    for tt in range(TT):
                        last = nc.vector.bn_aggr(mv[:, h, tt, :], stats[:, tt, :])
                    last.then_inc(ln_stats, 1)

                def normalise(h, stage, dst):
                    dve.wait_ge(ln_rstd, summed(it, h, stage))
                    for tt in range(TT):
                        last = nc.vector.tensor_scalar(dst[:, tt, :], r[h][:, tt, :], mv[:, h, tt, 0:1], rstd[:, h, tt:tt + 1],
                                                       ALU.subtract, ALU.mult)
                    last.then_inc(x_ready, 1)

                def two(b):
                    return b[:, :].rearrange("p (t n) -> p t n", t=2)

                def residual(h, stage, res):
                    b, done = filled(dve, it, h, stage, "out")
                    nc.vector.tensor_tensor(r[h][:, :, :], two(b), res[:, :, :], ALU.add).then_inc(done, 1)
                    emptied(dve, it, h, stage, "out")

                def rotary(h, stage, k, rope_t, width, cos, sin):
                    b, done = filled(dve, it, h, stage, ("qk", k))
                    heads = 512 // width
                    nc.vector.tensor_tensor(rope_t[:, 0, :].rearrange("p (h d) -> p h d", d=width),
                                            b[:, :].rearrange("p (h d) -> p h d", d=width),
                                            cos[:, None, :].broadcast_to([P, heads, width]), ALU.mult)
                    half = width // 2
                    for s in range(2):
                        last = nc.vector.tensor_tensor(
                            rope_t[:, 1, :].rearrange("p (h s d) -> p h s d", s=2, d=half)[:, :, s, :],
                            b[:, :].rearrange("p (h s d) -> p h s d", s=2, d=half)[:, :, 1 - s, :],
                            sin[:, None, s * half:(s + 1) * half].broadcast_to([P, heads, half]), ALU.mult)
                    last.then_inc(done, 1)

                def normalised(h, stage, dst, tt, guard):
                    b, done = filled(dve, it, h, stage, ("o", tt))
                    o = b[:, :].rearrange("p (h d) -> p h d", h=H)
                    link(nc.vector.tensor_scalar(rden[:, 0, :], o[:, :, D1], guard, None, ALU.max))
                    link(nc.vector.reciprocal(rden[:, 1, :], rden[:, 0, :]))
                    nc.vector.tensor_tensor(dst[:, tt, :].rearrange("p (h d) -> p h d", h=H), o[:, :, 0:D1],
                                            rden[:, 1, :, None].broadcast_to([P, H, D1]), ALU.mult).then_inc(done, 1)

                for h, stage in ORDER:
                    if stage in NORM:
                        normalise(h, NORM[stage], xb[h] if stage == "nz" else x[h])
                    if stage == "tx":
                        dve.wait_ge(attx_in, ATTX_IN)
                    if stage == "outx":
                        dve.wait_ge(rest_in, REST_IN)
                    if stage == "qkv0.qk":
                        dve.wait_ge(rope_in, 16)
                        for k in range(N_ROPE):
                            tt, n = divmod(k, 4)
                            dve.wait_ge(rope_done, nth(it, N_ROPE, h, k + 1))
                            rotary(h, "qkv0", k, rope_t[:, k % 2, :, :], DH, rope0[:, tt, n // 2, 0, :], rope0[:, tt, n // 2, 1, :])
                    if stage.startswith("qkvx"):
                        kind, k = QKVX[2 * int(stage[-1]) + 1]
                        b, done = filled(dve, it, h, "qkvx", (kind, k))
                        if kind == "qk":
                            nc.vector.tensor_scalar(qkT[h][:, k, 0, :], b[:, 0:N], bq[:, k:k + 1], DH ** -0.5, ALU.add, ALU.mult)
                            nc.vector.tensor_scalar(qkT[h][:, k, 1, :], b[:, N:2 * N], bk[:, k:k + 1], None, ALU.add).then_inc(done, 1)
                        else:
                            tt, n = divmod(k, 2)
                            nc.vector.tensor_copy(V[h][:, tt, n * 512:(n + 1) * 512], b[:, :]).then_inc(done, 1)
                    if stage == "att":
                        step = h
                        if step == 0:
                            dve.wait_ge(out0_in, OUT0_IN)
                        if unit_at(step):
                            att, h, u = unit_at(step)
                            p, least = p_ring[:, step % P_SLOTS, :, :], negmax[:, step % SLOTS, :]
                            b, done = filled(dve, it, h, att, ("S", u))
                            if att == "attx":
                                nc.vector.tensor_reduce(least, two(b), AX.X, ALU.max, negate=True).then_inc(s_max, 1)
                            else:
                                passed(dve)
                                for s in range(2):
                                    keys = P * (s + 1) if att == "att0" else N
                                    mask = mask0[:, s:2 * s + 1, :].rearrange("p a n -> p (a n)") if att == "att0" else mask1[h][:, u % 2, :]
                                    last = nc.vector.tensor_tensor_reduce(p[:, s, 0:keys], b[:, s * N:s * N + keys], mask,
                                                                          1.0, BIG, ALU.add, ALU.min, least[:, s:s + 1])
                                last.then_inc(done, 1)
                        if pair_at(step - 1):
                            att, h, hp = pair_at(step - 1)
                            if att == "atty":
                                if hp % 2:
                                    b, done = filled(dve, it, h, att, ("O", hp - 1))
                                    nc.vector.tensor_copy(oTr[h][:, hp // 2, :], b[:, 0:N]).then_inc(done, 1)
                            else:
                                b, done = filled(dve, it, h, att, ("O", hp))
                                if att == "att0":
                                    nc.vector.tensor_copy(OT[h][:, hp, :], b[:, 0:N]).then_inc(done, 1)
                                else:
                                    nc.vector.tensor_scalar(OT[h][:, hp, :], b[:, 0:N], bv[:, hp:hp + 1], None, ALU.add).then_inc(done, 1)
                        if unit_at(step - 2) and unit_at(step - 2)[0] != "atty":
                            w = step - 2
                            att, h, u = WORK[w]
                            dve.wait_ge(inv_ready, probs(it, w))
                            nc.vector.tensor_scalar(p_ring[:, w % P_SLOTS, 1, :], p_ring[:, w % P_SLOTS, 1, :],
                                                    rowinv[:, w % SLOTS, 1:2], None, ALU.mult).then_inc(p_norm, 1)
                        if unit_at(step - 1) and unit_at(step - 1)[0] != "atty":
                            w = step - 1
                            att, h, u = WORK[w]
                            if att == "attx":
                                emptied(dve, it, h, att, ("S", u))
                            else:
                                dve.wait_ge(p_exp, nth(it, UNITS, h, u + 1, 0, 2))
                            nc.vector.reciprocal(rowinv[:, w % SLOTS, :], rowsum[:, w % SLOTS, :]).then_inc(inv_ready, 1)
                    if stage in ("out0", "outx", "out1"):
                        if stage == "out0":
                            dve.wait_ge(x_in[h], it * 32 + 32)
                        if stage == "outx":
                            dve.wait_ge(xb_ready, nth(it, 1, h, 1, 0, 2) + 4)
                        residual(h, stage, xb[h] if stage == "outx" else x[h])
                        statistics(h)
                    if stage == "quant":
                        b, done = filled(dve, it, h, stage, "xh")
                        link(nc.vector.tensor_reduce(amax[:, :], two(b), AX.X, ALU.max, apply_absolute_value=True))
                        link(nc.vector.tensor_scalar(aq[:, h, :], amax[:, :], 1e-5, 1.0 / 7.0, ALU.max, ALU.mult))
                        link(nc.vector.reciprocal(amax[:, :], aq[:, h, :]))
                        for tt in range(TT):
                            last = nc.vector.tensor_scalar(r[h][:, tt, :], b[:, tt * D:(tt + 1) * D], amax[:, tt:tt + 1], MAGIC, ALU.mult, ALU.add)
                        last.then_inc(done, 1)
                        emptied(dve, it, h, stage, "xh")
                        link(nc.vector.tensor_scalar(r[h][:, :, :], r[h][:, :, :], MAGIC, -8.0, ALU.subtract, ALU.max))
                        nc.vector.tensor_scalar(qn[h][:, :, :], r[h][:, :, :], 7.0, None, ALU.min).then_inc(qn_ready, 1)
                    if stage == "ffn":
                        b, done = filled(dve, it, h, stage, "out")
                        for tt in range(TT):
                            last = nc.vector.scalar_tensor_tensor(out=r[h][:, tt, :], in0=b[:, tt * D:(tt + 1) * D], scalar=aq[:, h, tt:tt + 1],
                                                                  in1=wscale_row[:, :], op0=ALU.mult, op1=ALU.mult)
                        last.then_inc(done, 1)
                        emptied(dve, it, h, stage, "out")
                        link(nc.vector.tensor_tensor(r[h][:, :, :], r[h][:, :, :], x[h][:, :, :], ALU.add))
                        statistics(h)
                    if stage == "qkv1":
                        for tt in range(TT):
                            rotary(h, stage, tt, rope_t1[h][:, tt, :, :], D1, rope1[:, tt, 0, :], rope1[:, tt, 1, :])
                            emptied(dve, it, h, stage, ("qk", tt))
                            nc.vector.tensor_tensor(qkf[h][:, tt, :], rope_t1[h][:, tt, 0, :], rope_t1[h][:, tt, 1, :], ALU.add).then_inc(lin_rot, 1)
                    if stage == "f1":
                        for tt in range(TT):
                            dve.wait_ge(lin_exp, nth(it, TT, h, tt + 1))
                            nc.vector.scalar_tensor_tensor(out=qkf[h][:, tt, :], in0=qkf[h][:, tt, :], scalar=0.0, in1=elu_m[h][:, tt, :],
                                                           op0=ALU.max, op1=ALU.add).then_inc(lin_feat, 1)
                    if stage == "tl":
                        b, done = filled(dve, it, h, stage, "qT")
                        for s in range(2):
                            last = nc.vector.tensor_scalar(qm[h][:, :, s, :], two(b), par[:, s:s + 1], None, ALU.mult)
                        last.then_inc(done, 1)
                    if stage == "lin":
                        b, done = filled(dve, it, h, stage, "KV")
                        nc.vector.tensor_tensor(KVm[h][:, :, :], two(b),
                                                bdm[:, :, :].rearrange("p h v -> p (h v)")[:, None, :].broadcast_to([P, KT, 8 * VW]),
                                                ALU.mult).then_inc(done, 1)
                        for c in range(TT):
                            for q in range(4):
                                b, done = filled(dve, it, h, stage, ("A", c, q))
                                nc.vector.tensor_tensor(AT[h][c][:, q, :, :], b[:, :].rearrange("p (a n) -> p a n", a=4),
                                                        tri[:, None, :].broadcast_to([P, 4, P]), ALU.mult).then_inc(done, 1)
                    if stage == "to":
                        for tt in range(TT):
                            normalised(h, stage, o_tok[h], tt, 1e-6)
                        emptied(dve, it, h, stage, ("o", TT - 1))
                    if stage == "qkvy":
                        b, done = filled(dve, it, h, stage, "k")
                        for kt in range(KT):
                            last = nc.vector.tensor_scalar(ky[h][:, kt, :], b[:, kt * N:(kt + 1) * N], bky[:, kt:kt + 1], None, ALU.add)
                        last.then_inc(done, 1)
                        dve.wait_ge(mask1_ready, nth(it, 1, h, 1))
                    if stage == "outy":
                        for tt in range(TT):
                            normalised(h, stage, y_tok[h], tt, 0.0)
                        emptied(dve, it, h, stage, ("o", TT - 1))
                        dve.wait_ge(xb_ready, nth(it, 1, h, 1, 1, 2) + 4)
                        link(nc.vector.tensor_tensor(r[h][:, :, :], y_tok[h][:, :, :], xb[h][:, :, :], ALU.add))
                        statistics(h)
                assert steps == DVE_LINKS, f"DVE_LINKS {steps}"

        @block.tensor
        def _(pe):
            mm, tr = nc.tensor.matmul, nc.tensor.transpose
            pe.wait_ge(setup_pool, 2)
            pe.wait_ge(setup_dve, N_SETUP_DVE - 2)
            for kt in range(KT):
                for ot in range(KT):
                    tr(bank[0][:, kt * D + ot * P:kt * D + (ot + 1) * P], xb[1][:, ot, kt * P:(kt + 1) * P], ident[:, :])
            for kt in range(KT):
                last = mm(bank[1][:, kt * P:(kt + 1) * P], ones[:, :], diag[:, kt, :], start=True, stop=True)
            last.then_inc(setup_pe, 1)
            pe.wait_ge(setup_dve, N_SETUP_DVE)
            with pe.Fori(0, ITERS) as it:

                def turn(h, stage, name, src, operands=()):
                    b, done = claim(pe, it, h, stage, name, operands)
                    for kt in range(KT):
                        for tt in range(TT):
                            last = tr(b[:, kt * N + tt * P:kt * N + (tt + 1) * P], src[:, tt, kt * P:(kt + 1) * P], ident[:, :])
                    last.then_inc(done, 1)

                def product(out, pairs):
                    for i, (lhsT, rhs) in enumerate(pairs):
                        last = mm(out, lhsT, rhs, start=(i == 0), stop=(i == len(pairs) - 1))
                    return last

                def token_tiles(h, stage, name, lhs, rhs, n, operands=()):
                    b, done = claim(pe, it, h, stage, name, operands)
                    for tt in range(TT):
                        last = product(b[:, tt * D:(tt + 1) * D], [(lhs(k, tt), rhs(k)) for k in range(n)])
                    last.then_inc(done, 1)

                def tok(t, tt):
                    return slice(tt * t, (tt + 1) * t)

                for h, stage in ORDER:
                    if stage == "out0":
                        pe.wait_ge(out0_in, OUT0_IN)
                    if stage == "tx":
                        pe.wait_ge(attx_in, ATTX_IN)
                    if stage == "outx":
                        pe.wait_ge(rest_in, REST_IN)
                    if stage == "load":
                        pe.wait_ge(x_in[h], it * 32 + 32)
                        turn(h, stage, "xT", x[h])
                        turn(h, stage, "cT", cx[h])
                    if stage in ("tx", "tq", "t1", "ty"):
                        pe.wait_ge(x_ready, normed(it, h, NORM["n" + stage[1]]))
                        turn(h, stage, "xT", x[h])
                    if stage in QKV0:
                        for kind, k in QKV0[stage]:
                            tt, n = divmod(k, 2 if kind == "v" else 4)
                            col = n * 512 + (2 * IN0 if kind == "v" else 0)
                            pe.wait_ge(w0_in[col // 512], 16)
                            b, done = claim(pe, it, h, "qkv0", (kind, k), [("load", "xT")])
                            product(b[:, :], [(xT[h][:, kt, tok(P, tt)], wqkv0[:, kt, col:col + 512]) for kt in range(KT)]).then_inc(done, 1)
                    if stage == "qkv0.t":
                        pe.wait_ge(rope_done, nth(it, N_ROPE, h, N_ROPE) + 2)
                        for hp in range(HP):
                            b, done = claim(pe, it, h, "qkv0", ("qkT", hp))
                            for s in range(2):
                                for tt in range(TT):
                                    last = tr(b[:, s * N + tt * P:s * N + (tt + 1) * P], roped[:, tt, s * IN0 + hp * P:s * IN0 + (hp + 1) * P], ident[:, :])
                            last.then_inc(done, 1)
                    if stage.startswith("qkvx"):
                        for kind, k in QKVX[2 * int(stage[-1]):2 * int(stage[-1]) + 2]:
                            b, done = claim(pe, it, h, "qkvx", (kind, k), [("load", "cT"), ("tx", "xT")])
                            if kind == "qk":
                                product(b[:, 0:N], [(wq[:, kt, tok(P, k)], xT[h][:, kt, :]) for kt in range(KT)])
                                product(b[:, N:2 * N], [(wk[:, kt, tok(P, k)], cT[h][:, kt, :]) for kt in range(KT)]).then_inc(done, 1)
                            else:
                                tt, n = divmod(k, 2)
                                product(b[:, :], [(cT[h][:, kt, tok(P, tt)], wv[:, kt, n * 512:(n + 1) * 512]) for kt in range(KT)]).then_inc(done, 1)
                    if stage == "att":
                        step = h
                        if unit_at(step):
                            att, h, u = unit_at(step)
                            hp, qb = divmod(u, 2)
                            prev = {"att0": "qkv0", "attx": "qkvx", "atty": "qkvy"}[att]
                            operands = []
                            if att != "atty":
                                operands.append((prev, ("qkT" if att == "att0" else "qk", hp)))
                            if u == 0:
                                operands += [(prev, name) for name in (("q", "k", "v") if att == "atty" else [("v", k) for k in range(4)])]
                            b, done = claim(pe, it, h, att, ("S", u), operands)
                            if att == "atty":
                                pe.wait_ge(km_ready, nth(it, H, h, 2 * hp + 2))
                                last = mm(b[:, :], xq[h][:, hp // 4, tok(P, qb)], km[h][:, 2 * hp:2 * hp + 2, :], start=True, stop=True)
                            else:
                                head = slice(DH * (u % 2), DH * (u % 2) + DH)
                                for qb in range(TT):
                                    keys = N if att == "attx" else P * (qb + 1)
                                    last = mm(b[:, qb * N:qb * N + keys], qkT[h][head, hp, 0, tok(P, qb)],
                                              qkT[h][head, hp, 1, 0:keys], start=True, stop=True)
                            last.then_inc(done, 1)
                        if unit_at(step - LAG):
                            w = step - LAG
                            att, h, u = WORK[w]
                            if att == "atty":
                                pe.wait_ge(p_exp, nth(it, UNITS, h, u + 1, 1, 2))
                            else:
                                pe.wait_ge(p_norm, probs(it, w))
                                pe.wait_ge(p_norm0, probs(it, w))
                            b, done = claim(pe, it, h, att, ("PT", u))
                            for s in range(2):
                                for kb in range(TT):
                                    if att == "att0" and kb > s:
                                        continue
                                    col = {"att0": kb + s, "attx": 2 * kb + s, "atty": 2 * s + kb}[att]
                                    last = tr(b[:, tok(P, col)], p_ring[:, w % P_SLOTS, s, tok(P, kb)], ident[:, :])
                            last.then_inc(done, 1)
                        if pair_at(step):
                            att, h, hp = pair_at(step)
                            slot = (step - O_LAG) // 2 % 2
                            operands = [(att, ("PT", 2 * hp)), (att, ("PT", 2 * hp + 1))]
                            if att == "atty":
                                if hp % 2 == 0:
                                    o_bank, o_done = claim(pe, it, h, att, ("O", hp), operands)
                                else:
                                    emptied_all(pe, it, h, att, [("PT", 2 * hp), ("PT", 2 * hp + 1)])
                                for kb in range(TT):
                                    for s in range(2):
                                        j = 2 * (hp % 2) + s
                                        last = mm(o_bank[32 * j:32 * j + 32, 0:N], Vy[h][:, kb, 2 * hp + s, :], PT[:, slot, 2 * s + kb, :],
                                                  start=(kb == 0), stop=(kb == 1))
                                if hp % 2:
                                    last.then_inc(o_done, 1)
                            else:
                                b, done = claim(pe, it, h, att, ("O", hp), operands)
                                for kb in range(TT):
                                    for s in range(2):
                                        q0 = P if att == "att0" and kb else 0
                                        last = mm(b[64 * s:64 * s + 64, q0:N], V[h][:, kb, (2 * hp + s) * DH:(2 * hp + s + 1) * DH],
                                                  pt_cols[:, slot, s, kb * N:kb * N + N - q0], start=(kb == 0), stop=(kb == 1))
                                last.then_inc(done, 1)
                    if stage in ("out0", "outx"):
                        att = "att0" if stage == "out0" else "attx"
                        w = wout0 if stage == "out0" else wo
                        token_tiles(h, stage, "out", lambda k, tt: OT[h][:, k, tok(P, tt)], lambda k: w[:, k, :], HP, [(att, ("O", HP - 1))])
                    if stage == "quant":
                        token_tiles(h, stage, "xh", lambda k, tt: xT[h][:, k, tok(P, tt)], lambda k: had[:, :] if k else had[:, None, 0:P].broadcast_to([P, 2, P]), KT,
                                    [("tq", "xT")])
                    if stage == "tf":
                        pe.wait_ge(qn_ready, nth(it, 1, h, 1))
                        b, done = claim(pe, it, h, stage, "qT")
                        bb = b[:, 0:256].bitcast(BF16)
                        for kt in range(KT):
                            for tt in range(TT):
                                last = tr(bb[:, kt * N + tt * P:kt * N + (tt + 1) * P], qn[h][:, tt, tok(P, kt)], identb[:, :])
                        last.then_inc(done, 1)
                    if stage == "ffn":
                        token_tiles(h, stage, "out", lambda k, tt: qnT[h][:, k, tok(P, tt)], lambda k: ternT[:, k, :], KT, [("tf", "qT")])
                    if stage == "qkv1":
                        for tt in range(TT):
                            b, done = claim(pe, it, h, stage, ("qk", tt), [("t1", "xT")])
                            product(b[:, :], [(xT[h][:, kt, tok(P, tt)], wqkv1[:, kt, 0:512]) for kt in range(KT)]).then_inc(done, 1)
                        token_tiles(h, stage, "v", lambda k, tt: xT[h][:, k, tok(P, tt)], lambda k: wqkv1[:, k, 512:768], KT)
                    if stage == "tl":
                        pe.wait_ge(lin_feat, nth(it, TT, h, TT))
                        turn(h, stage, "qT", qkf[h][:, :, 0:D])
                        turn(h, stage, "kT", qkf[h][:, :, D:2 * D])
                    if stage == "lin":
                        b, done = claim(pe, it, h, stage, "KV", [("qkv1", "v")])
                        for kt in range(KT):
                            last = mm(b[:, kt * 256:(kt + 1) * 256], qkf[h][:, 0, D + kt * P:D + (kt + 1) * P],
                                      Vy[h][:, 0, 8 * kt:8 * kt + 8, :], start=True, stop=True)
                        last.then_inc(done, 1)
                        for c in range(TT):
                            for q in range(4):
                                b, done = claim(pe, it, h, stage, ("A", c, q), [("tl", "qT"), ("tl", "kT")])
                                for kt in range(KT):
                                    last = mm(b[:, kt * 256:(kt + 1) * 256], kT[h][32 * q:32 * q + 32, kt, tok(P, c)],
                                              qm[h][32 * q:32 * q + 32, kt, :, tok(P, c)], start=True, stop=True)
                                last.then_inc(done, 1)
                    if stage == "lout":
                        operands = [("lin", "KV")] + [("lin", ("A", c, q)) for c in range(TT) for q in range(4)]
                        for kt in range(KT):
                            b, done = claim(pe, it, h, stage, ("oT", kt), operands)
                            for mi in range(2):
                                for c in range(TT):
                                    for j in range(4):
                                        lh = 4 * mi + j
                                        q, s = divmod(lh, 2)
                                        out = b[32 * j:32 * j + 32, mi * N + c * P:mi * N + (c + 1) * P]
                                        last = mm(out, Vy[h][:, c, 8 * kt + lh, :], AT[h][c][:, q, 2 * kt + s, :],
                                                  start=True, stop=(c == 0))
                                    if c == 1:
                                        for j in range(4):
                                            lh = 4 * mi + j
                                            out = b[32 * j:32 * j + 32, mi * N + P:mi * N + 2 * P]
                                            last = mm(out, KVm[h][:, kt, lh * VW:(lh + 1) * VW], qm[h][:, kt, lh % 2, P:2 * P],
                                                      start=False, stop=True)
                            last.then_inc(done, 1)
                    if stage in ("to", "outy"):
                        operands = [("lout", ("oT", kt)) for kt in range(KT)] if stage == "to" else [("atty", ("O", HP - 2))]
                        for tt in range(TT):
                            b, done = claim(pe, it, h, stage, ("o", tt), operands)
                            for m in range(4):
                                last = tr(b[:, tok(P, m)], oTr[h][:, m, tok(P, tt)], ident[:, :])
                            last.then_inc(done, 1)
                    if stage == "tp":
                        turn(h, stage, "oTT", o_tok[h], [("to", ("o", tt)) for tt in range(TT)])
                    if stage == "out1":
                        token_tiles(h, stage, "out", lambda k, tt: oTT[h][:, k, tok(P, tt)], lambda k: wout1[:, k, :], KT, [("tp", "oTT")])
                    if stage == "qkvy":
                        for name, w, src in (("q", wqy, xT[h]), ("k", wky, cT[h])):
                            b, done = claim(pe, it, h, stage, name, [("ty", "xT")])
                            for ft in range(KT):
                                last = product(b[:, ft * N:(ft + 1) * N], [(w[:, kt, tok(P, ft)], src[:, kt, :]) for kt in range(KT)])
                            last.then_inc(done, 1)
                        token_tiles(h, stage, "v", lambda k, tt: cT[h][:, k, tok(P, tt)], lambda k: wvy[:, k, :], KT)

        layers.close()

        xe, xeT, re, ye = x, xT, r, xb
        hT = [qk_area[i][:, 0:FT * N].rearrange("p (j n) -> p j n", j=FT) for i in HALVES]
        sg = v_area[0][:, 0:4 * N].rearrange("p (j n) -> p j n", j=4)

        def width(j):
            return P if j < FT - 1 else FR

        experts = ctx.enter_context(nc.Block())

        @experts.sync
        def _(sp):
            def tokens(i, e):
                sp.dma_start(xe[i][:, :, :], scratch[bass.ds(e, 1)].rearrange("o (t b) s n -> (b s) (o t) n", t=TT)).then_inc(tok_in[i], 16)

            def outputs(it, i):
                sp.wait_ge(y_ready, nth(it, 1, i, 1))
                for q in range(QTR):
                    to = out_d.rearrange("(t q) s n -> q s t n", q=QTR)[q, bass.ds((it * 2 + i) * TE, TE)]
                    sp.dma_start(to, ye[i][TE * q:TE * q + TE, :, :]).then_inc(y_stored[i], 16)

            for i in HALVES:
                tokens(i, i)
            with sp.Fori(0, ITERS - 1) as it:
                for i in HALVES:
                    b, k = moe_at(it, i, ("gu", FT - 1))
                    sp.wait_ge(drained[b], k + 2)
                    gate_weights(sp, i, it * 2 + i + 2)
                for i in HALVES:
                    b, k = moe_at(it, i, "out")
                    sp.wait_ge(drained[b], k + 2)
                    tokens(i, it * 2 + i + 2)
                    down_weight(sp, i, it * 2 + i + 2)
                for i in HALVES:
                    outputs(it, i)
            for i in HALVES:
                outputs(ITERS - 1, i)

        @experts.gpsimd
        def _(pool):
            with pool.Fori(0, ITERS) as it:
                for i in HALVES:
                    pool.wait_ge(moe_stats, nth(it, 1, i, 1))
                    passed(pool)
                    nc.gpsimd.tensor_scalar(var_e[:, i, :], mv[:, i, :, 1], EPS, None, ALU.add).then_inc(pool_seq, 1)
                    pool.wait_ge(pool_seq, nth(it, 1, i, 1) + ITERS * POOL_LINKS)
                    nc.gpsimd.tensor_tensor(rstd[:, i, :], var_e[:, i, :], half_neg[:, :], ALU.pow).then_inc(moe_rstd, 1)
                for i in HALVES:
                    pool.wait_ge(y_stored[i], it * (16 * QTR) + 16 * QTR)
                    pool.sem_inc(y_free[i], 1)

        @experts.scalar
        def _(act):
            with act.Fori(0, ITERS) as it:
                for i in HALVES:
                    b, k = moe_at(it, i, "xT")
                    act.wait_ge(full[b], k + 1)
                    nc.scalar.activation(xeT[i][:, :, :], bank[b][:, :].rearrange("p (k n) -> p k n", k=KT), ACT.Copy).then_inc(drained[b], 1)
                    for j in range(FT):
                        b, k = moe_at(it, i, ("gu", j))
                        act.wait_ge(full[b], k + 1)
                        w = width(j)
                        nc.scalar.activation(sg[0:w, b - 1, :], bank[b][0:w, 0:N], ACT.Silu).then_inc(silu_done, 1)

        @experts.vector
        def _(dve):
            steps = 0
            with dve.Fori(0, ITERS) as it:
                for i in HALVES:
                    for j in range(FT):
                        b, k = moe_at(it, i, ("gu", j))
                        w = width(j)
                        dve.wait_ge(silu_done, nth(it, FT, i, j + 1))
                        nc.vector.tensor_tensor(hT[i][0:w, j, :], sg[0:w, b - 1, :], bank[b][0:w, N:2 * N], ALU.mult).then_inc(drained[b], 1)
                for i in HALVES:
                    b, k = moe_at(it, i, "out")
                    dve.wait_ge(full[b], k + 1)
                    dve.wait_ge(tok_in[i], it * 16 + 16)
                    nc.vector.tensor_tensor(re[i][:, :, :], bank[b][:, :].rearrange("p (t n) -> p t n", t=TT), xe[i][:, :, :], ALU.add).then_inc(drained[b], 1)
                    dve.wait_ge(drained[b], k + 2)
                    for tt in range(TT):
                        last = nc.vector.bn_stats(stats[:, tt, :], re[i][:, tt, :])
                    last.then_inc(dve_seq, 1)
                    dve.wait_ge(dve_seq, nth(it, 1, i, 1) + ITERS * DVE_LINKS)
                    passed(dve)
                    for tt in range(TT):
                        last = nc.vector.bn_aggr(mv[:, i, tt, :], stats[:, tt, :])
                    last.then_inc(moe_stats, 1)
                    dve.wait_ge(moe_rstd, nth(it, 1, i, 1))
                    dve.wait_ge(y_free[i], it + 1)
                    for tt in range(TT):
                        last = nc.vector.tensor_scalar(ye[i][:, tt, :], re[i][:, tt, :], mv[:, i, tt, 0:1], rstd[:, i, tt:tt + 1],
                                                       ALU.subtract, ALU.mult)
                    last.then_inc(y_ready, 1)

        @experts.tensor
        def _(pe):
            mm = nc.tensor.matmul
            with pe.Fori(0, ITERS) as it:
                for i in HALVES:
                    pe.wait_ge(tok_in[i], it * 16 + 16)
                    b, k = moe_at(it, i, "xT")
                    pe.wait_ge(drained[b], k + 1)
                    for kt in range(KT):
                        for tt in range(TT):
                            last = nc.tensor.transpose(bank[b][:, kt * N + tt * P:kt * N + (tt + 1) * P], xe[i][:, tt, kt * P:(kt + 1) * P], ident[:, :])
                    last.then_inc(full[b], 1)
                    pe.wait_ge(drained[b], k + 2)
                    pe.wait_ge(w13_in[i], it * 32 + 32)
                    for j in range(FT):
                        b, k = moe_at(it, i, ("gu", j))
                        pe.wait_ge(drained[b], k + 1)
                        w = width(j)
                        for s, wx in enumerate((w1[i], w3[i])):
                            for kt in range(KT):
                                last = mm(bank[b][0:w, s * N:(s + 1) * N], wx[:, kt, j * P:j * P + w], xeT[i][:, kt, :],
                                          start=(kt == 0), stop=(kt == KT - 1))
                        last.then_inc(full[b], 1)
                for i in HALVES:
                    for j in range(FT - 4, FT):
                        gb, gk = moe_at(it, i, ("gu", j))
                        pe.wait_ge(drained[gb], gk + 2)
                    b, k = moe_at(it, i, "out")
                    pe.wait_ge(w2_in[i], it * 32 + 32)
                    pe.wait_ge(drained[b], k + 1)
                    for tt in range(TT):
                        for j in range(FT):
                            w = width(j)
                            last = mm(bank[b][:, tt * D:(tt + 1) * D], hT[i][0:w, j, tt * P:(tt + 1) * P], w2[i][0:w, j, :],
                                      start=(j == 0), stop=(j == FT - 1))
                    last.then_inc(full[b], 1)


def shape_constants():
    f32 = np.float32

    def rotary(dh, tokens):
        inv = (1.0 / 10000.0 ** (np.arange(0, dh, 2, dtype=np.float64) / dh)).astype(f32)
        angle = (np.arange(tokens, dtype=f32)[:, None] * inv[None, :]).astype(f32)
        c, s = np.cos(angle.astype(np.float64)), np.sin(angle.astype(np.float64))
        return np.concatenate([c, c], 1), np.concatenate([-s, s], 1)

    c0, s0 = rotary(DH, N)
    rope0 = np.stack([np.stack([-c0, -s0], 1) * DH ** -0.5, np.stack([c0, s0], 1)], 1)
    c1, s1 = rotary(D1, N)
    rope1 = np.stack([c1, s1], 1) * D1 ** -0.25
    q, k = np.arange(P)[:, None], np.arange(P)[None, :]
    causal = np.where(k <= q, 0.0, BIG)
    window = np.where(k >= q, 0.0, BIG)
    mask0 = np.stack([causal, window, causal], 1)
    tri = (q <= k) * 1.0
    parity = np.stack([(np.arange(P) % 32) < 16, (np.arange(P) % 32) >= 16], 1) * 1.0
    heads8 = (np.arange(P)[:, None] // D1 == np.arange(8)[None, :]) * 1.0
    bdm = np.repeat((np.arange(P)[:, None] // D1 == np.arange(8)[None, :])[:, :, None], VW, 2) * 1.0
    had = np.ones((1, 1))
    while had.shape[0] < D:
        had = np.block([[had, had], [had, -had]])
    had = had / np.sqrt(D)
    return {"c_ident": np.eye(P), "c_rope0": rope0.reshape(N, -1), "c_rope1": rope1.reshape(N, -1), "c_mask0": mask0,
            "c_tri": tri, "c_par": parity, "c_rows8": heads8, "c_bdm": bdm, "c_had": had[P:, :]}


def kernel(**inputs):
    import concourse.bacc as bacc
    from concourse.bass_utils import run_bass_kernel_spmd

    def arr(name):
        return np.asarray(inputs[name])

    def columns(a):
        return np.ascontiguousarray(a.reshape(-1, P).T)

    feeds = {
        "x": arr("x"), "ctx": arr("ctx_1024"),
        "padm": arr("mask_Bx1x1xS2_ik0").reshape(B, N), "subm": arr("mask_1x1xSxS2_ik0").reshape(N, N),
        "wqkv0": arr("L0_attn_W_qkv"), "wout0": arr("L0_attn_W_out"),
        "wq": arr("L0_xattn_Wq").reshape(D, IN0), "bq": columns(arr("L0_xattn_bq")),
        "wk": arr("L0_xattn_Wk").reshape(D, IN0), "bk": columns(arr("L0_xattn_bk")),
        "wv": arr("L0_xattn_Wv").reshape(D, IN0), "bv": columns(arr("L0_xattn_bv")),
        "wo": arr("L0_xattn_Wo").reshape(IN0, D), "bo": arr("L0_xattn_bo"),
        "ffn": arr("L0_ffn_weight"), "wqkv1": arr("L1_attn_w_qkv"), "wout1": arr("L1_attn_w_out"),
        "wqy": arr("L1_xattn_Wq").T, "bqy": columns(arr("L1_xattn_bq")),
        "wky": arr("L1_xattn_Wk").T, "bky": columns(arr("L1_xattn_bk")),
        "wvy": arr("L1_xattn_Wv").T, "bvy": arr("L1_xattn_bv"),
        "w1": arr("L1_ffn_w1"), "w3": arr("L1_ffn_w3"), "w2": arr("L1_ffn_w2"),
    }
    for name, a in shape_constants().items():
        feeds[name] = a.astype(np.float32)
    nc = bacc.Bacc("TRN2", target_bir_lowering=False, num_devices=1)
    arrays, args = {}, []
    for name, a in feeds.items():
        arrays[f"in_{name}"] = np.ascontiguousarray(a)
        args.append(nc.dram_tensor(f"in_{name}", a.shape, mybir.dt.from_np(a.dtype), kind="ExternalInput").ap())
    args.append(nc.dram_tensor("out_0", (B, N, D), F32, kind="ExternalOutput").ap())
    decoder_kernel(nc, *args)
    result = run_bass_kernel_spmd(nc, [arrays], core_ids=[0])
    return result.results[0]["out_0"]
```
